# Optimizing a Trainium2 kernel written in Bass

```python
import numpy as np
import jax
import jax.numpy as jnp

def _softmax(x, axis=-1):
    return jax.nn.softmax(x, axis=axis)

def _gelu(x):
    return jax.nn.gelu(x, approximate=True)

def _silu(x):
    return jax.nn.silu(x)

def _sigmoid(x):
    return jax.nn.sigmoid(x)

def _layernorm(x, axis=-1, eps=1e-05):
    m = jnp.mean(x, axis=axis, keepdims=True)
    v = jnp.var(x, axis=axis, keepdims=True)
    return (x - m) / jnp.sqrt(v + eps)

def _scatter_add(tgt, idx, src, axis=0):
    return tgt.at[idx].add(src)

def _segment_sum(src, seg, n):
    return jax.ops.segment_sum(src, seg, n)
kernel_name = 'mk_conv_preact_d4_conv_nchw64_r2_539ff7'

def setup_inputs(seed: int=0):
    np.random.seed(seed)
    _w = jnp.asarray

    def _rec_inputs():
        import jax
        import jax.numpy as jnp
        _gk = jax.random.key(seed)
        x = -7.109e-05 + 0.9999 * jax.random.normal(jax.random.fold_in(_gk, 1), (8, 32, 128, 128), jnp.float32)
        return x
    x = _rec_inputs()

    def _L0_conv_setup():
        import jax, jax.numpy as jnp
        import numpy as np
        CHANNELS = 32
        KSIZE = 2 * 5 + 1

        def _gaussian_kernel2d(sigma):
            s = jnp.abs(sigma) + 1e-06
            ax = jnp.arange(KSIZE, dtype=jnp.float32) - (KSIZE - 1) / 2.0
            gauss = jnp.exp(-0.5 * (ax / s) ** 2)
            gauss = gauss / gauss.sum()
            k2d = jnp.outer(gauss, gauss)
            k2d = k2d / k2d.sum()
            return k2d
        key = jax.random.key(seed)
        kx, _ = jax.random.split(key)
        x = jax.random.normal(kx, (16, CHANNELS, 128, 128), dtype=jnp.float32)
        sigma = jnp.float32(1.0)
        return {'x': x, 'sigma': sigma}
    _L0_conv_all = _L0_conv_setup()
    _L0_conv_in = {k: v for k, v in _L0_conv_all.items() if k in ('sigma',)}
    del _L0_conv_all

    def _L1_conv_setup():
        import jax, jax.numpy as jnp
        import numpy as np
        K = 3
        PAD = 1
        EPS = 1e-05
        key = jax.random.key(seed)
        ks = jax.random.split(key, 4)
        N, C, H, W = (32, 32, 64, 64)
        hidden = 32
        in_feat = C * K * K
        x = jax.random.normal(ks[0], (N, C, H, W), dtype=jnp.float32)
        proj_weight = jax.random.normal(ks[1], (hidden, in_feat), dtype=jnp.float32) * (1.0 / in_feat ** 0.5)
        proj_bias = jnp.zeros((hidden,), dtype=jnp.float32)
        bn_gamma = jnp.ones((hidden,), dtype=jnp.float32)
        bn_beta = jnp.zeros((hidden,), dtype=jnp.float32)
        scale_w = jax.random.normal(ks[2], (C, hidden), dtype=jnp.float32) * (1.0 / hidden ** 0.5)
        scale_b = jnp.zeros((C,), dtype=jnp.float32)
        return {'x': x, 'proj_weight': proj_weight, 'proj_bias': proj_bias, 'bn_gamma': bn_gamma, 'bn_beta': bn_beta, 'scale_w': scale_w, 'scale_b': scale_b}
    _L1_conv_all = _L1_conv_setup()
    _L1_conv_in = {k: v for k, v in _L1_conv_all.items() if k in ('proj_weight', 'proj_bias', 'bn_gamma', 'bn_beta', 'scale_w', 'scale_b')}
    del _L1_conv_all

    def _L2_conv_setup():
        import jax, jax.numpy as jnp
        import numpy as np
        K = 9
        CENTER = K // 2
        EXTEND = 1.0
        EPS = 1e-05
        B, C, O, H, W = (4, 32, 32, 64, 64)

        def group_norm(x, gamma, beta, groups, eps=EPS):
            b, c, h, w = x.shape
            xg = x.reshape(b, groups, c // groups, h, w)
            mu = xg.mean(axis=(2, 3, 4), keepdims=True)
            var = xg.var(axis=(2, 3, 4), keepdims=True)
            xg = (xg - mu) / jnp.sqrt(var + eps)
            return xg.reshape(b, c, h, w) * gamma[None, :, None, None] + beta[None, :, None, None]

        def bilinear_sample(img, ym, xm):
            c, h, w = img.shape
            y0 = jnp.floor(ym)
            x0 = jnp.floor(xm)
            wy = ym - y0
            wx = xm - x0
            y0i = jnp.clip(y0.astype(jnp.int32), 0, h - 1)
            x0i = jnp.clip(x0.astype(jnp.int32), 0, w - 1)
            y1i = jnp.clip(y0i + 1, 0, h - 1)
            x1i = jnp.clip(x0i + 1, 0, w - 1)
            g00 = img[:, y0i, x0i]
            g01 = img[:, y0i, x1i]
            g10 = img[:, y1i, x0i]
            g11 = img[:, y1i, x1i]
            return g00 * (1 - wy) * (1 - wx) + g01 * (1 - wy) * wx + g10 * wy * (1 - wx) + g11 * wy * wx
        key = jax.random.key(seed)
        ks = jax.random.split(key, 4)
        x = jax.random.normal(ks[0], (B, C, H, W), dtype=jnp.float32)
        w_off = jax.random.normal(ks[1], (2 * K, C, 3, 3), dtype=jnp.float32) * 0.05
        b_off = jnp.zeros((2 * K,), jnp.float32)
        gn_off_g = jnp.ones((2 * K,), jnp.float32)
        gn_off_b = jnp.zeros((2 * K,), jnp.float32)
        w_dsc = jax.random.normal(ks[2], (O, C, K, 1), dtype=jnp.float32) * 0.05
        b_dsc = jnp.zeros((O,), jnp.float32)
        gn_g = jnp.ones((O,), jnp.float32)
        gn_b = jnp.zeros((O,), jnp.float32)
        return {'x': x, 'w_off': w_off, 'b_off': b_off, 'gn_off_g': gn_off_g, 'gn_off_b': gn_off_b, 'w_dsc': w_dsc, 'b_dsc': b_dsc, 'gn_g': gn_g, 'gn_b': gn_b}
    _L2_conv_all = _L2_conv_setup()
    _L2_conv_in = {k: v for k, v in _L2_conv_all.items() if k in ('w_off', 'b_off', 'gn_off_g', 'gn_off_b', 'w_dsc', 'b_dsc', 'gn_g', 'gn_b')}
    del _L2_conv_all

    def _L3_conv_setup():
        import jax, jax.numpy as jnp
        import numpy as np
        K = 3
        STRIDE = 1
        PAD = 1
        DIL = 1
        K2 = K * K

        def conv2d(x, w, b):
            y = jax.lax.conv_general_dilated(x, w, window_strides=(STRIDE, STRIDE), padding=[(PAD, PAD), (PAD, PAD)], rhs_dilation=(DIL, DIL), dimension_numbers=('NCHW', 'OIHW', 'NCHW'))
            return y + b[None, :, None, None]

        def _forward(x, weight, bias, offset_w, offset_b, mod_w, mod_b):
            B, C, H, W = x.shape
            O = weight.shape[0]
            offsets = conv2d(x, offset_w, offset_b)
            mod = jax.nn.sigmoid(conv2d(x, mod_w, mod_b))
            Ho, Wo = (offsets.shape[2], offsets.shape[3])
            off = offsets.reshape(B, 2, K2, Ho, Wo)
            base_y = jnp.arange(Ho, dtype=x.dtype) * STRIDE - PAD + K // 2 * DIL
            base_x = jnp.arange(Wo, dtype=x.dtype) * STRIDE - PAD + K // 2 * DIL
            sy = base_y[None, None, :, None] + off[:, 0]
            sx = base_x[None, None, None, :] + off[:, 1]
            y0 = jnp.floor(sy)
            x0 = jnp.floor(sx)
            wy1 = sy - y0
            wx1 = sx - x0
            y0i = y0.astype(jnp.int32)
            x0i = x0.astype(jnp.int32)
            P = K2 * Ho * Wo
            xf = x.reshape(B, C, H * W)

            def gather(yi, xi):
                valid = (yi >= 0) & (yi < H) & (xi >= 0) & (xi < W)
                lin = (jnp.clip(yi, 0, H - 1) * W + jnp.clip(xi, 0, W - 1)).reshape(B, P)
                g = jax.vmap(lambda xb, lb: xb[:, lb])(xf, lin)
                return g * valid.reshape(B, 1, P).astype(x.dtype)
            wy1f = wy1.reshape(B, 1, P)
            wx1f = wx1.reshape(B, 1, P)
            g00 = gather(y0i, x0i)
            g01 = gather(y0i, x0i + 1)
            g10 = gather(y0i + 1, x0i)
            g11 = gather(y0i + 1, x0i + 1)
            sampled = (1.0 - wy1f) * ((1.0 - wx1f) * g00 + wx1f * g01) + wy1f * ((1.0 - wx1f) * g10 + wx1f * g11)
            sampled = sampled.reshape(B, C, K2, Ho * Wo)
            wk = weight.reshape(O, C, K2)
            out = jnp.einsum('bckp,ock->bop', sampled, wk).reshape(B, O, Ho, Wo)
            out = out * mod.mean(axis=1, keepdims=True) + bias[None, :, None, None]
            return out
        key = jax.random.key(seed)
        ks = jax.random.split(key, 7)
        B, C, H, W, O = (4, 32, 64, 64, 32)
        x = jax.random.normal(ks[0], (B, C, H, W), jnp.float32)
        weight = jax.random.normal(ks[1], (O, C, K, K), jnp.float32) * 0.05
        bias = jax.random.normal(ks[2], (O,), jnp.float32) * 0.05
        offset_w = jax.random.normal(ks[3], (2 * K2, C, K, K), jnp.float32) * 0.01
        offset_b = jax.random.normal(ks[4], (2 * K2,), jnp.float32) * 0.1
        mod_w = jax.random.normal(ks[5], (K2, C, K, K), jnp.float32) * 0.01
        mod_b = jnp.ones((K2,), jnp.float32)
        return dict(x=x, weight=weight, bias=bias, offset_w=offset_w, offset_b=offset_b, mod_w=mod_w, mod_b=mod_b)
    _L3_conv_all = _L3_conv_setup()
    _L3_conv_in = {k: v for k, v in _L3_conv_all.items() if k in ('weight', 'bias', 'offset_w', 'offset_b', 'mod_w', 'mod_b')}
    del _L3_conv_all
    return {'x': x, 'L0_conv_sigma': _L0_conv_in['sigma'], 'L1_conv_proj_weight': _L1_conv_in['proj_weight'], 'L1_conv_proj_bias': _L1_conv_in['proj_bias'], 'L1_conv_bn_gamma': _L1_conv_in['bn_gamma'], 'L1_conv_bn_beta': _L1_conv_in['bn_beta'], 'L1_conv_scale_w': _L1_conv_in['scale_w'], 'L1_conv_scale_b': _L1_conv_in['scale_b'], 'L2_conv_w_off': _L2_conv_in['w_off'], 'L2_conv_b_off': _L2_conv_in['b_off'], 'L2_conv_gn_off_g': _L2_conv_in['gn_off_g'], 'L2_conv_gn_off_b': _L2_conv_in['gn_off_b'], 'L2_conv_w_dsc': _L2_conv_in['w_dsc'], 'L2_conv_b_dsc': _L2_conv_in['b_dsc'], 'L2_conv_gn_g': _L2_conv_in['gn_g'], 'L2_conv_gn_b': _L2_conv_in['gn_b'], 'L3_conv_weight': _L3_conv_in['weight'], 'L3_conv_bias': _L3_conv_in['bias'], 'L3_conv_offset_w': _L3_conv_in['offset_w'], 'L3_conv_offset_b': _L3_conv_in['offset_b'], 'L3_conv_mod_w': _L3_conv_in['mod_w'], 'L3_conv_mod_b': _L3_conv_in['mod_b']}

def reference(x, L0_conv_sigma, L1_conv_proj_weight, L1_conv_proj_bias, L1_conv_bn_gamma, L1_conv_bn_beta, L1_conv_scale_w, L1_conv_scale_b, L2_conv_w_off, L2_conv_b_off, L2_conv_gn_off_g, L2_conv_gn_off_b, L2_conv_w_dsc, L2_conv_b_dsc, L2_conv_gn_g, L2_conv_gn_b, L3_conv_weight, L3_conv_bias, L3_conv_offset_w, L3_conv_offset_b, L3_conv_mod_w, L3_conv_mod_b):
    import jax
    import jax.numpy as jnp

    def _L0_conv_ref(x, sigma):
        import jax, jax.numpy as jnp
        import numpy as np
        CHANNELS = 32
        KSIZE = 2 * 5 + 1

        def _gaussian_kernel2d(sigma):
            s = jnp.abs(sigma) + 1e-06
            ax = jnp.arange(KSIZE, dtype=jnp.float32) - (KSIZE - 1) / 2.0
            gauss = jnp.exp(-0.5 * (ax / s) ** 2)
            gauss = gauss / gauss.sum()
            k2d = jnp.outer(gauss, gauss)
            k2d = k2d / k2d.sum()
            return k2d
        k2d = _gaussian_kernel2d(sigma)
        kernel = jnp.broadcast_to(k2d, (CHANNELS, 1, KSIZE, KSIZE))
        pad = (KSIZE - 1) // 2
        out = jax.lax.conv_general_dilated(x, kernel, window_strides=(1, 1), padding=[(pad, pad), (pad, pad)], dimension_numbers=('NCHW', 'OIHW', 'NCHW'), feature_group_count=CHANNELS)
        return out

    def _L1_conv_ref(x, proj_weight, proj_bias, bn_gamma, bn_beta, scale_w, scale_b):
        import jax, jax.numpy as jnp
        import numpy as np
        K = 3
        PAD = 1
        EPS = 1e-05
        N, C, H, W = x.shape
        xp = jnp.pad(x, ((0, 0), (0, 0), (PAD, PAD), (PAD, PAD)), mode='wrap')
        w = proj_weight.reshape(-1, C, K, K)
        h = jax.lax.conv_general_dilated(xp, w, window_strides=(1, 1), padding='VALID', dimension_numbers=('NCHW', 'OIHW', 'NCHW'))
        h = h + proj_bias[None, :, None, None]
        h = jax.nn.silu(h)
        mu = h.mean(axis=(0, 2, 3), keepdims=True)
        var = jnp.mean((h - mu) ** 2, axis=(0, 2, 3), keepdims=True)
        hn = (h - mu) * jax.lax.rsqrt(var + EPS)
        hn = hn * bn_gamma[None, :, None, None] + bn_beta[None, :, None, None]
        pooled = hn.mean(axis=(2, 3))
        logits = pooled @ scale_w.T + scale_b
        scale = jax.nn.sigmoid(logits)[:, :, None, None]
        return jax.nn.silu(x * scale + 0.1 * x)

    def _L2_conv_ref(x, w_off, b_off, gn_off_g, gn_off_b, w_dsc, b_dsc, gn_g, gn_b):
        import jax, jax.numpy as jnp
        import numpy as np
        K = 9
        CENTER = K // 2
        EXTEND = 1.0
        EPS = 1e-05
        B, C, O, H, W = (4, 32, 32, 64, 64)

        def group_norm(x, gamma, beta, groups, eps=EPS):
            b, c, h, w = x.shape
            xg = x.reshape(b, groups, c // groups, h, w)
            mu = xg.mean(axis=(2, 3, 4), keepdims=True)
            var = xg.var(axis=(2, 3, 4), keepdims=True)
            xg = (xg - mu) / jnp.sqrt(var + eps)
            return xg.reshape(b, c, h, w) * gamma[None, :, None, None] + beta[None, :, None, None]

        def bilinear_sample(img, ym, xm):
            c, h, w = img.shape
            y0 = jnp.floor(ym)
            x0 = jnp.floor(xm)
            wy = ym - y0
            wx = xm - x0
            y0i = jnp.clip(y0.astype(jnp.int32), 0, h - 1)
            x0i = jnp.clip(x0.astype(jnp.int32), 0, w - 1)
            y1i = jnp.clip(y0i + 1, 0, h - 1)
            x1i = jnp.clip(x0i + 1, 0, w - 1)
            g00 = img[:, y0i, x0i]
            g01 = img[:, y0i, x1i]
            g10 = img[:, y1i, x0i]
            g11 = img[:, y1i, x1i]
            return g00 * (1 - wy) * (1 - wx) + g01 * (1 - wy) * wx + g10 * wy * (1 - wx) + g11 * wy * wx
        b, c, h, w = x.shape
        off = jax.lax.conv_general_dilated(x, w_off, (1, 1), ((1, 1), (1, 1)), dimension_numbers=('NCHW', 'OIHW', 'NCHW')) + b_off[None, :, None, None]
        off = group_norm(off, gn_off_g, gn_off_b, groups=K)
        off = jnp.tanh(off)
        y_off = off[:, :K]
        up = jnp.cumsum(y_off[:, CENTER + 1:], axis=1)
        down = jnp.cumsum(y_off[:, :CENTER][:, ::-1], axis=1)[:, ::-1]
        zero = jnp.zeros_like(y_off[:, :1])
        y_off_new = jnp.concatenate([down, zero, up], axis=1)
        y_new = jnp.arange(h, dtype=x.dtype)[None, None, :, None] + y_off_new * EXTEND
        x_spread = jnp.linspace(-CENTER, CENTER, K, dtype=x.dtype)
        x_new = jnp.arange(w, dtype=x.dtype)[None, None, None, :] + x_spread[None, :, None, None]
        x_new = jnp.broadcast_to(x_new, y_new.shape)
        ymap = jnp.transpose(y_new, (0, 2, 1, 3)).reshape(b, h * K, w)
        xmap = jnp.transpose(x_new, (0, 2, 1, 3)).reshape(b, h * K, w)
        ymap = jnp.clip(ymap, 0.0, h - 1)
        xmap = jnp.clip(xmap, 0.0, w - 1)
        deformed = jax.vmap(bilinear_sample)(x, ymap, xmap)
        d5 = deformed.reshape(b, c, h, K, w)
        out = jnp.einsum('bchkw,ock->bohw', d5, w_dsc[:, :, :, 0]) + b_dsc[None, :, None, None]
        out = group_norm(out, gn_g, gn_b, groups=out.shape[1] // 4)
        return jax.nn.relu(out)

    def _L3_conv_ref(x, weight, bias, offset_w, offset_b, mod_w, mod_b):
        import jax, jax.numpy as jnp
        import numpy as np
        K = 3
        STRIDE = 1
        PAD = 1
        DIL = 1
        K2 = K * K

        def conv2d(x, w, b):
            y = jax.lax.conv_general_dilated(x, w, window_strides=(STRIDE, STRIDE), padding=[(PAD, PAD), (PAD, PAD)], rhs_dilation=(DIL, DIL), dimension_numbers=('NCHW', 'OIHW', 'NCHW'))
            return y + b[None, :, None, None]

        def _forward(x, weight, bias, offset_w, offset_b, mod_w, mod_b):
            B, C, H, W = x.shape
            O = weight.shape[0]
            offsets = conv2d(x, offset_w, offset_b)
            mod = jax.nn.sigmoid(conv2d(x, mod_w, mod_b))
            Ho, Wo = (offsets.shape[2], offsets.shape[3])
            off = offsets.reshape(B, 2, K2, Ho, Wo)
            base_y = jnp.arange(Ho, dtype=x.dtype) * STRIDE - PAD + K // 2 * DIL
            base_x = jnp.arange(Wo, dtype=x.dtype) * STRIDE - PAD + K // 2 * DIL
            sy = base_y[None, None, :, None] + off[:, 0]
            sx = base_x[None, None, None, :] + off[:, 1]
            y0 = jnp.floor(sy)
            x0 = jnp.floor(sx)
            wy1 = sy - y0
            wx1 = sx - x0
            y0i = y0.astype(jnp.int32)
            x0i = x0.astype(jnp.int32)
            P = K2 * Ho * Wo
            xf = x.reshape(B, C, H * W)

            def gather(yi, xi):
                valid = (yi >= 0) & (yi < H) & (xi >= 0) & (xi < W)
                lin = (jnp.clip(yi, 0, H - 1) * W + jnp.clip(xi, 0, W - 1)).reshape(B, P)
                g = jax.vmap(lambda xb, lb: xb[:, lb])(xf, lin)
                return g * valid.reshape(B, 1, P).astype(x.dtype)
            wy1f = wy1.reshape(B, 1, P)
            wx1f = wx1.reshape(B, 1, P)
            g00 = gather(y0i, x0i)
            g01 = gather(y0i, x0i + 1)
            g10 = gather(y0i + 1, x0i)
            g11 = gather(y0i + 1, x0i + 1)
            sampled = (1.0 - wy1f) * ((1.0 - wx1f) * g00 + wx1f * g01) + wy1f * ((1.0 - wx1f) * g10 + wx1f * g11)
            sampled = sampled.reshape(B, C, K2, Ho * Wo)
            wk = weight.reshape(O, C, K2)
            out = jnp.einsum('bckp,ock->bop', sampled, wk).reshape(B, O, Ho, Wo)
            out = out * mod.mean(axis=1, keepdims=True) + bias[None, :, None, None]
            return out
        return _forward(x, weight, bias, offset_w, offset_b, mod_w, mod_b)

    def _gn(v, G=32, eps=1e-05):
        B_, C_, H_, W_ = v.shape
        g = v.reshape(B_, G, C_ // G, H_, W_)
        m = jnp.mean(g, axis=(2, 3, 4), keepdims=True)
        s = jnp.var(g, axis=(2, 3, 4), keepdims=True)
        return ((g - m) / jnp.sqrt(s + eps)).reshape(v.shape)

    def _ln_c(v, eps=1e-06):
        m = jnp.mean(v, axis=1, keepdims=True)
        s = jnp.var(v, axis=1, keepdims=True)
        return (v - m) / jnp.sqrt(s + eps)

    def _ln_t(v, eps=1e-05):
        m = jnp.mean(v, axis=-1, keepdims=True)
        s = jnp.var(v, axis=-1, keepdims=True)
        return (v - m) / jnp.sqrt(s + eps)

    def _to_tokens(v):
        B_, C_, H_, W_ = v.shape
        return v.reshape(B_, C_, H_ * W_).transpose(0, 2, 1)

    def _from_tokens(t, like):
        B_, C_, H_, W_ = like.shape
        return t.transpose(0, 2, 1).reshape(B_, C_, H_, W_)
    x = x + _L0_conv_ref(_gn(x), L0_conv_sigma)
    x = x + _L1_conv_ref(_gn(x), L1_conv_proj_weight, L1_conv_proj_bias, L1_conv_bn_gamma, L1_conv_bn_beta, L1_conv_scale_w, L1_conv_scale_b)
    x = x + _L2_conv_ref(_gn(x), L2_conv_w_off, L2_conv_b_off, L2_conv_gn_off_g, L2_conv_gn_off_b, L2_conv_w_dsc, L2_conv_b_dsc, L2_conv_gn_g, L2_conv_gn_b)
    x = x + _L3_conv_ref(_gn(x), L3_conv_weight, L3_conv_bias, L3_conv_offset_w, L3_conv_offset_b, L3_conv_mod_w, L3_conv_mod_b)
    return x

_drawn_inputs = setup_inputs


def setup_inputs(seed=0):
    import zlib

    import numpy as np

    out = dict(_drawn_inputs(seed))
    spreads = {'L1_conv_proj_bias': (0.0, 0.8),
     'L1_conv_bn_gamma': (1.0, 0.6),
     'L1_conv_bn_beta': (0.0, 0.739),
     'L1_conv_scale_b': (0.0, 0.713),
     'L2_conv_b_off': (0.0, 0.1),
     'L2_conv_gn_off_g': (1.0, 0.2),
     'L2_conv_gn_off_b': (0.0, 0.1),
     'L2_conv_b_dsc': (0.0, 0.1),
     'L2_conv_gn_g': (1.0, 0.2),
     'L2_conv_gn_b': (0.0, 0.1),
     'L3_conv_mod_b': (1.0, 0.6)}
    factors = {'L1_conv_proj_weight': 8.0, 'L1_conv_scale_w': 4.438, 'L3_conv_mod_w': 8.0}
    for name, (base, spread) in spreads.items():
        noise = np.random.default_rng([zlib.crc32(name.encode()), seed]).standard_normal(out[name].shape)
        drawn = base * np.exp(spread * noise) if base else spread * noise
        out[name] = jnp.asarray(drawn.astype(out[name].dtype))
    for name, factor in factors.items():
        out[name] = (out[name] * factor).astype(out[name].dtype)
    return out
```

```python
from contextlib import ExitStack

import concourse.bass as bass
from concourse import mybir

F32 = mybir.dt.float32
I32 = mybir.dt.int32
U32 = mybir.dt.uint32
ALU = mybir.AluOpType
ACT = mybir.ActivationFunctionType
AX = mybir.AxisListType

B, C, H, W = 8, 32, 128, 128
P = 128
GI = P // C
NG = B // GI
PX = H * W
BANK = 512
GN_EPS = 1e-5


class Space:

    def __init__(self, nc, ctx, tag):
        self.nc, self.ctx, self.tag = nc, ctx, tag
        self.sems = []
        ctx.callback(self.close)

    def sb(self, name, shape, dt=F32):
        return self.ctx.enter_context(self.nc.sbuf_tensor(f"{self.tag}_{name}", shape, dt))

    def ps(self, name, shape=(P, BANK), dt=F32):
        return self.ctx.enter_context(self.nc.psum_tensor(f"{self.tag}_{name}", list(shape), dt))

    def sem(self, name):
        self.sems.append(self.nc.alloc_semaphore(f"{self.tag}_{name}"))
        return self.sems[-1]

    def close(self):
        if self.sems:
            self.nc.clear_and_free_semaphores(self.sems)
            self.nc.all_engine_barrier()


def in_pairs(eng, n, body):
    body(0, 0, True)
    body(1, 1, True)
    if n > 2:
        with eng.Fori(1, n // 2) as i:
            body(i * 2, 0, False)
            body(i * 2 + 1, 1, False)


def turn(t):
    return t // 2
SNAKE_TAPS = (0, 8, 1, 7, 2, 6, 3, 5)


def in_pairs_last(eng, n, body):
    body(0, 0, True, False)
    body(1, 1, True, False)
    with eng.Fori(1, n // 2 - 1) as i:
        body(i * 2, 0, False, False)
        body(i * 2 + 1, 1, False, False)
    body(n - 2, 0, False, False)
    body(n - 1, 1, False, True)


OFFS = GI * 18 + GI


def blur(nc, x, sigma, x1):
    NB = 16
    CH = B * C // NB
    COLS = NB * W
    Q = COLS // BANK
    R = 5
    K = 2 * R + 1
    x_v = x.rearrange("b c h w -> h (b c) w")
    x1_v = x1.rearrange("b c h w -> h (b c) w")

    with ExitStack() as ctx:
        s = Space(nc, ctx, "blur")
        xs = [s.sb(f"x{i}", [P, NB, W]) for i in range(2)]
        cen = [s.sb(f"centred{i}", [P, NB, W]) for i in range(2)]
        squares = s.sb("squares", [P, NB, W])
        rowsum = s.sb("rowsum", [P, NB])
        sqsum = s.sb("sqsum", [P, NB])
        std = s.sb("std", [P, NB])
        rstd = s.sb("rstd", [P, NB])
        half = s.sb("half", [P, Q, BANK])
        mean_w = s.sb("mean_w", [P, P])
        band = s.sb("band", [P, P])
        dist = s.sb("dist", [P, P])
        term = s.sb("term", [P, P])
        sg = s.sb("sigma", [P, 1])
        rs = s.sb("rsigma", [P, 1])
        ax = s.sb("ax", [P, K])
        ax2 = s.sb("ax2", [P, K])
        g = s.sb("g", [P, K])
        gs = s.sb("gsum", [P, 1])
        eps = s.sb("eps", [P, 1])
        p_stat = s.ps("stat", [P, 2, 32])
        p_half = [s.ps(f"half{i}") for i in range(2)]
        p_out = [s.ps(f"out{i}") for i in range(Q)]

        sigma_in = s.sem("sigma_in")
        iota_done = s.sem("iota_done")
        chain = s.sem("vector_chain")
        exp_in = s.sem("exp_in")
        exp_done = s.sem("exp_done")
        consts = s.sem("constants_ready")
        loaded = [s.sem(f"loaded{i}") for i in range(2)]
        stored = [s.sem(f"stored{i}") for i in range(2)]
        rowsum_ready = s.sem("rowsum_ready")
        mean_ready = s.sem("mean_ready")
        centred = s.sem("centred")
        squared = s.sem("squared")
        sqsum_ready = s.sem("sqsum_ready")
        var_ready = s.sem("var_ready")
        std_ready = s.sem("std_ready")
        rstd_ready = s.sem("rstd_ready")
        normed = s.sem("normed")
        half_ready = s.sem("half_ready")
        half_copied = s.sem("half_copied")
        out_ready = s.sem("out_ready")
        x1_ready = s.sem("x1_ready")
        block = ctx.enter_context(nc.Block())

        @block.sync
        def _(sp):
            sp.dma_start(sg[:, :], bass.AP(tensor=sigma.tensor, offset=0, ap=[[0, P], [1, 1]])).then_inc(sigma_in, 16)

            def load(t, slot, first):
                if not first:
                    sp.wait_ge(stored[slot], turn(t) * 16)
                sp.dma_start(xs[slot][:, :, :], x_v[:, t * NB:(t + 1) * NB, :]).then_inc(loaded[slot], 16)

            for t in range(CH):
                load(t, t % 2, t < 2)
            for slot in range(2):
                sp.wait_ge(stored[slot], CH // 2 * 16)

        @block.gpsimd
        def _(pool):
            pool.iota(dist[:, :], pattern=[[1, P]], base=0, channel_multiplier=-1,
                      allow_small_or_imprecise_dtypes=True).then_inc(iota_done, 1)
            pool.iota(ax[:, :], pattern=[[1, K]], base=-R, channel_multiplier=0,
                      allow_small_or_imprecise_dtypes=True).then_inc(iota_done, 1)

            def norm(t, slot, first):
                pool.wait_ge(rstd_ready, t + 1)
                pool.tensor_tensor(cen[slot][:, :, :], cen[slot][:, :, :], rstd[:, :].unsqueeze(2).to_broadcast((P, NB, W)),
                                   ALU.mult).then_inc(normed, 1)

            in_pairs(pool, CH, norm)

        @block.scalar
        def _(act):
            act.wait_ge(exp_in, 1)
            act.activation(g[:, :], ax2[:, :], ACT.Exp, scale=-0.5).then_inc(exp_done, 1)

            def store(t, slot):
                act.wait_ge(x1_ready, t + 1)
                act.dma_start(x1_v[:, bass.ds(t * NB, NB), :], xs[slot][:, :, :]).then_inc(stored[slot], 16)

            def chunk(t, slot, first):
                act.wait_ge(centred, t + 1)
                if not (first and slot == 0):
                    act.wait_ge(sqsum_ready, t)
                act.activation(squares[:, :, :], cen[slot][:, :, :], ACT.Square).then_inc(squared, 1)
                if not (first and slot == 0):
                    store(t - 1, 1 - slot)
                act.wait_ge(var_ready, t + 1)
                act.activation(std[:, :], p_stat[:, 1, 0:NB], ACT.Sqrt, bias=eps[:, :]).then_inc(std_ready, 1)
                for q in range(Q):
                    act.wait_ge(half_ready, t * Q + q + 1)
                    if not (first and slot == 0):
                        act.wait_ge(out_ready, (t - 1) * Q + q + 1)
                    act.activation(half[:, q, :], p_half[q % 2][:, :], ACT.Copy).then_inc(half_copied, 1)

            in_pairs(act, CH, chunk)
            store(CH - 1, 1)

        @block.vector
        def _(dve):
            n = [0]

            def link(ins):
                n[0] += 1
                ins.then_inc(chain, 1)
                dve.wait_ge(chain, n[0])

            dve.memset(mean_w[:, :], 1.0 / PX)
            dve.memset(eps[:, :], GN_EPS)
            dve.wait_ge(sigma_in, 16)
            link(dve.tensor_scalar(rs[:, :], sg[:, :], -1.0, None, ALU.mult))
            link(dve.tensor_tensor(rs[:, :], rs[:, :], sg[:, :], ALU.max))
            link(dve.tensor_scalar(rs[:, :], rs[:, :], 1e-6, None, ALU.add))
            link(dve.reciprocal(rs[:, :], rs[:, :]))
            dve.wait_ge(iota_done, 2)
            link(dve.tensor_scalar(ax[:, :], ax[:, :], rs[:, :], None, ALU.mult))
            dve.tensor_tensor(ax2[:, :], ax[:, :], ax[:, :], ALU.mult).then_inc(exp_in, 1)
            dve.wait_ge(exp_done, 1)
            for _ in range(2):
                link(dve.tensor_reduce(gs[:, :], g[:, :], AX.X, ALU.add))
                link(dve.reciprocal(gs[:, :], gs[:, :]))
                link(dve.tensor_scalar(g[:, :], g[:, :], gs[:, :], None, ALU.mult))
            link(dve.tensor_scalar(band[:, :], dist[:, :], float(-R), g[:, 0:1], ALU.is_equal, ALU.mult))
            for k in range(1, K):
                link(dve.tensor_scalar(term[:, :], dist[:, :], float(k - R), g[:, k:k + 1], ALU.is_equal, ALU.mult))
                ins = dve.tensor_tensor(band[:, :], band[:, :], term[:, :], ALU.add)
                if k < K - 1:
                    link(ins)
            ins.then_inc(consts, 1)

            def finish(t, slot):
                for q in range(Q):
                    dve.wait_ge(out_ready, t * Q + q + 1)
                    v = xs[slot][:, :, :].rearrange("p n w -> p (n w)")[:, q * BANK:(q + 1) * BANK]
                    ins = dve.tensor_tensor(v, v, p_out[q][:, :], ALU.add)
                ins.then_inc(x1_ready, 1)

            def chunk(t, slot, first):
                dve.wait_ge(loaded[slot], turn(t) * 16 + 16)
                if not (first and slot == 0):
                    dve.wait_ge(mean_ready, t)
                dve.tensor_reduce(rowsum[:, :], xs[slot][:, :, :], AX.X, ALU.add).then_inc(rowsum_ready, 1)
                if not (first and slot == 0):
                    finish(t - 1, 1 - slot)
                dve.wait_ge(mean_ready, t + 1)
                dve.tensor_tensor(cen[slot][:, :, :], xs[slot][:, :, :],
                                  p_stat[:, 0, 0:NB].unsqueeze(2).to_broadcast((P, NB, W)), ALU.subtract).then_inc(centred, 1)
                dve.wait_ge(squared, t + 1)
                dve.tensor_reduce(sqsum[:, :], squares[:, :, :], AX.X, ALU.add).then_inc(sqsum_ready, 1)
                dve.wait_ge(std_ready, t + 1)
                if not (first and slot == 0):
                    dve.wait_ge(normed, t)
                dve.reciprocal(rstd[:, :], std[:, :]).then_inc(rstd_ready, 1)

            in_pairs(dve, CH, chunk)
            finish(CH - 1, 1)

        @block.tensor
        def _(pe):
            pe.wait_ge(consts, 1)

            def chunk(t, slot, first):
                pe.wait_ge(rowsum_ready, t + 1)
                if not (first and slot == 0):
                    pe.wait_ge(centred, t)
                pe.matmul(p_stat[:, 0, 0:NB], mean_w[:, :], rowsum[:, :], start=True, stop=True).then_inc(mean_ready, 1)
                pe.wait_ge(sqsum_ready, t + 1)
                pe.matmul(p_stat[:, 1, 0:NB], mean_w[:, :], sqsum[:, :], start=True, stop=True).then_inc(var_ready, 1)
                pe.wait_ge(normed, t + 1)

                def along_h(q):
                    if not (first and slot == 0 and q < 2):
                        pe.wait_ge(half_copied, t * Q + q - 1)
                    for j in range(4):
                        ins = pe.matmul(p_half[q % 2][:, j * W:(j + 1) * W], cen[slot][:, q * 4 + j, :], band[:, :],
                                        start=True, stop=True)
                    ins.then_inc(half_ready, 1)

                def along_w(q):
                    pe.wait_ge(half_copied, t * Q + q + 1)
                    if q == 0 and not (first and slot == 0):
                        pe.wait_ge(x1_ready, t)
                    for j in range(4):
                        ins = pe.matmul(p_out[q][:, j * W:(j + 1) * W], half[:, q, j * W:(j + 1) * W], band[:, :],
                                        start=True, stop=True)
                    ins.then_inc(out_ready, 1)

                along_h(0)
                for q in range(1, Q):
                    along_h(q)
                    along_w(q - 1)
                along_w(Q - 1)

            in_pairs(pe, CH, chunk)


class Kept:

    VECTORS = ['L1_conv_proj_bias', 'L1_conv_bn_gamma', 'L1_conv_bn_beta', 'L1_conv_scale_b', 'L2_conv_b_off',
               'L2_conv_gn_off_g', 'L2_conv_gn_off_b', 'L2_conv_b_dsc', 'L2_conv_gn_g', 'L2_conv_gn_b', 'L3_conv_bias']
    N_PAR = len(VECTORS) + 1

    def __init__(self, nc, ctx):
        s = Space(nc, ctx, "kept")
        self.const = s.sb("const", [P, 4 * P + 32])
        self.ident = self.const[:, 0:P]
        self.pair_mean = self.const[:, P:2 * P]
        self.quad_mean = self.const[:, 2 * P:3 * P]
        self.image_mean = self.const[:, 3 * P:4 * P]
        self.cumulate = self.const[:, 4 * P:4 * P + 32]
        self.par = s.sb("par", [P, self.N_PAR])
        self.w_gate = s.sb("w_gate", [P, 9, P])
        self.w_scale = s.sb("w_scale", [P, 1, P])
        self.w_off2 = s.sb("w_off2", [P, 9, P])
        self.w_dsc = s.sb("w_dsc", [P, 9, P])
        self.w_off3 = s.sb("w_off3", [P, 9, P])
        self.w_dcn = s.sb("w_dcn", [P, 9, P])
        self.eps = s.sb("eps", [P, 1])
        self.norm1 = s.sb("norm1", [P, NG, 2])
        self.hidden = s.sb("hidden", [P, NG, 2])
        self.gate = s.sb("gate", [P, NG, 2])
        self.dense = s.sb("dense", [1, 1], I32)
        self.snake_gn = s.sb("snake_gn", [P, 2])

    def vec(self, name):
        i = self.VECTORS.index(name)
        return self.par[:, i:i + 1]

    @property
    def bias3(self):
        return self.par[:, self.N_PAR - 1:self.N_PAR]


def make_weights(nc, a, k):
    jobs = [(k.w_gate, [('L1_conv_proj_weight', 0, 32)], 9), (k.w_scale, [('L1_conv_scale_w', 0, 32)], 1),
            (k.w_off2, [('L2_conv_w_off', 0, 18)], 9), (k.w_dsc, [('L2_conv_w_dsc', 0, 32)], 9),
            (k.w_off3, [('L3_conv_offset_w', 0, 18), ('L3_conv_mod_w', 18, 9)], 9), (k.w_dcn, [('L3_conv_weight', 0, 32)], 9)]
    with ExitStack() as ctx:
        s = Space(nc, ctx, "weights")
        nat = [s.sb(f"nat{n}", [P, C, j[2]]) for n, j in enumerate(jobs)]
        big = [s.sb(f"big{n}", [P, j[2], P]) for n, j in enumerate(jobs)]
        rows = s.sb("rows", [k.N_PAR, GI, 32])
        tr = [s.ps(f"tr{i}") for i in range(4)]
        cleared = s.sem("cleared")
        const_in = s.sem("const_in")
        rows_in = s.sem("rows_in")
        nat_in = s.sem("nat_in")
        blocks = s.sem("blocks")
        turned = s.sem("turned")
        copied = s.sem("copied")
        turns = [(n, t0, min(4, j[2] - t0)) for n, j in enumerate(jobs) for t0 in range(0, j[2], 4)]
        block = ctx.enter_context(nc.Block())

        @block.gpsimd
        def _(pool):
            pool.memset(rows[:, :, :], 0.0).then_inc(cleared, 1)
            for n in range(len(jobs)):
                pool.memset(nat[n][:, :, :], 0.0).then_inc(cleared, 1)

        @block.sync
        def _(sp):
            sp.dma_start(k.const[:, :], a["const"]).then_inc(const_in, 16)
            sp.wait_ge(cleared, 1)
            for i, name in enumerate(k.VECTORS + ['L3_conv_offset_b']):
                n = a[name].shape[0]
                sp.dma_start(rows[i:i + 1, :, 0:n], bass.AP(tensor=a[name].tensor, offset=0, ap=[[0, 1], [0, GI], [1, n]])).then_inc(rows_in, 16)
            sp.dma_start(rows[k.N_PAR - 1:k.N_PAR, :, 18:27],
                         bass.AP(tensor=a['L3_conv_mod_b'].tensor, offset=0, ap=[[0, 1], [0, GI], [1, 9]])).then_inc(rows_in, 16)
            sp.wait_ge(cleared, 1 + len(jobs))
            for n, (_, parts, taps) in enumerate(jobs):
                for name, o0, no in parts:
                    src = bass.AP(tensor=a[name].tensor, offset=0, ap=[[C * taps, no], [1, C * taps]])
                    for b in range(GI):
                        sp.dma_start(nat[n][32 * b + o0:32 * b + o0 + no, :, :].rearrange("p c t -> p (c t)"), src).then_inc(nat_in, 16)

        @block.vector
        def _(dve):
            dve.memset(k.eps[:, :], GN_EPS)
            for n in range(len(jobs)):
                ins = dve.memset(big[n][:, :, :], 0.0)
            ins.then_inc(blocks, 1)
            dve.wait_ge(blocks, 1)
            dve.wait_ge(nat_in, 16 * GI * sum(len(j[1]) for j in jobs))
            for n in range(len(jobs)):
                for b in range(GI):
                    r = slice(32 * b, 32 * b + 32)
                    ins = dve.tensor_copy(big[n][r, :, r], nat[n][r, :, :].rearrange("p c t -> p t c"))
            ins.then_inc(blocks, 1)

        @block.tensor
        def _(pe):
            pe.wait_ge(const_in, 16)
            pe.wait_ge(rows_in, 16 * (k.N_PAR + 1))
            pe.transpose(tr[0][:, 0:k.N_PAR], rows[:, :, :].rearrange("v b o -> v (b o)"), k.ident[0:k.N_PAR, 0:k.N_PAR]).then_inc(turned, 1)
            pe.wait_ge(blocks, 2)
            for i, (n, t0, nt) in enumerate(turns, 1):
                if i >= 4:
                    pe.wait_ge(copied, i - 3)
                for t in range(nt):
                    ins = pe.transpose(tr[i % 4][:, t * P:(t + 1) * P], big[n][:, t0 + t, :], k.ident)
                ins.then_inc(turned, 1)

        @block.scalar
        def _(act):
            act.wait_ge(turned, 1)
            act.activation(k.par[:, :], tr[0][:, 0:k.N_PAR], ACT.Copy).then_inc(copied, 1)
            for i, (n, t0, nt) in enumerate(turns, 1):
                act.wait_ge(turned, i + 1)
                act.activation(jobs[n][0][:, t0:t0 + nt, :].rearrange("p t o -> p (t o)"), tr[i % 4][:, 0:nt * P],
                               ACT.Copy).then_inc(copied, 1)


PAD = 4
HP = H + 2 * PAD


def gate_conv(nc, k, x1, g):
    x1_v = x1.rearrange("(g b) c h w -> g (b c) h w", g=NG)[g]
    LR = 16
    NL = H // LR
    UR = BANK // W
    NU = H // UR
    with ExitStack() as ctx:
        s = Space(nc, ctx, f"gateconv{g}")
        xg = s.sb("x", [P, H, W])
        xn = s.sb("xn", [P, H + 2, W + 2])
        st = s.sb("stats", [P, NU, 6])
        mv = s.sb("mean_var", [P, 2])
        std = s.sb("std", [P, 1])
        hid = [s.sb(f"hid{i}", [P, BANK]) for i in range(2)]
        hst = s.sb("hid_stats", [P, NU, 6])
        acc = [s.ps(f"acc{i}") for i in range(2)]
        loaded = [s.sem(f"loaded{i}") for i in range(NL)]
        chain = s.sem("vector_chain")
        var_ready = s.sem("var_ready")
        std_ready = s.sem("std_ready")
        coef_ready = s.sem("coef_ready")
        normed = s.sem("normed")
        padded = s.sem("padded")
        conv_done = s.sem("conv_done")
        hid_ready = s.sem("hid_ready")
        hid_used = s.sem("hid_used")
        block = ctx.enter_context(nc.Block())

        @block.sync
        def _(sp):
            for l in range(NL):
                sp.dma_start(xg[:, l * LR:(l + 1) * LR, :], x1_v[:, l * LR:(l + 1) * LR, :]).then_inc(loaded[l], 16)

        @block.vector
        def _(dve):
            n = [0]

            def link(ins):
                n[0] += 1
                ins.then_inc(chain, 1)
                dve.wait_ge(chain, n[0])

            for u in range(NU):
                if u % (LR // UR) == 0:
                    dve.wait_ge(loaded[u // (LR // UR)], 16)
                ins = dve.bn_stats(st[:, u, :], xg[:, u * UR:(u + 1) * UR, :].rearrange("p h w -> p (h w)"))
            link(ins)
            dve.bn_aggr(mv[:, :], st[:, :, :].rearrange("p u s -> p (u s)")).then_inc(var_ready, 1)
            dve.wait_ge(std_ready, 1)
            link(dve.reciprocal(k.norm1[:, g, 0:1], std[:, :]))
            dve.scalar_tensor_tensor(k.norm1[:, g, 1:2], mv[:, 0:1], -1.0, k.norm1[:, g, 0:1], ALU.mult, ALU.mult).then_inc(coef_ready, 1)
            dve.wait_ge(normed, 1)
            dve.tensor_copy(xn[:, 1:H + 1, 0:1], xn[:, 1:H + 1, W:W + 1])
            link(dve.tensor_copy(xn[:, 1:H + 1, W + 1:W + 2], xn[:, 1:H + 1, 1:2]))
            dve.tensor_copy(xn[:, 0, :], xn[:, H, :])
            dve.tensor_copy(xn[:, H + 1, :], xn[:, 1, :]).then_inc(padded, 1)

            def stats(u, slot, first):
                dve.wait_ge(hid_ready, u + 1)
                dve.bn_stats(hst[:, bass.ds(u, 1), :].rearrange("p u s -> p (u s)"), hid[slot][:, :]).then_inc(hid_used, 1)

            in_pairs(dve, NU, stats)
            dve.wait_ge(hid_used, NU)
            dve.bn_aggr(k.hidden[:, g, :], hst[:, :, :].rearrange("p u s -> p (u s)"))

        @block.scalar
        def _(act):
            act.wait_ge(var_ready, 1)
            act.activation(std[:, :], mv[:, 1:2], ACT.Sqrt, bias=k.eps[:, :]).then_inc(std_ready, 1)
            act.wait_ge(coef_ready, 1)
            act.activation(xn[:, 1:H + 1, 1:W + 1], xg[:, :, :], ACT.Identity, bias=k.norm1[:, g, 1:2],
                           scale=k.norm1[:, g, 0:1]).then_inc(normed, 1)

            def silu(u, slot, first):
                act.wait_ge(conv_done, u + 1)
                if not first:
                    act.wait_ge(hid_used, u - 1)
                act.activation(hid[slot][:, :], acc[slot][:, :], ACT.Silu, bias=k.vec('L1_conv_proj_bias')).then_inc(hid_ready, 1)

            in_pairs(act, NU, silu)

        @block.tensor
        def _(pe):
            pe.wait_ge(padded, 1)

            def conv(u, slot, first):
                if not first:
                    pe.wait_ge(hid_ready, u - 1)
                for t in range(9):
                    dy, dx = divmod(t, 3)
                    ins = pe.matmul(acc[slot][:, :], k.w_gate[:, t, :], xn[:, bass.ds(u * UR + dy, UR), dx:dx + W],
                                    start=(t == 0), stop=(t == 8))
                ins.then_inc(conv_done, 1)

            in_pairs(pe, NU, conv)


def gate_scale(nc, k):
    with ExitStack() as ctx:
        s = Space(nc, ctx, "gatescale")
        mu = s.sb("mu", [P, 1])
        d = s.sb("d", [P, NG])
        e = s.sb("e", [P, NG])
        std = s.sb("std", [P, 1])
        pooled = s.sb("pooled", [P, NG])
        sig = s.sb("sig", [P, NG])
        p_mean = s.ps("mean")
        p_var = s.ps("var")
        p_log = s.ps("logits")
        chain = s.sem("vector_chain")
        mean_ready = s.sem("mean_ready")
        spread_in = s.sem("spread_in")
        spread_ready = s.sem("spread_ready")
        var_in = s.sem("var_in")
        std_ready = s.sem("std_ready")
        pooled_ready = s.sem("pooled_ready")
        logits_ready = s.sem("logits_ready")
        sig_ready = s.sem("sig_ready")
        block = ctx.enter_context(nc.Block())

        @block.tensor
        def _(pe):
            pe.matmul(p_mean[:, 0:NG], k.image_mean, k.hidden[:, :, 0], start=True, stop=True).then_inc(mean_ready, 1)
            pe.wait_ge(spread_in, 1)
            pe.matmul(p_var[:, 0:NG], k.image_mean, e[:, :], start=True, stop=True).then_inc(spread_ready, 1)
            pe.wait_ge(pooled_ready, 1)
            pe.matmul(p_log[:, 0:NG], k.w_scale[:, 0, :], pooled[:, :], start=True, stop=True).then_inc(logits_ready, 1)

        @block.scalar
        def _(act):
            act.wait_ge(var_in, 1)
            act.activation(std[:, :], mu[:, :], ACT.Sqrt, bias=k.eps[:, :], scale=1.0 / NG).then_inc(std_ready, 1)
            act.wait_ge(logits_ready, 1)
            act.activation(sig[:, :], p_log[:, 0:NG], ACT.Sigmoid, bias=k.vec('L1_conv_scale_b')).then_inc(sig_ready, 1)

        @block.vector
        def _(dve):
            n = [0]

            def link(ins):
                n[0] += 1
                ins.then_inc(chain, 1)
                dve.wait_ge(chain, n[0])

            dve.wait_ge(mean_ready, 1)
            link(dve.tensor_reduce(mu[:, :], p_mean[:, 0:NG], AX.X, ALU.add))
            link(dve.tensor_scalar(mu[:, :], mu[:, :], 1.0 / NG, None, ALU.mult))
            link(dve.tensor_scalar(d[:, :], k.hidden[:, :, 0], mu[:, :], None, ALU.subtract))
            link(dve.tensor_tensor(e[:, :], d[:, :], d[:, :], ALU.mult))
            dve.tensor_tensor(e[:, :], e[:, :], k.hidden[:, :, 1], ALU.add).then_inc(spread_in, 1)
            dve.wait_ge(spread_ready, 1)
            dve.tensor_reduce(mu[:, :], p_var[:, 0:NG], AX.X, ALU.add).then_inc(var_in, 1)
            dve.wait_ge(std_ready, 1)
            link(dve.reciprocal(std[:, :], std[:, :]))
            link(dve.tensor_tensor(std[:, :], std[:, :], k.vec('L1_conv_bn_gamma'), ALU.mult))
            dve.tensor_scalar(pooled[:, :], d[:, :], std[:, :], k.vec('L1_conv_bn_beta'), ALU.mult, ALU.add).then_inc(pooled_ready, 1)
            dve.wait_ge(sig_ready, 1)
            link(dve.tensor_scalar(sig[:, :], sig[:, :], 0.1, None, ALU.add))
            dve.tensor_tensor(k.gate[:, :, :], k.norm1[:, :, :], sig[:, :].unsqueeze(2).to_broadcast((P, NG, 2)), ALU.mult)


def residual(nc, k, base, inner, func, scale, bias, result, xn, g):
    base_v, result_v = (t.rearrange("(g b) c h w -> g (b c) h w", g=NG)[g] for t in (base, result))
    UR = 8
    NU = H // UR
    HALF = UR // 2
    with ExitStack() as ctx:
        s = Space(nc, ctx, f"residual{g}{func.name}")
        xg = s.sb("x", [P, H, W])
        act_out = [s.sb(f"act{i}", [P, UR, W]) for i in range(2)]
        st = s.sb("stats", [P, 2 * NU, 6])
        mv = s.sb("mean_var", [P, 2])
        std = s.sb("std", [P, 1])
        coef = s.sb("coef", [P, 2])
        loaded = [s.sem(f"loaded{i}") for i in range(NU)]
        inner_loaded = [s.sem(f"inner_loaded{i}") for i in range(2)]
        chain = s.sem("vector_chain")
        act_ready = s.sem("act_ready")
        sum_ready = s.sem("sum_ready")
        stored = s.sem("stored")
        var_ready = s.sem("var_ready")
        std_ready = s.sem("std_ready")
        coef_ready = s.sem("coef_ready")
        block = ctx.enter_context(nc.Block())

        @block.sync
        def _(sp):
            for u in range(NU):
                if inner is not None:
                    if u >= 2:
                        sp.wait_ge(sum_ready, u - 1)
                    sp.dma_start(act_out[u % 2][:, :, :], inner[:, u * UR:(u + 1) * UR, :]).then_inc(inner_loaded[u % 2], 16)
                sp.dma_start(xg[:, u * UR:(u + 1) * UR, :], base_v[:, u * UR:(u + 1) * UR, :]).then_inc(loaded[u], 16)

        @block.gpsimd
        def _(pool):
            for r in (PAD - 1, PAD + H):
                pool.memset(xn[:, r, PAD - 1:PAD + W + 1], 0.0)
            for c in (PAD - 1, PAD + W):
                pool.memset(xn[:, PAD:PAD + H, c:c + 1], 0.0)
            for u in range(NU):
                pool.wait_ge(sum_ready, u + 1)
                pool.dma_start(result_v[:, u * UR:(u + 1) * UR, :], xg[:, u * UR:(u + 1) * UR, :]).then_inc(stored, 16)
            pool.wait_ge(stored, 16 * NU)

        @block.scalar
        def _(act):
            for u in range(NU):
                if inner is not None:
                    act.wait_ge(inner_loaded[u % 2], 16 * (u // 2 + 1))
                    src = act_out[u % 2][:, :, :]
                else:
                    act.wait_ge(loaded[u], 16)
                    if u >= 2:
                        act.wait_ge(sum_ready, u - 1)
                    src = xg[:, u * UR:(u + 1) * UR, :]
                act.activation(act_out[u % 2][:, :, :], src, func, bias=bias, scale=scale).then_inc(act_ready, 1)
            act.wait_ge(var_ready, 1)
            act.activation(std[:, :], mv[:, 1:2], ACT.Sqrt, bias=k.eps[:, :]).then_inc(std_ready, 1)
            act.wait_ge(coef_ready, 1)
            act.activation(xn[:, PAD:PAD + H, PAD:PAD + W], xg[:, :, :], ACT.Identity, bias=coef[:, 1:2], scale=coef[:, 0:1])

        @block.vector
        def _(dve):
            n = [0]

            def link(ins):
                n[0] += 1
                ins.then_inc(chain, 1)
                dve.wait_ge(chain, n[0])

            for u in range(NU):
                dve.wait_ge(loaded[u], 16)
                dve.wait_ge(act_ready, u + 1)
                v = xg[:, u * UR:(u + 1) * UR, :]
                dve.tensor_tensor(v, v, act_out[u % 2][:, :, :], ALU.add).then_inc(sum_ready, 1)
                dve.wait_ge(sum_ready, u + 1)
                for i in range(2):
                    ins = dve.bn_stats(st[:, 2 * u + i, :], xg[:, u * UR + i * HALF:u * UR + (i + 1) * HALF, :].rearrange("p h w -> p (h w)"))
            link(ins)
            dve.bn_aggr(mv[:, :], st[:, :, :].rearrange("p u s -> p (u s)")).then_inc(var_ready, 1)
            dve.wait_ge(std_ready, 1)
            link(dve.reciprocal(coef[:, 0:1], std[:, :]))
            dve.scalar_tensor_tensor(coef[:, 1:2], mv[:, 0:1], -1.0, coef[:, 0:1], ALU.mult, ALU.mult).then_inc(coef_ready, 1)


def snake_offsets(nc, k, xn, off, g):
    UR = BANK // W
    NU = H // UR
    TR = 8
    NT = H // TR
    with ExitStack() as ctx:
        s = Space(nc, ctx, f"snakeoff{g}")
        raw = s.sb("raw", [P, H, W])
        tanh = [s.sb(f"tanh{i}", [P, TR, W]) for i in range(2)]
        st = s.sb("stats", [P, NU, 6])
        mv = s.sb("mean_var", [P, 2])
        gm = s.sb("group_mean", [P, 1])
        d = s.sb("d", [P, 1])
        e = s.sb("e", [P, 1])
        std = s.sb("std", [P, 1])
        coef = s.sb("coef", [P, 2])
        acc = [s.ps(f"acc{i}") for i in range(2)]
        p_mean = s.ps("mean")
        p_var = s.ps("var")
        p_off = [s.ps(f"off{i}", [P, TR, 32]) for i in range(2)]
        chain = s.sem("vector_chain")
        conv_done = s.sem("conv_done")
        raw_ready = s.sem("raw_ready")
        stats_done = s.sem("stats_done")
        mean_in = s.sem("mean_in")
        mean_ready = s.sem("mean_ready")
        var_in = s.sem("var_in")
        var_ready = s.sem("var_ready")
        std_ready = s.sem("std_ready")
        coef_ready = s.sem("coef_ready")
        tanh_ready = s.sem("tanh_ready")
        sums_ready = s.sem("sums_ready")
        off_ready = s.sem("off_ready")
        block = ctx.enter_context(nc.Block())

        @block.tensor
        def _(pe):
            def conv(u, slot, first):
                if not first:
                    pe.wait_ge(raw_ready, u - 1)
                for t in range(9):
                    dy, dx = divmod(t, 3)
                    ins = pe.matmul(acc[slot][:, :], k.w_off2[:, t, :],
                                    xn[:, bass.ds(u * UR + (PAD - 1 + dy), UR), PAD - 1 + dx:PAD - 1 + dx + W],
                                    start=(t == 0), stop=(t == 8))
                ins.then_inc(conv_done, 1)

            in_pairs(pe, NU, conv)
            pe.wait_ge(mean_in, 1)
            pe.matmul(p_mean[:, 0:1], k.pair_mean, mv[:, 0:1], start=True, stop=True).then_inc(mean_ready, 1)
            pe.wait_ge(var_in, 1)
            pe.matmul(p_var[:, 0:1], k.pair_mean, e[:, :], start=True, stop=True).then_inc(var_ready, 1)

            def cumulate(t, slot, first):
                pe.wait_ge(tanh_ready, t + 1)
                if not first:
                    pe.wait_ge(off_ready, t - 1)
                for i in range(TR):
                    ins = pe.matmul(p_off[slot][:, i, :], tanh[slot][:, i, :], k.cumulate, start=True, stop=True)
                ins.then_inc(sums_ready, 1)

            in_pairs(pe, NT, cumulate)

        @block.scalar
        def _(act):
            def evacuate(u, slot, first):
                act.wait_ge(conv_done, u + 1)
                act.activation(raw[:, bass.ds(u * UR, UR), :].rearrange("p h w -> p (h w)"), acc[slot][:, :], ACT.Identity,
                               bias=k.vec('L2_conv_b_off')).then_inc(raw_ready, 1)

            in_pairs(act, NU, evacuate)
            act.wait_ge(var_ready, 1)
            act.activation(std[:, :], p_var[:, 0:1], ACT.Sqrt, bias=k.eps[:, :]).then_inc(std_ready, 1)
            act.wait_ge(coef_ready, 1)

            def squash(t, slot, first):
                if not first:
                    act.wait_ge(sums_ready, t - 1)
                act.activation(tanh[slot][:, :, :], raw[:, bass.ds(t * TR, TR), :], ACT.Tanh, bias=coef[:, 1:2],
                               scale=coef[:, 0:1]).then_inc(tanh_ready, 1)

            in_pairs(act, NT, squash)

        @block.vector
        def _(dve):
            n = [0]

            def link(ins):
                n[0] += 1
                ins.then_inc(chain, 1)
                dve.wait_ge(chain, n[0])

            def stats(u, slot, first):
                dve.wait_ge(raw_ready, u + 1)
                dve.bn_stats(st[:, bass.ds(u, 1), :].rearrange("p u s -> p (u s)"),
                             raw[:, bass.ds(u * UR, UR), :].rearrange("p h w -> p (h w)")).then_inc(stats_done, 1)

            in_pairs(dve, NU, stats)
            dve.wait_ge(stats_done, NU)
            dve.bn_aggr(mv[:, :], st[:, :, :].rearrange("p u s -> p (u s)")).then_inc(mean_in, 1)
            dve.wait_ge(mean_in, 1)
            dve.wait_ge(mean_ready, 1)
            link(dve.tensor_copy(gm[:, :], p_mean[:, 0:1]))
            link(dve.tensor_tensor(d[:, :], mv[:, 0:1], gm[:, :], ALU.subtract))
            link(dve.tensor_tensor(d[:, :], d[:, :], d[:, :], ALU.mult))
            dve.tensor_tensor(e[:, :], d[:, :], mv[:, 1:2], ALU.add).then_inc(var_in, 1)
            dve.wait_ge(std_ready, 1)
            link(dve.reciprocal(std[:, :], std[:, :]))
            link(dve.tensor_tensor(coef[:, 0:1], std[:, :], k.vec('L2_conv_gn_off_g'), ALU.mult))
            link(dve.tensor_tensor(d[:, :], gm[:, :], coef[:, 0:1], ALU.mult))
            dve.tensor_tensor(coef[:, 1:2], k.vec('L2_conv_gn_off_b'), d[:, :], ALU.subtract).then_inc(coef_ready, 1)

            def keep(t, slot, first):
                dve.wait_ge(sums_ready, t + 1)
                dve.tensor_copy(off[:, bass.ds(t * TR, TR), :], p_off[slot][:, :, :]).then_inc(off_ready, 1)

            in_pairs(dve, NT, keep)


def snake(nc, k, xn, off, pre, g):
    UR = 8
    NU = H // UR
    COLS = UR * W
    REACH = [abs(t - 4) for t in SNAKE_TAPS]
    NS = len(SNAKE_TAPS)
    DR = UR + 7
    GROUPS = [[(r, min(4, UR - 1 + 2 * n - r)) for r in range(0, UR - 1 + 2 * n, 4)] for n in REACH]
    ON_POOL = [2, 2, 2, 2, 2, 1, 1, 0]
    ON_DVE = [2 * n - m for n, m in zip(REACH, ON_POOL)]
    NV, NP_, NG_ = sum(ON_DVE), sum(ON_POOL), sum(len(x) for x in GROUPS)
    RV, RP = 4, 2
    assert NV % RV == 0 and NP_ % RP == 0 and NG_ % 2 == 0
    first_v = [sum(ON_DVE[:q]) for q in range(NS)]
    first_p = [sum(ON_POOL[:q]) for q in range(NS)]
    first_g = [sum(len(x) for x in GROUPS[:q]) for q in range(NS)]

    def terms(q):
        n = REACH[q]
        order = [(sg, j) for j in range(n) for sg in (0, 1)]
        return order[:ON_POOL[q]], order[ON_POOL[q]:]

    BASE_J = [0, 8, 14, 18]
    with ExitStack() as ctx:
        s = Space(nc, ctx, f"snake{g}")
        diff = s.sb("diff", [P, DR, HP])
        dk = [s.sb(f"dk{i}", [P, DR, P]) for i in range(2)]
        clip = [s.sb(f"clip{i}", [P, 2, 20, UR, GI]) for i in range(2)]
        prod_v = [s.sb(f"prod_v{i}", [P, UR, P]) for i in range(RV)]
        prod_p = [s.sb(f"prod_p{i}", [P, UR, P]) for i in range(RP)]
        tk = [s.sb(f"tk{i}", [P, COLS]) for i in range(2)]
        ob = s.sb("ob", [P, COLS])
        st = s.sb("stats", [P, 2 * NU, 6])
        mv = s.sb("mean_var", [P, 2])
        gm = s.sb("group_mean", [P, 1])
        d = s.sb("d", [P, 1])
        e = s.sb("e", [P, 1])
        std = s.sb("std", [P, 1])
        p_d = [s.ps(f"d{i}") for i in range(2)]
        p_t = [s.ps(f"t{i}", [P, COLS]) for i in range(2)]
        p_o = s.ps("o", [P, COLS])
        chain = s.sem("vector_chain")
        padded = s.sem("padded")
        diff_ready = s.sem("diff_ready")
        clip_ready = s.sem("clip_ready")
        turned = s.sem("turned")
        dk_copied = s.sem("dk_copied")
        v_ready = s.sem("v_ready")
        v_used = s.sem("v_used")
        p_ready = s.sem("p_ready")
        p_used = s.sem("p_used")
        t_ready = s.sem("t_ready")
        t_copied = s.sem("t_copied")
        w_done = s.sem("w_done")
        out_ready = s.sem("out_ready")
        out_copied = s.sem("out_copied")
        ob_stats = s.sem("ob_stats")
        stored = s.sem("stored")
        mean_in = s.sem("mean_in")
        mean_ready = s.sem("mean_ready")
        var_in = s.sem("var_in")
        var_ready = s.sem("var_ready")
        std_ready = s.sem("std_ready")
        block = ctx.enter_context(nc.Block())

        def units(eng, body):
            body(0, True, False)
            with eng.Fori(1, NU - 1) as u:
                body(u, False, False)
            body(NU - 1, False, True)

        @block.sync
        def _(sp):
            def store(u, first, last):
                sp.wait_ge(out_copied, u + 1)
                sp.dma_start(pre[:, bass.ds(u * UR, UR), :].rearrange("p h w -> p (h w)"), ob[:, :]).then_inc(stored, 16)

            units(sp, store)
            sp.wait_ge(stored, 16 * NU)

        @block.tensor
        def _(pe):
            def turn_d(u, q, first):
                tap, n = SNAKE_TAPS[q], REACH[q]
                if q == 0:
                    pe.wait_ge(diff_ready, u + 1)
                for i, (r0, nr) in enumerate(GROUPS[q]):
                    G = first_g[q] + i
                    if not (first and G < 2):
                        pe.wait_ge(dk_copied, u * NG_ + (G - 1))
                    for r in range(nr):
                        ins = pe.transpose(p_d[G % 2][:, r * P:(r + 1) * P], diff[:, 4 - n + r0 + r, tap:tap + W], k.ident)
                    ins.then_inc(turned, 1)

            def add_products(u, q, first):
                if not (first and q < 2):
                    pe.wait_ge(t_copied, u * NS + (q - 1))
                pool_terms, dve_terms = terms(q)
                total = 2 * REACH[q]
                at = 0
                for engine, n_terms, n0, ring, ready, used in (("v", len(dve_terms), first_v[q], prod_v, v_ready, v_used),
                                                               ("p", len(pool_terms), first_p[q], prod_p, p_ready, p_used)):
                    per = NV if engine == "v" else NP_
                    for m in range(n_terms):
                        pe.wait_ge(ready, u * per + (n0 + m + 1))
                        for r in range(UR):
                            ins = pe.matmul(p_t[q % 2][:, r * W:(r + 1) * W], ring[(n0 + m) % len(ring)][:, r, :], k.ident,
                                            start=(at == 0 and r % 4 == 0), stop=(at == total - 1 and r % 4 == 3), is_transpose=True,
                                            skip_group_check=False)
                        ins.then_inc(used, 1)
                        at += 1
                return ins

            def middle_taps(u, first):
                if not first:
                    pe.wait_ge(out_copied, u)
                for half in range(2):
                    for t in range(9):
                        pe.matmul(p_o[:, half * BANK:(half + 1) * BANK], k.w_dsc[:, t, :],
                                  xn[:, bass.ds(u * UR + (PAD + 4 * half), 4), t:t + W], start=(t == 0), stop=False)

            def weigh(u, q):
                pe.wait_ge(t_copied, u * NS + (q + 1))
                for half in range(2):
                    ins = pe.matmul(p_o[:, half * BANK:(half + 1) * BANK], k.w_dsc[:, SNAKE_TAPS[q], :],
                                    tk[q % 2][:, half * BANK:(half + 1) * BANK], start=False, stop=(q == NS - 1))
                ins.then_inc(w_done, 1)

            pe.wait_ge(padded, 1)
            turn_d(0, 0, True)

            def unit(u, first, last):
                for q in range(NS):
                    if q < NS - 1:
                        turn_d(u, q + 1, first)
                    elif not last:
                        turn_d(u + 1, 0, False)
                    add_products(u, q, first)
                    if q == 0 and not first:
                        weigh(u - 1, NS - 1)
                    if q == 1:
                        middle_taps(u, first)
                    if q > 0:
                        weigh(u, q - 1)

            units(pe, unit)
            weigh(NU - 1, NS - 1)
            pe.wait_ge(mean_in, 1)
            pe.matmul(p_d[0][:, 0:1], k.quad_mean, mv[:, 0:1], start=True, stop=True).then_inc(mean_ready, 1)
            pe.wait_ge(var_in, 1)
            pe.matmul(p_d[1][:, 0:1], k.quad_mean, e[:, :], start=True, stop=True).then_inc(var_ready, 1)

        @block.scalar
        def _(act):
            def copy_d(u, q, first):
                if not (first and q < 2):
                    if q >= 2:
                        v, p = u * NV + first_v[q - 1], u * NP_ + first_p[q - 1]
                    else:
                        v, p = (u - 1) * NV + (first_v + [NV])[q + NS - 1], (u - 1) * NP_ + (first_p + [NP_])[q + NS - 1]
                    act.wait_ge(v_ready, v)
                    act.wait_ge(p_ready, p)
                for i, (r0, nr) in enumerate(GROUPS[q]):
                    G = first_g[q] + i
                    act.wait_ge(turned, u * NG_ + (G + 1))
                    act.activation(dk[q % 2][:, r0:r0 + nr, :].rearrange("p r c -> p (r c)"), p_d[G % 2][:, 0:nr * P],
                                   ACT.Copy).then_inc(dk_copied, 1)

            def copy_t(u, q, first):
                m = q + 1
                act.wait_ge(v_used, u * NV + (first_v + [NV])[q + 1])
                act.wait_ge(p_used, u * NP_ + (first_p + [NP_])[q + 1])
                if not (first and q < 2):
                    act.wait_ge(w_done, u * NS + (q - 1))
                act.activation(tk[q % 2][:, :], p_t[q % 2][:, :], ACT.Copy).then_inc(t_copied, 1)

            def copy_out(u, first):
                act.wait_ge(w_done, u * NS + NS)
                if not first:
                    act.wait_ge(stored, u * 16)
                    act.wait_ge(ob_stats, u)
                act.activation(ob[:, :], p_o[:, :], ACT.Identity, bias=k.vec('L2_conv_b_dsc')).then_inc(out_copied, 1)

            copy_d(0, 0, True)

            def unit(u, first, last):
                for q in range(NS):
                    if q < NS - 1:
                        copy_d(u, q + 1, first)
                    elif not last:
                        copy_d(u + 1, 0, False)
                    copy_t(u, q, first)
                    if q == 0 and not first:
                        if last:
                            copy_out(u - 1, False)
                        else:
                            copy_out_loop(u)

            def copy_out_loop(u):
                act.wait_ge(w_done, u * NS)
                act.wait_ge(stored, (u - 1) * 16)
                act.wait_ge(ob_stats, u - 1)
                act.activation(ob[:, :], p_o[:, :], ACT.Identity, bias=k.vec('L2_conv_b_dsc')).then_inc(out_copied, 1)

            units(act, unit)
            copy_out(NU - 1, False)
            act.wait_ge(var_ready, 1)
            act.activation(std[:, :], p_d[1][:, 0:1], ACT.Sqrt, bias=k.eps[:, :]).then_inc(std_ready, 1)

        def product(eng, out_ap, slot, q, sg, j, on_vector):
            n = REACH[q]
            r = n + j if sg == 0 else n - 1 - j
            rows = dk[q % 2][:, r:r + UR, :].rearrange("p r (b c) -> p (r b) c", b=GI)
            f = clip[slot][:, sg, BASE_J[j] + q, :, :].rearrange("p r b -> p (r b)").unsqueeze(2).to_broadcast((P, UR * GI, C))
            o = out_ap[:, :, :].rearrange("p r (b c) -> p (r b) c", b=GI)
            if on_vector and j:
                return eng.scalar_tensor_tensor(o, f, float(-j if sg == 0 else j), rows, ALU.add, ALU.mult)
            return eng.tensor_tensor(o, f, rows, ALU.mult)

        @block.gpsimd
        def _(pool):
            def unit(u, slot, first):
                pool.wait_ge(clip_ready, u + 1)
                for q in range(NS):
                    for m, (sg, j) in enumerate(terms(q)[0]):
                        assert j == 0
                        N = first_p[q] + m
                        if m == 0:
                            pool.wait_ge(dk_copied, u * NG_ + first_g[q] + len(GROUPS[q]))
                        if not (first and slot == 0 and N < RP):
                            pool.wait_ge(p_used, u * NP_ + (N - RP + 1))
                        product(pool, prod_p[N % RP], slot, q, sg, j, False).then_inc(p_ready, 1)

            in_pairs(pool, NU, unit)

        @block.vector
        def _(dve):
            n = [0]

            def link(ins):
                n[0] += 1
                ins.then_inc(chain, 1)
                dve.wait_ge(chain, n[0])

            dve.tensor_copy(xn[:, 0:PAD, PAD:PAD + W], xn[:, PAD:PAD + 1, PAD:PAD + W].to_broadcast((P, PAD, W)))
            link(dve.tensor_copy(xn[:, PAD + H:HP, PAD:PAD + W], xn[:, PAD + H - 1:PAD + H, PAD:PAD + W].to_broadcast((P, PAD, W))))
            dve.tensor_copy(xn[:, :, 0:PAD], xn[:, :, PAD:PAD + 1].to_broadcast((P, HP, PAD)))
            dve.tensor_copy(xn[:, :, PAD + W:HP], xn[:, :, PAD + W - 1:PAD + W].to_broadcast((P, HP, PAD))).then_inc(padded, 1)
            dve.wait_ge(padded, 1)

            def differences(u):
                dve.tensor_tensor(diff[:, :, :], xn[:, bass.ds(u * UR + 1, DR), :], xn[:, bass.ds(u * UR, DR), :],
                                  ALU.subtract).then_inc(diff_ready, 1)

            def clips(u, slot):
                for sg in range(2):
                    for j in range(4):
                        w = 2 * (4 - j)
                        lo, hi = (float(j), float(j + 1)) if sg == 0 else (float(-j - 1), float(-j))
                        ins = dve.tensor_scalar(clip[slot][:, sg, BASE_J[j]:BASE_J[j] + w, :, :],
                                                off[:, bass.ds(u * UR, UR), 0:w * GI].rearrange("p r (s b) -> p s r b", b=GI), lo, hi, ALU.max, ALU.min)
                ins.then_inc(clip_ready, 1)

            def stats(u):
                dve.wait_ge(out_copied, u + 1)
                for i in range(2):
                    ins = dve.bn_stats(st[:, bass.ds(2 * u + i, 1), :].rearrange("p u s -> p (u s)"), ob[:, i * BANK:(i + 1) * BANK])
                ins.then_inc(ob_stats, 1)

            differences(0)

            def unit(u, slot, first, last=False):
                if not (first and slot == 0):
                    if not first:
                        dve.wait_ge(p_ready, (u - 1) * NP_)
                clips(u, slot)
                dve.wait_ge(clip_ready, u + 1)
                for q in range(NS):
                    if q == NS - 1 and not last:
                        dve.wait_ge(turned, u * NG_ + NG_)
                        differences(u + 1)
                    if q == 3 and not (first and slot == 0):
                        stats(u - 1)
                    for m, (sg, j) in enumerate(terms(q)[1]):
                        N = first_v[q] + m
                        if m == 0:
                            dve.wait_ge(dk_copied, u * NG_ + first_g[q] + len(GROUPS[q]))
                        if not (first and slot == 0 and N < RV):
                            dve.wait_ge(v_used, u * NV + (N - RV + 1))
                        product(dve, prod_v[N % RV], slot, q, sg, j, True).then_inc(v_ready, 1)

            unit(0, 0, True)
            unit(1, 1, True)
            with dve.Fori(1, NU // 2 - 1) as i:
                unit(i * 2, 0, False)
                unit(i * 2 + 1, 1, False)
            unit(NU - 2, 0, False)
            unit(NU - 1, 1, False, True)
            stats(NU - 1)
            dve.wait_ge(ob_stats, NU)
            dve.bn_aggr(mv[:, :], st[:, :, :].rearrange("p u s -> p (u s)")).then_inc(mean_in, 1)
            dve.wait_ge(mean_in, 1)
            dve.wait_ge(mean_ready, 1)
            link(dve.tensor_copy(gm[:, :], p_d[0][:, 0:1]))
            link(dve.tensor_tensor(d[:, :], mv[:, 0:1], gm[:, :], ALU.subtract))
            link(dve.tensor_tensor(d[:, :], d[:, :], d[:, :], ALU.mult))
            dve.tensor_tensor(e[:, :], d[:, :], mv[:, 1:2], ALU.add).then_inc(var_in, 1)
            dve.wait_ge(std_ready, 1)
            link(dve.reciprocal(std[:, :], std[:, :]))
            link(dve.tensor_tensor(k.snake_gn[:, 0:1], std[:, :], k.vec('L2_conv_gn_g'), ALU.mult))
            link(dve.tensor_tensor(d[:, :], gm[:, :], k.snake_gn[:, 0:1], ALU.mult))
            dve.tensor_tensor(k.snake_gn[:, 1:2], k.vec('L2_conv_gn_b'), d[:, :], ALU.subtract)


def dcn_offsets(nc, k, xn, offs, g):
    UR = 8
    NU = H // UR
    K2 = 9
    with ExitStack() as ctx:
        s = Space(nc, ctx, f"dcnoff{g}")
        cm = [s.sb(f"cm{i}", [P, UR, W]) for i in range(2)]
        sig = [s.sb(f"sig{i}", [P, UR, GI, K2]) for i in range(2)]
        msum = [s.sb(f"msum{i}", [P, UR, GI]) for i in range(2)]
        keep = [s.sb(f"keep{i}", [P, UR, OFFS]) for i in range(2)]
        far = s.sb("far", [P, NU])
        far1 = s.sb("far1", [P, 1])
        far0 = s.sb("far0", [1, 1])
        acc = [s.ps(f"acc{i}", [P, UR * W]) for i in range(2)]
        p_t = [s.ps(f"t{i}", [P, UR, GI, 32]) for i in range(2)]
        conv_done = s.sem("conv_done")
        cm_ready = s.sem("cm_ready")
        turned = s.sem("turned")
        sig_ready = s.sem("sig_ready")
        msum_ready = s.sem("msum_ready")
        keep_ready = s.sem("keep_ready")
        stored = [s.sem(f"stored{i}") for i in range(2)]
        far_ready = s.sem("far_ready")
        far_turned = s.sem("far_turned")
        chain = s.sem("vector_chain")
        block = ctx.enter_context(nc.Block())

        @block.tensor
        def _(pe):
            def turn_back(u, slot, first):
                pe.wait_ge(cm_ready, u + 1)
                if not first:
                    pe.wait_ge(keep_ready, u - 1)
                for r in range(UR):
                    ins = pe.transpose(p_t[slot][:, r, :, :].rearrange("p b o -> p (b o)"), cm[slot][:, r, :], k.ident)
                ins.then_inc(turned, 1)

            def conv(u, slot, first):
                if not first:
                    pe.wait_ge(cm_ready, u - 1)
                for half in range(2):
                    for t in range(9):
                        dy, dx = divmod(t, 3)
                        ins = pe.matmul(acc[slot][:, half * BANK:(half + 1) * BANK], k.w_off3[:, t, :],
                                        xn[:, bass.ds(u * UR + (4 * half + PAD - 1 + dy), 4), PAD - 1 + dx:PAD - 1 + dx + W],
                                        start=(t == 0), stop=(t == 8))
                ins.then_inc(conv_done, 1)

            conv(0, 0, True)
            conv(1, 1, True)
            turn_back(0, 0, True)
            conv(2, 0, False)
            turn_back(1, 1, True)
            conv(3, 1, False)
            with pe.Fori(2, NU // 2) as i:
                turn_back(i * 2 - 2, 0, False)
                conv(i * 2, 0, False)
                turn_back(i * 2 - 1, 1, False)
                conv(i * 2 + 1, 1, False)
            turn_back(NU - 2, 0, False)
            turn_back(NU - 1, 1, False)
            pe.wait_ge(far_ready, 1)
            pe.matmul(acc[0][0:1, 0:P], far1[:, :], k.ident, start=True, stop=True).then_inc(far_turned, 1)

        @block.scalar
        def _(act):
            def bias(u, slot, first):
                act.wait_ge(conv_done, u + 1)
                if not first:
                    act.wait_ge(turned, u - 1)
                act.activation(cm[slot][:, :, :].rearrange("p h w -> p (h w)"), acc[slot][:, :], ACT.Identity, bias=k.bias3).then_inc(cm_ready, 1)

            def sigmoid(u, slot, first):
                act.wait_ge(turned, u + 1)
                if not first:
                    act.wait_ge(msum_ready, u - 1)
                act.activation(sig[slot][:, :, :, :], p_t[slot][:, :, :, 18:27], ACT.Sigmoid).then_inc(sig_ready, 1)

            bias(0, 0, True)
            bias(1, 1, True)
            sigmoid(0, 0, True)
            bias(2, 0, False)
            sigmoid(1, 1, True)
            bias(3, 1, False)
            with act.Fori(2, NU // 2) as i:
                sigmoid(i * 2 - 2, 0, False)
                bias(i * 2, 0, False)
                sigmoid(i * 2 - 1, 1, False)
                bias(i * 2 + 1, 1, False)
            sigmoid(NU - 2, 0, False)
            sigmoid(NU - 1, 1, False)

        @block.vector
        def _(dve):
            def unit(u, slot, first):
                dve.wait_ge(sig_ready, u + 1)
                o = p_t[slot][:, :, :, 0:18]
                dve.tensor_reduce(msum[slot][:, :, :], sig[slot][:, :, :, :], AX.X, ALU.add).then_inc(msum_ready, 1)
                dve.tensor_reduce(far[:, bass.ds(u, 1)], o, AX.XYZ, ALU.max, apply_absolute_value=True)
                if not first:
                    dve.wait_ge(stored[slot], turn(u) * 16)
                dve.tensor_copy(keep[slot][:, :, 0:GI * 18].rearrange("p h (b o) -> p h b o", b=GI), o)
                dve.wait_ge(msum_ready, u + 1)
                dve.tensor_scalar(keep[slot][:, :, GI * 18:OFFS], msum[slot][:, :, :], 1.0 / K2, None, ALU.mult).then_inc(keep_ready, 1)

            in_pairs(dve, NU, unit)
            dve.wait_ge(keep_ready, NU)
            dve.tensor_reduce(far1[:, :], far[:, :], AX.X, ALU.max).then_inc(far_ready, 1)
            dve.wait_ge(far_turned, 1)
            dve.tensor_reduce(far0[:, :], acc[0][0:1, 0:P], AX.X, ALU.max).then_inc(chain, 1)
            dve.wait_ge(chain, 1)
            dve.tensor_scalar(k.dense[:, :], far0[:, :], 1.0, None, ALU.is_le)

        @block.sync
        def _(sp):
            def store(u, slot, first):
                sp.wait_ge(keep_ready, u + 1)
                sp.dma_start(offs[bass.ds(u * UR, UR), :, :].rearrange("h w f -> w h f"), keep[slot][:, :, :]).then_inc(stored[slot], 16)

            in_pairs(sp, NU, store)
            for slot in range(2):
                sp.wait_ge(stored[slot], NU // 2 * 16)


def dcn_gather(nc, k, xn, offs, table, x3, out, g):
    x3_v, out_v = (t.rearrange("(g b) c h w -> g (b c) h w", g=NG)[g] for t in (x3, out))
    table_v = table.rearrange("(b h w) c -> b w h c", b=GI, h=H)
    UR = 4
    NU = H // UR
    with ExitStack() as ctx:
        s = Space(nc, ctx, f"table{g}")
        win = s.sb("win", [P, UR, W])
        tb = s.sb("tb", [P, UR, P])
        p_w = s.ps("w", [P, UR * P])
        win_ready = s.sem("win_ready")
        turned = s.sem("turned")
        tb_ready = s.sem("tb_ready")
        stored = s.sem("stored")
        block = ctx.enter_context(nc.Block())

        def rows(eng, n, body):
            body(0, True)
            with eng.Fori(1, n) as u:
                body(u, False)

        @block.scalar
        def _(act):
            def stage(u, first):
                if not first:
                    act.wait_ge(turned, u)
                act.activation(win[:, :, :], xn[:, bass.ds(u * UR + PAD, UR), PAD:PAD + W], ACT.Copy).then_inc(win_ready, 1)

            rows(act, NU, stage)

        @block.tensor
        def _(pe):
            def turn_rows(u, first):
                pe.wait_ge(win_ready, u + 1)
                if not first:
                    pe.wait_ge(tb_ready, u)
                for r in range(UR):
                    ins = pe.transpose(p_w[:, r * P:(r + 1) * P], win[:, r, :], k.ident)
                ins.then_inc(turned, 1)

            rows(pe, NU, turn_rows)

        @block.vector
        def _(dve):
            def copy(u, first):
                dve.wait_ge(turned, u + 1)
                if not first:
                    dve.wait_ge(stored, u * (16 * GI))
                dve.tensor_copy(tb[:, :, :].rearrange("p r c -> p (r c)"), p_w[:, :]).then_inc(tb_ready, 1)

            rows(dve, NU, copy)

        @block.sync
        def _(sp):
            def store(u, first):
                sp.wait_ge(tb_ready, u + 1)
                for b in range(GI):
                    sp.dma_start(table_v[b, :, bass.ds(u * UR, UR), :], tb[:, :, b * C:(b + 1) * C]).then_inc(stored, 16)

            rows(sp, NU, store)
            sp.wait_ge(stored, 16 * GI * NU)
    for part in range(2):
        gather_rows(nc, k, offs, table, x3_v, out_v, f"{g}_{part}", part * (H // 2), H // 2)


def gather_rows(nc, k, offs, table, x3_v, out_v, tag, h0, n_rows):
    K2 = 9
    with ExitStack() as ctx:
        s = Space(nc, ctx, f"gather{tag}")
        off = s.sb("off", [P, OFFS])
        xr = s.sb("x3", [P, W])
        ob = s.sb("ob", [P, W])
        row = s.sb("row", [P, 1])
        col = s.sb("col", [P, 1])
        image = s.sb("image", [P, GI, K2])
        pos = s.sb("pos", [P, GI, 18])
        inside = s.sb("inside", [P, GI, 18])
        whole = s.sb("whole", [P, GI, 18], I32)
        base = s.sb("base", [P, GI, 18])
        gt = s.sb("gt", [P, GI, 18])
        dist = s.sb("dist", [P, 2, GI, 18])
        dabs = s.sb("dabs", [P, 2, GI, 18])
        hat = s.sb("hat", [P, 2, GI, 18])
        weight = s.sb("weight", [P, 4, GI, K2])
        flat = s.sb("flat", [P, GI, K2])
        index = s.sb("index", [P, 4, GI, K2], U32)
        near = [s.sb(f"near{i}", [P, 4, GI, C]) for i in range(3)]
        prod = s.sb("prod", [P, 4, GI, C])
        half = s.sb("half", [P, 2, P])
        samp = [s.sb(f"samp{i}", [P, P]) for i in range(2)]
        tk = [s.sb(f"tk{i}", [P, P]) for i in range(2)]
        p_t = [s.ps(f"t{i}") for i in range(2)]
        p_o = s.ps("o")
        iota_done = s.sem("iota_done")
        loaded = s.sem("loaded")
        x3_loaded = s.sem("x3_loaded")
        chain = s.sem("vector_chain")
        index_ready = s.sem("index_ready")
        gathered = [s.sem(f"gathered{i}") for i in range(3)]
        near_used = s.sem("near_used")
        samp_ready = s.sem("samp_ready")
        turned = s.sem("turned")
        tk_ready = s.sem("tk_ready")
        w_done = s.sem("w_done")
        ob_ready = s.sem("ob_ready")
        stored = s.sem("stored")
        index_step = s.sem("index_step")
        gather_go = s.sem("gather_go")
        half_ready = s.sem("half_ready")
        block = ctx.enter_context(nc.Block())

        def rows(eng, body):
            body(0, True)
            with eng.Fori(1, n_rows) as h:
                body(h, False)

        @block.sync
        def _(sp):
            def load(h, first):
                if not first:
                    sp.wait_ge(index_ready, h)
                sp.dma_start(off[:, :], offs[bass.ds(h + h0, 1), :, :].rearrange("h w f -> (h w) f")).then_inc(loaded, 16)
                if not first:
                    sp.wait_ge(ob_ready, h)
                sp.dma_start(xr[:, :], x3_v[:, bass.ds(h + h0, 1), :].rearrange("p h w -> p (h w)")).then_inc(x3_loaded, 16)
                sp.wait_ge(ob_ready, h + 1)
                sp.dma_start(out_v[:, bass.ds(h + h0, 1), :].rearrange("p h w -> p (h w)"), ob[:, :]).then_inc(stored, 16)

            rows(sp, load)
            sp.wait_ge(stored, 16 * n_rows)

        @block.gpsimd
        def _(pool):
            pool.iota(col[:, :], pattern=[[0, 1]], base=0, channel_multiplier=1, allow_small_or_imprecise_dtypes=True).then_inc(iota_done, 1)
            pool.iota(image[:, :, :], pattern=[[PX, GI], [0, K2]], base=0, channel_multiplier=0,
                      allow_small_or_imprecise_dtypes=True).then_inc(iota_done, 1)

            def gather(h, first):
                pool.wait_ge(index_ready, h + 1)
                for t in range(K2):
                    if not (first and t < 3):
                        pool.wait_ge(near_used, h * K2 + (t - 2))
                    pool.sem_inc(gather_go, 1)
                    for corner in range(4):
                        for b in range(GI):
                            pool.indirect_dma_start(out=near[t % 3][:, corner, b, :], out_offset=None, in_=table,
                                                    in_offset=bass.IndirectOffsetOnAxis(ap=index[:, corner, b, t:t + 1], axis=0)
                                                    ).then_inc(gathered[t % 3], 16)

            rows(pool, gather)

        @block.vector
        def _(dve):
            dve.wait_ge(iota_done, 2)
            dve.memset(row[:, :], float(h0)).then_inc(chain, 1)
            dve.wait_ge(chain, 1)
            STEPS = 15

            def positions(h, first):
                n = [0]

                def link(ins):
                    n[0] += 1
                    ins.then_inc(chain, 1)
                    dve.wait_ge(chain, h * STEPS + (n[0] + 1))

                dve.wait_ge(loaded, h * 16 + 16)
                o = off[:, 0:GI * 18].rearrange("p (b o) -> p b o", b=GI)
                dve.tensor_scalar(pos[:, :, 0:K2], o[:, :, 0:K2], row[:, :], None, ALU.add)
                link(dve.tensor_scalar(pos[:, :, K2:18], o[:, :, K2:18], col[:, :], None, ALU.add))
                link(dve.tensor_scalar(row[:, :], row[:, :], 1.0, None, ALU.add))
                link(dve.tensor_scalar(inside[:, :, :], pos[:, :, :], 0.0, float(H - 1), ALU.max, ALU.min))
                link(dve.tensor_copy(whole[:, :, :], inside[:, :, :]))
                link(dve.tensor_copy(base[:, :, :], whole[:, :, :]))
                link(dve.tensor_tensor(gt[:, :, :], base[:, :, :], inside[:, :, :], ALU.is_gt))
                link(dve.tensor_tensor(base[:, :, :], base[:, :, :], gt[:, :, :], ALU.subtract))
                link(dve.tensor_scalar(base[:, :, :], base[:, :, :], float(H - 2), None, ALU.min))
                link(dve.tensor_tensor(dist[:, 0, :, :], pos[:, :, :], base[:, :, :], ALU.subtract))
                link(dve.tensor_scalar(dist[:, 1, :, :], dist[:, 0, :, :], -1.0, None, ALU.add))
                link(dve.tensor_scalar(dabs[:, :, :, :], dist[:, :, :, :], -1.0, None, ALU.mult))
                link(dve.tensor_tensor(dabs[:, :, :, :], dabs[:, :, :, :], dist[:, :, :, :], ALU.max))
                link(dve.tensor_scalar(hat[:, :, :, :], dabs[:, :, :, :], -1.0, 1.0, ALU.mult, ALU.add))
                link(dve.tensor_scalar(hat[:, :, :, :], hat[:, :, :, :], 0.0, None, ALU.max))
                dve.tensor_scalar(flat[:, :, :], base[:, :, 0:K2], float(W), None, ALU.mult)
                link(dve.tensor_tensor(hat[:, :, :, 0:K2], hat[:, :, :, 0:K2],
                                       off[:, GI * 18:OFFS].unsqueeze(1).unsqueeze(3).to_broadcast((P, 2, GI, K2)), ALU.mult))
                assert n[0] == STEPS
                for corner in range(4):
                    dy, dx = divmod(corner, 2)
                    dve.tensor_tensor(weight[:, corner, :, :], hat[:, dy, :, 0:K2], hat[:, dx, :, K2:18], ALU.mult)

            def indices(h, first):
                m = [0]

                def link(ins):
                    m[0] += 1
                    ins.then_inc(index_step, 1)
                    dve.wait_ge(index_step, h * 2 + m[0])

                link(dve.tensor_tensor(flat[:, :, :], flat[:, :, :], base[:, :, K2:18], ALU.add))
                link(dve.tensor_tensor(flat[:, :, :], flat[:, :, :], image[:, :, :], ALU.add))
                for corner in range(4):
                    dy, dx = divmod(corner, 2)
                    ins = dve.tensor_scalar(index[:, corner, :, :], flat[:, :, :], float(dy * W + dx), None, ALU.add)
                ins.then_inc(index_ready, 1)

            def row_of(h, first):
                if not first:
                    dve.wait_ge(near_used, h * K2)
                positions(h, first)
                indices(h, first)
                for t in range(K2):
                    dve.wait_ge(gathered[t % 3], h * (3 * 256) + (t // 3 + 1) * 256)
                    for corner in range(4):
                        ins = dve.tensor_tensor(prod[:, corner, :, :], near[t % 3][:, corner, :, :],
                                                weight[:, corner, :, t:t + 1].to_broadcast((P, GI, C)), ALU.mult)
                    ins.then_inc(near_used, 1)
                    dve.wait_ge(near_used, h * K2 + (t + 1))
                    dve.tensor_tensor(half[:, :, :].rearrange("p s (b c) -> p s b c", b=GI), prod[:, 0:2, :, :], prod[:, 2:4, :, :],
                                      ALU.add).then_inc(half_ready, 1)
                    dve.wait_ge(half_ready, h * K2 + (t + 1))
                    if t == 0 and not first:
                        dve.wait_ge(turned, h * K2)
                    elif t >= 2 or not first:
                        dve.wait_ge(turned, h * K2 + (t - 1))
                    dve.tensor_tensor(samp[t % 2][:, :], half[:, 0, :], half[:, 1, :], ALU.add).then_inc(samp_ready, 1)
                dve.wait_ge(w_done, h * K2 + K2)
                dve.wait_ge(x3_loaded, h * 16 + 16)
                if not first:
                    dve.wait_ge(stored, h * 16)
                dve.scalar_tensor_tensor(ob[:, :], p_o[:, 0:W], k.vec('L3_conv_bias'), xr[:, :], ALU.add, ALU.add).then_inc(ob_ready, 1)

            rows(dve, row_of)

        @block.tensor
        def _(pe):
            def row_of(h, first):
                for t in range(K2):
                    pe.wait_ge(samp_ready, h * K2 + (t + 1))
                    if t == 0 and not first:
                        pe.wait_ge(tk_ready, h * K2)
                    elif t >= 2 or not first:
                        pe.wait_ge(tk_ready, h * K2 + (t - 1))
                    pe.transpose(p_t[t % 2][:, 0:P], samp[t % 2][:, :], k.ident).then_inc(turned, 1)
                    pe.wait_ge(tk_ready, h * K2 + (t + 1))
                    if t == 0 and not first:
                        pe.wait_ge(ob_ready, h)
                    pe.matmul(p_o[:, 0:W], k.w_dcn[:, t, :], tk[t % 2][:, :], start=(t == 0), stop=(t == K2 - 1)).then_inc(w_done, 1)

            rows(pe, row_of)

        @block.scalar
        def _(act):
            def row_of(h, first):
                for t in range(K2):
                    act.wait_ge(turned, h * K2 + (t + 1))
                    if t == 0 and not first:
                        act.wait_ge(w_done, h * K2)
                    elif t >= 2 or not first:
                        act.wait_ge(w_done, h * K2 + (t - 1))
                    act.activation(tk[t % 2][:, :], p_t[t % 2][:, 0:P], ACT.Copy).then_inc(tk_ready, 1)

            rows(act, row_of)


def dcn_dense(nc, k, xn, offs, x3, out, g):
    x3_v, out_v = (t.rearrange("(g b) c h w -> g (b c) h w", g=NG)[g] for t in (x3, out))
    UR = 8
    NU = H // UR
    COLS = UR * W
    K2 = 9
    HB = UR * GI
    WR = UR + 2
    GROUPS = [(i, min(4, 3 * WR - i)) for i in range(0, 3 * WR, 4)]
    NG_ = len(GROUPS)
    ON_POOL = [(0, 1), (2,)]
    ON_DVE = [(3, 4), (5,), (6,), (7,), (8,)]
    MV, MP = len(ON_DVE), len(ON_POOL)
    NV, NP_ = MV * K2, MP * K2
    RV, RP = 3, 2
    PAIRS_V, PAIRS_P = sum(len(x) == 2 for x in ON_DVE), sum(len(x) == 2 for x in ON_POOL)
    assert NG_ % 2 == 0 and NV % RV == 0 and NP_ % RP == 0
    with ExitStack() as ctx:
        s = Space(nc, ctx, f"dense{g}")
        win = s.sb("win", [P, WR, W + 2])
        xw = [s.sb(f"xw{i}", [P, 3 * WR, P]) for i in range(2)]
        off = [s.sb(f"off{i}", [P, UR, OFFS]) for i in range(2)]
        hats = s.sb("hats", [P, 3, 18, HB])
        modt = s.sb("modt", [P, HB])
        weight = s.sb("weight", [P, K2, K2, HB])
        prod_v = [s.sb(f"prod_v{i}", [P, UR, P]) for i in range(RV)]
        prod_p = [s.sb(f"prod_p{i}", [P, UR, P]) for i in range(RP)]
        more_v = s.sb("more_v", [P, UR, P])
        more_p = s.sb("more_p", [P, UR, P])
        tk = [s.sb(f"tk{i}", [P, COLS]) for i in range(2)]
        xr = s.sb("x3", [P, COLS])
        p_w = [s.ps(f"w{i}") for i in range(2)]
        p_t = [s.ps(f"t{i}", [P, COLS]) for i in range(2)]
        p_o = s.ps("o", [P, COLS])
        off_in = [s.sem(f"off_in{i}") for i in range(2)]
        x3_in = s.sem("x3_in")
        win_ready = s.sem("win_ready")
        turned = s.sem("turned")
        xw_copied = s.sem("xw_copied")
        chain = s.sem("vector_chain")
        weights_ready = s.sem("weights_ready")
        v_pair = s.sem("v_pair")
        p_pair = s.sem("p_pair")
        v_ready = s.sem("v_ready")
        v_used = s.sem("v_used")
        p_ready = s.sem("p_ready")
        p_used = s.sem("p_used")
        t_copied = s.sem("t_copied")
        w_done = s.sem("w_done")
        out_done = s.sem("out_done")
        stored = s.sem("stored")
        block = ctx.enter_context(nc.Block())
        STEPS = 4

        @block.sync
        def _(sp):
            def unit(u, slot, first, last):
                if not first:
                    sp.wait_ge(weights_ready, u - 1)
                sp.dma_start(off[slot][:, :, :], offs[bass.ds(u * UR, UR), :, :].rearrange("h w f -> w h f")).then_inc(off_in[slot], 16)
                if not (first and slot == 0):
                    finish(u - 1)
                sp.dma_start(xr[:, :], x3_v[:, bass.ds(u * UR, UR), :].rearrange("p h w -> p (h w)")).then_inc(x3_in, 16)

            def finish(u):
                sp.wait_ge(out_done, u + 1)
                sp.dma_start(out_v[:, bass.ds(u * UR, UR), :].rearrange("p h w -> p (h w)"), xr[:, :]).then_inc(stored, 16)
                sp.wait_ge(stored, u * 16 + 16)

            in_pairs_last(sp, NU, unit)
            finish(NU - 1)

        @block.scalar
        def _(act):
            def stage(u):
                act.activation(win[:, :, :], xn[:, bass.ds(u * UR + (PAD - 1), WR), PAD - 1:PAD + W + 1], ACT.Copy).then_inc(win_ready, 1)

            def copy_rows(u, slot, i):
                act.wait_ge(turned, u * NG_ + (i + 1))
                r0, nr = GROUPS[i]
                act.activation(xw[slot][:, r0:r0 + nr, :].rearrange("p r c -> p (r c)"), p_w[i % 2][:, 0:nr * P], ACT.Copy).then_inc(xw_copied, 1)

            stage(0)
            for i in range(NG_):
                copy_rows(0, 0, i)

            def unit(u, slot, first, last):
                if not last:
                    act.wait_ge(turned, u * NG_ + NG_)
                    stage(u + 1)
                    if not (first and slot == 0):
                        act.wait_ge(v_ready, u * NV)
                        act.wait_ge(p_ready, u * NP_)
                for t in range(K2):
                    if t < NG_ and not last:
                        copy_rows(u + 1, 1 - slot, t)
                    act.wait_ge(v_used, u * NV + (t + 1) * MV)
                    act.wait_ge(p_used, u * NP_ + (t + 1) * MP)
                    if not (first and slot == 0 and t < 2):
                        act.wait_ge(w_done, u * K2 + (t - 1))
                    ts = (slot + t) % 2
                    act.activation(tk[ts][:, :], p_t[ts][:, :], ACT.Copy).then_inc(t_copied, 1)

            in_pairs_last(act, NU, unit)

        @block.tensor
        def _(pe):
            def turn_rows(u, i, first):
                r0, nr = GROUPS[i]
                if i == 0:
                    pe.wait_ge(win_ready, u + 1)
                if not (first and i < 2):
                    pe.wait_ge(xw_copied, u * NG_ + (i - 1))
                for r in range(nr):
                    dx, row = divmod(r0 + r, WR)
                    ins = pe.transpose(p_w[i % 2][:, r * P:(r + 1) * P], win[:, row, dx:dx + W], k.ident)
                ins.then_inc(turned, 1)

            def weigh(u, t, ts, first):
                pe.wait_ge(t_copied, u * K2 + (t + 1))
                if t == 0 and not first:
                    pe.wait_ge(out_done, u)
                for half in range(2):
                    ins = pe.matmul(p_o[:, half * BANK:(half + 1) * BANK], k.w_dcn[:, t, :],
                                    tk[ts][:, half * BANK:(half + 1) * BANK], start=(t == 0), stop=(t == K2 - 1))
                ins.then_inc(w_done, 1)

            for i in range(NG_):
                turn_rows(0, i, True)

            def unit(u, slot, first, last):
                for t in range(K2):
                    if t < NG_ and not last:
                        turn_rows(u + 1, t, False)
                    ts = (slot + t) % 2
                    if not (first and slot == 0 and t < 2):
                        pe.wait_ge(t_copied, u * K2 + (t - 1))
                    at, total = 0, MV + MP
                    for m_all, n0, ring, ready, used in ((MV, t * MV, prod_v, v_ready, v_used), (MP, t * MP, prod_p, p_ready, p_used)):
                        for m in range(m_all):
                            pe.wait_ge(ready, u * (m_all * K2) + (n0 + m + 1))
                            for r in range(UR):
                                ins = pe.matmul(p_t[ts][:, r * W:(r + 1) * W], ring[(n0 + m) % len(ring)][:, r, :], k.ident,
                                                start=(at == 0 and r % 4 == 0), stop=(at == total - 1 and r % 4 == 3), is_transpose=True)
                            ins.then_inc(used, 1)
                            at += 1
                    if t == 0:
                        if not (first and slot == 0):
                            weigh(u - 1, K2 - 1, 1 - ts, False)
                    else:
                        weigh(u, t - 1, 1 - ts, first and slot == 0)

            in_pairs_last(pe, NU, unit)
            weigh(NU - 1, K2 - 1, (1 + K2 - 1) % 2, False)

        def multiply(eng, u, slot, t, groups, n0, per, ring, more, ready, pair, pairs, used, fresh):
            p0 = 0
            for m, terms in enumerate(groups):
                N = n0 + m
                if not (fresh and N < len(ring)):
                    eng.wait_ge(used, u * per + (N - len(ring) + 1))
                for i, d in enumerate(terms):
                    dy, dx = divmod(d, 3)
                    rows = xw[slot][:, dx * WR + dy:dx * WR + dy + UR, :].rearrange("p r (b c) -> p (r b) c", b=GI)
                    f = weight[:, t, d, :].unsqueeze(2).to_broadcast((P, HB, C))
                    o = (ring[N % len(ring)] if i == 0 else more)[:, :, :]
                    ins = eng.tensor_tensor(o.rearrange("p r (b c) -> p (r b) c", b=GI), rows, f, ALU.mult)
                if len(terms) == 2:
                    p0 += 1
                    ins.then_inc(pair, 1)
                    eng.wait_ge(pair, u * (pairs * K2) + (t * pairs + p0))
                    o = ring[N % len(ring)][:, :, :]
                    ins = eng.tensor_tensor(o, o, more[:, :, :], ALU.add)
                ins.then_inc(ready, 1)

        @block.gpsimd
        def _(pool):
            def unit(u, slot, first, last):
                pool.wait_ge(weights_ready, u + 1)
                pool.wait_ge(xw_copied, u * NG_ + NG_)
                for t in range(K2):
                    multiply(pool, u, slot, t, ON_POOL, t * MP, NP_, prod_p, more_p, p_ready, p_pair, PAIRS_P, p_used, first and slot == 0)

            in_pairs_last(pool, NU, unit)

        @block.vector
        def _(dve):
            def make_hats(u, slot):
                n = [0]

                def link(ins):
                    n[0] += 1
                    ins.then_inc(chain, 1)
                    dve.wait_ge(chain, u * STEPS + n[0])

                dve.wait_ge(off_in[slot], turn(u) * 16 + 16)
                o = off[slot][:, :, 0:GI * 18].rearrange("p h (b o) -> p o h b", b=GI)
                h = [hats[:, i, :, :].rearrange("p o (h b) -> p o h b", b=GI) for i in range(3)]
                dve.tensor_copy(modt[:, :].rearrange("p (h b) -> p h b", b=GI), off[slot][:, :, GI * 18:OFFS])
                for r in range(2):
                    q = slice(9 * r, 9 * r + 9)
                    dve.tensor_scalar(h[2][:, q], o[:, q], 0.0, None, ALU.max)
                    ins = dve.tensor_scalar(h[0][:, q], o[:, q], -1.0, 0.0, ALU.mult, ALU.max)
                link(ins)
                link(dve.tensor_tensor(hats[:, 1, :, :], hats[:, 0, :, :], hats[:, 2, :, :], ALU.add))
                link(dve.tensor_scalar(hats[:, 1, :, :], hats[:, 1, :, :], -1.0, 1.0, ALU.mult, ALU.add))
                for i in range(3):
                    ins = dve.tensor_tensor(hats[:, i, 0:9, :], hats[:, i, 0:9, :], modt[:, :].unsqueeze(1).to_broadcast((P, K2, HB)), ALU.mult)
                link(ins)

            def make_weights_(u, slot, fresh):
                if not fresh:
                    dve.wait_ge(p_ready, u * NP_)
                    dve.wait_ge(v_ready, u * NV)
                for dy in range(3):
                    for dx in range(3):
                        ins = dve.tensor_tensor(weight[:, :, 3 * dy + dx, :], hats[:, dy, 0:9, :], hats[:, dx, 9:18, :], ALU.mult)
                ins.then_inc(weights_ready, 1)

            def finish(u):
                dve.wait_ge(w_done, u * K2 + K2)
                dve.wait_ge(x3_in, u * 16 + 16)
                dve.scalar_tensor_tensor(xr[:, :], p_o[:, :], k.vec('L3_conv_bias'), xr[:, :], ALU.add, ALU.add).then_inc(out_done, 1)

            make_hats(0, 0)

            def unit(u, slot, first, last):
                fresh = first and slot == 0
                make_weights_(u, slot, fresh)
                dve.wait_ge(weights_ready, u + 1)
                dve.wait_ge(xw_copied, u * NG_ + NG_)
                for t in range(K2):
                    if t == 1 and not fresh:
                        finish(u - 1)
                    if t == 4 and not last:
                        make_hats(u + 1, 1 - slot)
                    multiply(dve, u, slot, t, ON_DVE, t * MV, NV, prod_v, more_v, v_ready, v_pair, PAIRS_V, v_used, fresh)

            in_pairs_last(dve, NU, unit)
            finish(NU - 1)


def build(nc, a, out):
    x1 = nc.dram_tensor("x1", (B, C, H, W), F32).ap()
    x2 = nc.dram_tensor("x2", (B, C, H, W), F32).ap()
    x3 = nc.dram_tensor("x3", (B, C, H, W), F32).ap()
    pre = [nc.dram_tensor(f"pre{g}", (P, H, W), F32).ap() for g in range(NG)]
    offs = [nc.dram_tensor(f"offs{g}", (H, W, OFFS), F32).ap() for g in range(NG)]
    table = nc.dram_tensor("table", (GI * PX, C), F32).ap()
    with ExitStack() as ctx:
        k = Kept(nc, ctx)
        make_weights(nc, a, k)
        blur(nc, a["x"], a["L0_conv_sigma"], x1)
        for g in range(NG):
            gate_conv(nc, k, x1, g)
        gate_scale(nc, k)
        xn = ctx.enter_context(nc.sbuf_tensor("xn", [P, HP, HP], F32))
        for g in range(NG):
            residual(nc, k, x1, None, ACT.Silu, k.gate[:, g, 0:1], k.gate[:, g, 1:2], x2, xn, g)
            with nc.sbuf_tensor(f"snake_off{g}", [P, H, 32], F32) as off:
                snake_offsets(nc, k, xn, off, g)
                snake(nc, k, xn, off, pre[g], g)
            residual(nc, k, x2, pre[g], ACT.Relu, k.snake_gn[:, 0:1], k.snake_gn[:, 1:2], x3, xn, g)
            dcn_offsets(nc, k, xn, offs[g], g)
            dense = nc.values_load(k.dense[:, :], min_val=0, max_val=1)
            with nc.If(dense > 0):
                dcn_dense(nc, k, xn, offs[g], x3, out, g)
            with nc.Else():
                dcn_gather(nc, k, xn, offs[g], table, x3, out, g)


_INS = ['x', 'L0_conv_sigma', 'L1_conv_proj_weight', 'L1_conv_proj_bias', 'L1_conv_bn_gamma', 'L1_conv_bn_beta',
        'L1_conv_scale_w', 'L1_conv_scale_b', 'L2_conv_w_off', 'L2_conv_b_off', 'L2_conv_gn_off_g', 'L2_conv_gn_off_b',
        'L2_conv_w_dsc', 'L2_conv_b_dsc', 'L2_conv_gn_g', 'L2_conv_gn_b', 'L3_conv_weight', 'L3_conv_bias',
        'L3_conv_offset_w', 'L3_conv_offset_b', 'L3_conv_mod_w', 'L3_conv_mod_b']


def _constants():
    import numpy as _np

    p, f = _np.arange(P)[:, None], _np.arange(P)[None, :]
    cumulate = _np.zeros((P, 8, 4), _np.float32)
    for b in range(4):
        for slot, tap in enumerate(SNAKE_TAPS):
            for step in (range(tap, 4) if tap < 4 else range(5, tap + 1)):
                cumulate[32 * b + step, slot, b] = 1
    return _np.concatenate([p == f, (p // 2 == f // 2) / 2, (p // 4 == f // 4) / 4, (p % 32 == f % 32) / 4,
                            cumulate.reshape(P, 32)], axis=1).astype(_np.float32)


def kernel(**inputs):
    import numpy as _np
    import concourse.bacc as _bacc
    from concourse import mybir as _mybir
    from concourse.bass_utils import run_bass_kernel_spmd as _run

    nc = _bacc.Bacc("TRN2", target_bir_lowering=False, num_devices=1)
    arrays, args = {"in_const": _constants()}, {}
    for name in _INS:
        a = _np.ascontiguousarray(inputs[name])
        arrays[f"in_{name}"] = a.reshape(a.shape or (1,))
    for name, a in arrays.items():
        args[name[3:]] = nc.dram_tensor(name, a.shape, _mybir.dt.from_np(a.dtype), kind="ExternalInput").ap()
    out = nc.dram_tensor("out", (8, 32, 128, 128), _mybir.dt.float32, kind="ExternalOutput").ap()
    build(nc, args, out)
    r = _run(nc, [arrays], core_ids=[0])
    return r.results[0]["out"]
```

```python
from contextlib import ExitStack

import concourse.bass as bass
from concourse import mybir

F32 = mybir.dt.float32
I32 = mybir.dt.int32
U32 = mybir.dt.uint32
ALU = mybir.AluOpType
ACT = mybir.ActivationFunctionType
AX = mybir.AxisListType

B, C, H, W = 8, 32, 128, 128
P = 128
GI = P // C
NG = B // GI
PX = H * W
BANK = 512
GN_EPS = 1e-5


class Space:

    def __init__(self, nc, ctx, tag):
        self.nc, self.ctx, self.tag = nc, ctx, tag
        self.sems = []
        ctx.callback(self.close)

    def sb(self, name, shape, dt=F32):
        return self.ctx.enter_context(self.nc.sbuf_tensor(f"{self.tag}_{name}", shape, dt))

    def ps(self, name, shape=(P, BANK), dt=F32):
        return self.ctx.enter_context(self.nc.psum_tensor(f"{self.tag}_{name}", list(shape), dt))

    def sem(self, name):
        self.sems.append(self.nc.alloc_semaphore(f"{self.tag}_{name}"))
        return self.sems[-1]

    def close(self):
        if self.sems:
            self.nc.clear_and_free_semaphores(self.sems)
            self.nc.all_engine_barrier()


def in_pairs(eng, n, body):
    body(0, 0, True)
    body(1, 1, True)
    if n > 2:
        with eng.Fori(1, n // 2) as i:
            body(i * 2, 0, False)
            body(i * 2 + 1, 1, False)


def turn(t):
    return t // 2
SNAKE_TAPS = (0, 8, 1, 7, 2, 6, 3, 5)


def in_pairs_last(eng, n, body):
    body(0, 0, True, False)
    body(1, 1, True, False)
    with eng.Fori(1, n // 2 - 1) as i:
        body(i * 2, 0, False, False)
        body(i * 2 + 1, 1, False, False)
    body(n - 2, 0, False, False)
    body(n - 1, 1, False, True)


OFFS = GI * 18 + GI


def blur(nc, x, sigma, x1):
    NB = 16
    CH = B * C // NB
    COLS = NB * W
    Q = COLS // BANK
    R = 5
    K = 2 * R + 1
    x_v = x.rearrange("b c h w -> h (b c) w")
    x1_v = x1.rearrange("b c h w -> h (b c) w")

    with ExitStack() as ctx:
        s = Space(nc, ctx, "blur")
        xs = [s.sb(f"x{i}", [P, NB, W]) for i in range(2)]
        cen = [s.sb(f"centred{i}", [P, NB, W]) for i in range(2)]
        squares = s.sb("squares", [P, NB, W])
        rowsum = s.sb("rowsum", [P, NB])
        sqsum = s.sb("sqsum", [P, NB])
        std = s.sb("std", [P, NB])
        rstd = s.sb("rstd", [P, NB])
        half = s.sb("half", [P, Q, BANK])
        mean_w = s.sb("mean_w", [P, P])
        band = s.sb("band", [P, P])
        dist = s.sb("dist", [P, P])
        term = s.sb("term", [P, P])
        sg = s.sb("sigma", [P, 1])
        rs = s.sb("rsigma", [P, 1])
        ax = s.sb("ax", [P, K])
        ax2 = s.sb("ax2", [P, K])
        g = s.sb("g", [P, K])
        gs = s.sb("gsum", [P, 1])
        eps = s.sb("eps", [P, 1])
        p_stat = s.ps("stat", [P, 2, 32])
        p_half = [s.ps(f"half{i}") for i in range(2)]
        p_out = [s.ps(f"out{i}") for i in range(Q)]

        sigma_in = s.sem("sigma_in")
        iota_done = s.sem("iota_done")
        chain = s.sem("vector_chain")
        exp_in = s.sem("exp_in")
        exp_done = s.sem("exp_done")
        consts = s.sem("constants_ready")
        loaded = [s.sem(f"loaded{i}") for i in range(2)]
        stored = [s.sem(f"stored{i}") for i in range(2)]
        rowsum_ready = s.sem("rowsum_ready")
        mean_ready = s.sem("mean_ready")
        centred = s.sem("centred")
        squared = s.sem("squared")
        sqsum_ready = s.sem("sqsum_ready")
        var_ready = s.sem("var_ready")
        std_ready = s.sem("std_ready")
        rstd_ready = s.sem("rstd_ready")
        normed = s.sem("normed")
        half_ready = s.sem("half_ready")
        half_copied = s.sem("half_copied")
        out_ready = s.sem("out_ready")
        x1_ready = s.sem("x1_ready")
        block = ctx.enter_context(nc.Block())

        @block.sync
        def _(sp):
            sp.dma_start(sg[:, :], bass.AP(tensor=sigma.tensor, offset=0, ap=[[0, P], [1, 1]])).then_inc(sigma_in, 16)

            def load(t, slot, first):
                if not first:
                    sp.wait_ge(stored[slot], turn(t) * 16)
                sp.dma_start(xs[slot][:, :, :], x_v[:, t * NB:(t + 1) * NB, :]).then_inc(loaded[slot], 16)

            for t in range(CH):
                load(t, t % 2, t < 2)
            for slot in range(2):
                sp.wait_ge(stored[slot], CH // 2 * 16)

        @block.gpsimd
        def _(pool):
            pool.iota(dist[:, :], pattern=[[1, P]], base=0, channel_multiplier=-1,
                      allow_small_or_imprecise_dtypes=True).then_inc(iota_done, 1)
            pool.iota(ax[:, :], pattern=[[1, K]], base=-R, channel_multiplier=0,
                      allow_small_or_imprecise_dtypes=True).then_inc(iota_done, 1)

            def norm(t, slot, first):
                pool.wait_ge(rstd_ready, t + 1)
                pool.tensor_tensor(cen[slot][:, :, :], cen[slot][:, :, :], rstd[:, :].unsqueeze(2).to_broadcast((P, NB, W)),
                                   ALU.mult).then_inc(normed, 1)

            in_pairs(pool, CH, norm)

        @block.scalar
        def _(act):
            act.wait_ge(exp_in, 1)
            act.activation(g[:, :], ax2[:, :], ACT.Exp, scale=-0.5).then_inc(exp_done, 1)

            def store(t, slot):
                act.wait_ge(x1_ready, t + 1)
                act.dma_start(x1_v[:, bass.ds(t * NB, NB), :], xs[slot][:, :, :]).then_inc(stored[slot], 16)

            def chunk(t, slot, first):
                act.wait_ge(centred, t + 1)
                if not (first and slot == 0):
                    act.wait_ge(sqsum_ready, t)
                act.activation(squares[:, :, :], cen[slot][:, :, :], ACT.Square).then_inc(squared, 1)
                if not (first and slot == 0):
                    store(t - 1, 1 - slot)
                act.wait_ge(var_ready, t + 1)
                act.activation(std[:, :], p_stat[:, 1, 0:NB], ACT.Sqrt, bias=eps[:, :]).then_inc(std_ready, 1)
                for q in range(Q):
                    act.wait_ge(half_ready, t * Q + q + 1)
                    if not (first and slot == 0):
                        act.wait_ge(out_ready, (t - 1) * Q + q + 1)
                    act.activation(half[:, q, :], p_half[q % 2][:, :], ACT.Copy).then_inc(half_copied, 1)

            in_pairs(act, CH, chunk)
            store(CH - 1, 1)

        @block.vector
        def _(dve):
            n = [0]

            def link(ins):
                n[0] += 1
                ins.then_inc(chain, 1)
                dve.wait_ge(chain, n[0])

            dve.memset(mean_w[:, :], 1.0 / PX)
            dve.memset(eps[:, :], GN_EPS)
            dve.wait_ge(sigma_in, 16)
            link(dve.tensor_scalar(rs[:, :], sg[:, :], -1.0, None, ALU.mult))
            link(dve.tensor_tensor(rs[:, :], rs[:, :], sg[:, :], ALU.max))
            link(dve.tensor_scalar(rs[:, :], rs[:, :], 1e-6, None, ALU.add))
            link(dve.reciprocal(rs[:, :], rs[:, :]))
            dve.wait_ge(iota_done, 2)
            link(dve.tensor_scalar(ax[:, :], ax[:, :], rs[:, :], None, ALU.mult))
            dve.tensor_tensor(ax2[:, :], ax[:, :], ax[:, :], ALU.mult).then_inc(exp_in, 1)
            dve.wait_ge(exp_done, 1)
            for _ in range(2):
                link(dve.tensor_reduce(gs[:, :], g[:, :], AX.X, ALU.add))
                link(dve.reciprocal(gs[:, :], gs[:, :]))
                link(dve.tensor_scalar(g[:, :], g[:, :], gs[:, :], None, ALU.mult))
            link(dve.tensor_scalar(band[:, :], dist[:, :], float(-R), g[:, 0:1], ALU.is_equal, ALU.mult))
            for k in range(1, K):
                link(dve.tensor_scalar(term[:, :], dist[:, :], float(k - R), g[:, k:k + 1], ALU.is_equal, ALU.mult))
                ins = dve.tensor_tensor(band[:, :], band[:, :], term[:, :], ALU.add)
                if k < K - 1:
                    link(ins)
            ins.then_inc(consts, 1)

            def finish(t, slot):
                for q in range(Q):
                    dve.wait_ge(out_ready, t * Q + q + 1)
                    v = xs[slot][:, :, :].rearrange("p n w -> p (n w)")[:, q * BANK:(q + 1) * BANK]
                    ins = dve.tensor_tensor(v, v, p_out[q][:, :], ALU.add)
                ins.then_inc(x1_ready, 1)

            def chunk(t, slot, first):
                dve.wait_ge(loaded[slot], turn(t) * 16 + 16)
                if not (first and slot == 0):
                    dve.wait_ge(mean_ready, t)
                dve.tensor_reduce(rowsum[:, :], xs[slot][:, :, :], AX.X, ALU.add).then_inc(rowsum_ready, 1)
                if not (first and slot == 0):
                    finish(t - 1, 1 - slot)
                dve.wait_ge(mean_ready, t + 1)
                dve.tensor_tensor(cen[slot][:, :, :], xs[slot][:, :, :],
                                  p_stat[:, 0, 0:NB].unsqueeze(2).to_broadcast((P, NB, W)), ALU.subtract).then_inc(centred, 1)
                dve.wait_ge(squared, t + 1)
                dve.tensor_reduce(sqsum[:, :], squares[:, :, :], AX.X, ALU.add).then_inc(sqsum_ready, 1)
                dve.wait_ge(std_ready, t + 1)
                if not (first and slot == 0):
                    dve.wait_ge(normed, t)
                dve.reciprocal(rstd[:, :], std[:, :]).then_inc(rstd_ready, 1)

            in_pairs(dve, CH, chunk)
            finish(CH - 1, 1)

        @block.tensor
        def _(pe):
            pe.wait_ge(consts, 1)

            def chunk(t, slot, first):
                pe.wait_ge(rowsum_ready, t + 1)
                if not (first and slot == 0):
                    pe.wait_ge(centred, t)
                pe.matmul(p_stat[:, 0, 0:NB], mean_w[:, :], rowsum[:, :], start=True, stop=True).then_inc(mean_ready, 1)
                pe.wait_ge(sqsum_ready, t + 1)
                pe.matmul(p_stat[:, 1, 0:NB], mean_w[:, :], sqsum[:, :], start=True, stop=True).then_inc(var_ready, 1)
                pe.wait_ge(normed, t + 1)

                def along_h(q):
                    if not (first and slot == 0 and q < 2):
                        pe.wait_ge(half_copied, t * Q + q - 1)
                    for j in range(4):
                        ins = pe.matmul(p_half[q % 2][:, j * W:(j + 1) * W], cen[slot][:, q * 4 + j, :], band[:, :],
                                        start=True, stop=True)
                    ins.then_inc(half_ready, 1)

                def along_w(q):
                    pe.wait_ge(half_copied, t * Q + q + 1)
                    if q == 0 and not (first and slot == 0):
                        pe.wait_ge(x1_ready, t)
                    for j in range(4):
                        ins = pe.matmul(p_out[q][:, j * W:(j + 1) * W], half[:, q, j * W:(j + 1) * W], band[:, :],
                                        start=True, stop=True)
                    ins.then_inc(out_ready, 1)

                along_h(0)
                for q in range(1, Q):
                    along_h(q)
                    along_w(q - 1)
                along_w(Q - 1)

            in_pairs(pe, CH, chunk)


class Kept:

    VECTORS = ['L1_conv_proj_bias', 'L1_conv_bn_gamma', 'L1_conv_bn_beta', 'L1_conv_scale_b', 'L2_conv_b_off',
               'L2_conv_gn_off_g', 'L2_conv_gn_off_b', 'L2_conv_b_dsc', 'L2_conv_gn_g', 'L2_conv_gn_b', 'L3_conv_bias']
    N_PAR = len(VECTORS) + 1

    def __init__(self, nc, ctx):
        s = Space(nc, ctx, "kept")
        self.const = s.sb("const", [P, 4 * P + 32])
        self.ident = self.const[:, 0:P]
        self.pair_mean = self.const[:, P:2 * P]
        self.quad_mean = self.const[:, 2 * P:3 * P]
        self.image_mean = self.const[:, 3 * P:4 * P]
        self.cumulate = self.const[:, 4 * P:4 * P + 32]
        self.par = s.sb("par", [P, self.N_PAR])
        self.w_off2 = s.sb("w_off2", [P, 9, P])
        self.w_dsc = s.sb("w_dsc", [P, 9, P])
        self.w_off3 = s.sb("w_off3", [P, 9, P])
        self.w_dcn = s.sb("w_dcn", [P, 9, P])
        self.eps = s.sb("eps", [P, 1])
        self.norm1 = s.sb("norm1", [P, NG, 2])
        self.hidden = s.sb("hidden", [P, NG, 2])
        self.gate = s.sb("gate", [P, NG, 2])
        self.dense = s.sb("dense", [1, 1], I32)
        self.snake_gn = s.sb("snake_gn", [P, 2])

    def for_gate(self, nc, ctx):
        s = Space(nc, ctx, "kept_gate")
        self.w_gate = s.sb("w_gate", [P, 9, P])
        self.w_scale = s.sb("w_scale", [P, 1, P])

    def vec(self, name):
        i = self.VECTORS.index(name)
        return self.par[:, i:i + 1]

    @property
    def bias3(self):
        return self.par[:, self.N_PAR - 1:self.N_PAR]


def make_weights(nc, a, k):
    jobs = [(k.w_gate, [('L1_conv_proj_weight', 0, 32)], 9), (k.w_scale, [('L1_conv_scale_w', 0, 32)], 1),
            (k.w_off2, [('L2_conv_w_off', 0, 18)], 9), (k.w_dsc, [('L2_conv_w_dsc', 0, 32)], 9),
            (k.w_off3, [('L3_conv_offset_w', 0, 18), ('L3_conv_mod_w', 18, 9)], 9), (k.w_dcn, [('L3_conv_weight', 0, 32)], 9)]
    with ExitStack() as ctx:
        s = Space(nc, ctx, "weights")
        nat = [s.sb(f"nat{n}", [P, C, j[2]]) for n, j in enumerate(jobs)]
        big = [s.sb(f"big{n}", [P, j[2], P]) for n, j in enumerate(jobs)]
        rows = s.sb("rows", [k.N_PAR, GI, 32])
        tr = [s.ps(f"tr{i}") for i in range(4)]
        cleared = s.sem("cleared")
        const_in = s.sem("const_in")
        rows_in = s.sem("rows_in")
        nat_in = s.sem("nat_in")
        blocks = s.sem("blocks")
        turned = s.sem("turned")
        copied = s.sem("copied")
        turns = [(n, t0, min(4, j[2] - t0)) for n, j in enumerate(jobs) for t0 in range(0, j[2], 4)]
        block = ctx.enter_context(nc.Block())

        @block.gpsimd
        def _(pool):
            pool.memset(rows[:, :, :], 0.0).then_inc(cleared, 1)
            for n in range(len(jobs)):
                pool.memset(nat[n][:, :, :], 0.0).then_inc(cleared, 1)

        @block.sync
        def _(sp):
            sp.dma_start(k.const[:, :], a["const"]).then_inc(const_in, 16)
            sp.wait_ge(cleared, 1)
            for i, name in enumerate(k.VECTORS + ['L3_conv_offset_b']):
                n = a[name].shape[0]
                sp.dma_start(rows[i:i + 1, :, 0:n], bass.AP(tensor=a[name].tensor, offset=0, ap=[[0, 1], [0, GI], [1, n]])).then_inc(rows_in, 16)
            sp.dma_start(rows[k.N_PAR - 1:k.N_PAR, :, 18:27],
                         bass.AP(tensor=a['L3_conv_mod_b'].tensor, offset=0, ap=[[0, 1], [0, GI], [1, 9]])).then_inc(rows_in, 16)
            sp.wait_ge(cleared, 1 + len(jobs))
            for n, (_, parts, taps) in enumerate(jobs):
                for name, o0, no in parts:
                    src = bass.AP(tensor=a[name].tensor, offset=0, ap=[[C * taps, no], [1, C * taps]])
                    for b in range(GI):
                        sp.dma_start(nat[n][32 * b + o0:32 * b + o0 + no, :, :].rearrange("p c t -> p (c t)"), src).then_inc(nat_in, 16)

        @block.vector
        def _(dve):
            dve.memset(k.eps[:, :], GN_EPS)
            for n in range(len(jobs)):
                ins = dve.memset(big[n][:, :, :], 0.0)
            ins.then_inc(blocks, 1)
            dve.wait_ge(blocks, 1)
            dve.wait_ge(nat_in, 16 * GI * sum(len(j[1]) for j in jobs))
            for n in range(len(jobs)):
                for b in range(GI):
                    r = slice(32 * b, 32 * b + 32)
                    ins = dve.tensor_copy(big[n][r, :, r], nat[n][r, :, :].rearrange("p c t -> p t c"))
            ins.then_inc(blocks, 1)

        @block.tensor
        def _(pe):
            pe.wait_ge(const_in, 16)
            pe.wait_ge(rows_in, 16 * (k.N_PAR + 1))
            pe.transpose(tr[0][:, 0:k.N_PAR], rows[:, :, :].rearrange("v b o -> v (b o)"), k.ident[0:k.N_PAR, 0:k.N_PAR]).then_inc(turned, 1)
            pe.wait_ge(blocks, 2)
            for i, (n, t0, nt) in enumerate(turns, 1):
                if i >= 4:
                    pe.wait_ge(copied, i - 3)
                for t in range(nt):
                    ins = pe.transpose(tr[i % 4][:, t * P:(t + 1) * P], big[n][:, t0 + t, :], k.ident)
                ins.then_inc(turned, 1)

        @block.scalar
        def _(act):
            act.wait_ge(turned, 1)
            act.activation(k.par[:, :], tr[0][:, 0:k.N_PAR], ACT.Copy).then_inc(copied, 1)
            for i, (n, t0, nt) in enumerate(turns, 1):
                act.wait_ge(turned, i + 1)
                act.activation(jobs[n][0][:, t0:t0 + nt, :].rearrange("p t o -> p (t o)"), tr[i % 4][:, 0:nt * P],
                               ACT.Copy).then_inc(copied, 1)


PAD = 4
HP = H + 2 * PAD


def gate_conv(nc, k, x1, g):
    x1_v = x1.rearrange("(g b) c h w -> g (b c) h w", g=NG)[g]
    LR = 16
    NL = H // LR
    UR = BANK // W
    NU = H // UR
    with ExitStack() as ctx:
        s = Space(nc, ctx, f"gateconv{g}")
        xg = s.sb("x", [P, H, W])
        xn = s.sb("xn", [P, H + 2, W + 2])
        st = s.sb("stats", [P, NU, 6])
        mv = s.sb("mean_var", [P, 2])
        std = s.sb("std", [P, 1])
        hid = [s.sb(f"hid{i}", [P, BANK]) for i in range(2)]
        hst = s.sb("hid_stats", [P, NU, 6])
        acc = [s.ps(f"acc{i}") for i in range(2)]
        loaded = [s.sem(f"loaded{i}") for i in range(NL)]
        chain = s.sem("vector_chain")
        var_ready = s.sem("var_ready")
        std_ready = s.sem("std_ready")
        coef_ready = s.sem("coef_ready")
        normed = s.sem("normed")
        padded = s.sem("padded")
        conv_done = s.sem("conv_done")
        hid_ready = s.sem("hid_ready")
        hid_used = s.sem("hid_used")
        block = ctx.enter_context(nc.Block())

        @block.sync
        def _(sp):
            for l in range(NL):
                sp.dma_start(xg[:, l * LR:(l + 1) * LR, :], x1_v[:, l * LR:(l + 1) * LR, :]).then_inc(loaded[l], 16)

        @block.vector
        def _(dve):
            n = [0]

            def link(ins):
                n[0] += 1
                ins.then_inc(chain, 1)
                dve.wait_ge(chain, n[0])

            for u in range(NU):
                if u % (LR // UR) == 0:
                    dve.wait_ge(loaded[u // (LR // UR)], 16)
                ins = dve.bn_stats(st[:, u, :], xg[:, u * UR:(u + 1) * UR, :].rearrange("p h w -> p (h w)"))
            link(ins)
            dve.bn_aggr(mv[:, :], st[:, :, :].rearrange("p u s -> p (u s)")).then_inc(var_ready, 1)
            dve.wait_ge(std_ready, 1)
            link(dve.reciprocal(k.norm1[:, g, 0:1], std[:, :]))
            dve.scalar_tensor_tensor(k.norm1[:, g, 1:2], mv[:, 0:1], -1.0, k.norm1[:, g, 0:1], ALU.mult, ALU.mult).then_inc(coef_ready, 1)
            dve.wait_ge(normed, 1)
            dve.tensor_copy(xn[:, 1:H + 1, 0:1], xn[:, 1:H + 1, W:W + 1])
            link(dve.tensor_copy(xn[:, 1:H + 1, W + 1:W + 2], xn[:, 1:H + 1, 1:2]))
            dve.tensor_copy(xn[:, 0, :], xn[:, H, :])
            dve.tensor_copy(xn[:, H + 1, :], xn[:, 1, :]).then_inc(padded, 1)

            def stats(u, slot, first):
                dve.wait_ge(hid_ready, u + 1)
                dve.bn_stats(hst[:, bass.ds(u, 1), :].rearrange("p u s -> p (u s)"), hid[slot][:, :]).then_inc(hid_used, 1)

            in_pairs(dve, NU, stats)
            dve.wait_ge(hid_used, NU)
            dve.bn_aggr(k.hidden[:, g, :], hst[:, :, :].rearrange("p u s -> p (u s)"))

        @block.scalar
        def _(act):
            act.wait_ge(var_ready, 1)
            act.activation(std[:, :], mv[:, 1:2], ACT.Sqrt, bias=k.eps[:, :]).then_inc(std_ready, 1)
            act.wait_ge(coef_ready, 1)
            act.activation(xn[:, 1:H + 1, 1:W + 1], xg[:, :, :], ACT.Identity, bias=k.norm1[:, g, 1:2],
                           scale=k.norm1[:, g, 0:1]).then_inc(normed, 1)

            def silu(u, slot, first):
                act.wait_ge(conv_done, u + 1)
                if not first:
                    act.wait_ge(hid_used, u - 1)
                act.activation(hid[slot][:, :], acc[slot][:, :], ACT.Silu, bias=k.vec('L1_conv_proj_bias')).then_inc(hid_ready, 1)

            in_pairs(act, NU, silu)

        @block.tensor
        def _(pe):
            pe.wait_ge(padded, 1)

            def conv(u, slot, first):
                if not first:
                    pe.wait_ge(hid_ready, u - 1)
                for t in range(9):
                    dy, dx = divmod(t, 3)
                    ins = pe.matmul(acc[slot][:, :], k.w_gate[:, t, :], xn[:, bass.ds(u * UR + dy, UR), dx:dx + W],
                                    start=(t == 0), stop=(t == 8))
                ins.then_inc(conv_done, 1)

            in_pairs(pe, NU, conv)


def gate_scale(nc, k):
    with ExitStack() as ctx:
        s = Space(nc, ctx, "gatescale")
        mu = s.sb("mu", [P, 1])
        d = s.sb("d", [P, NG])
        e = s.sb("e", [P, NG])
        std = s.sb("std", [P, 1])
        pooled = s.sb("pooled", [P, NG])
        sig = s.sb("sig", [P, NG])
        p_mean = s.ps("mean")
        p_var = s.ps("var")
        p_log = s.ps("logits")
        chain = s.sem("vector_chain")
        mean_ready = s.sem("mean_ready")
        spread_in = s.sem("spread_in")
        spread_ready = s.sem("spread_ready")
        var_in = s.sem("var_in")
        std_ready = s.sem("std_ready")
        pooled_ready = s.sem("pooled_ready")
        logits_ready = s.sem("logits_ready")
        sig_ready = s.sem("sig_ready")
        block = ctx.enter_context(nc.Block())

        @block.tensor
        def _(pe):
            pe.matmul(p_mean[:, 0:NG], k.image_mean, k.hidden[:, :, 0], start=True, stop=True).then_inc(mean_ready, 1)
            pe.wait_ge(spread_in, 1)
            pe.matmul(p_var[:, 0:NG], k.image_mean, e[:, :], start=True, stop=True).then_inc(spread_ready, 1)
            pe.wait_ge(pooled_ready, 1)
            pe.matmul(p_log[:, 0:NG], k.w_scale[:, 0, :], pooled[:, :], start=True, stop=True).then_inc(logits_ready, 1)

        @block.scalar
        def _(act):
            act.wait_ge(var_in, 1)
            act.activation(std[:, :], mu[:, :], ACT.Sqrt, bias=k.eps[:, :], scale=1.0 / NG).then_inc(std_ready, 1)
            act.wait_ge(logits_ready, 1)
            act.activation(sig[:, :], p_log[:, 0:NG], ACT.Sigmoid, bias=k.vec('L1_conv_scale_b')).then_inc(sig_ready, 1)

        @block.vector
        def _(dve):
            n = [0]

            def link(ins):
                n[0] += 1
                ins.then_inc(chain, 1)
                dve.wait_ge(chain, n[0])

            dve.wait_ge(mean_ready, 1)
            link(dve.tensor_reduce(mu[:, :], p_mean[:, 0:NG], AX.X, ALU.add))
            link(dve.tensor_scalar(mu[:, :], mu[:, :], 1.0 / NG, None, ALU.mult))
            link(dve.tensor_scalar(d[:, :], k.hidden[:, :, 0], mu[:, :], None, ALU.subtract))
            link(dve.tensor_tensor(e[:, :], d[:, :], d[:, :], ALU.mult))
            dve.tensor_tensor(e[:, :], e[:, :], k.hidden[:, :, 1], ALU.add).then_inc(spread_in, 1)
            dve.wait_ge(spread_ready, 1)
            dve.tensor_reduce(mu[:, :], p_var[:, 0:NG], AX.X, ALU.add).then_inc(var_in, 1)
            dve.wait_ge(std_ready, 1)
            link(dve.reciprocal(std[:, :], std[:, :]))
            link(dve.tensor_tensor(std[:, :], std[:, :], k.vec('L1_conv_bn_gamma'), ALU.mult))
            dve.tensor_scalar(pooled[:, :], d[:, :], std[:, :], k.vec('L1_conv_bn_beta'), ALU.mult, ALU.add).then_inc(pooled_ready, 1)
            dve.wait_ge(sig_ready, 1)
            link(dve.tensor_scalar(sig[:, :], sig[:, :], 0.1, None, ALU.add))
            dve.tensor_tensor(k.gate[:, :, :], k.norm1[:, :, :], sig[:, :].unsqueeze(2).to_broadcast((P, NG, 2)), ALU.mult)


def residual(nc, k, base, inner, func, scale, bias, result, xn, g):
    base_v, result_v = (t.rearrange("(g b) c h w -> g (b c) h w", g=NG)[g] for t in (base, result))
    UR = 8
    NU = H // UR
    HALF = UR // 2
    with ExitStack() as ctx:
        s = Space(nc, ctx, f"residual{g}{func.name}")
        xg = s.sb("x", [P, H, W])
        act_out = [s.sb(f"act{i}", [P, UR, W]) for i in range(2)]
        st = s.sb("stats", [P, 2 * NU, 6])
        mv = s.sb("mean_var", [P, 2])
        std = s.sb("std", [P, 1])
        coef = s.sb("coef", [P, 2])
        loaded = [s.sem(f"loaded{i}") for i in range(NU)]
        inner_loaded = [s.sem(f"inner_loaded{i}") for i in range(2)]
        chain = s.sem("vector_chain")
        act_ready = s.sem("act_ready")
        sum_ready = s.sem("sum_ready")
        stored = s.sem("stored")
        var_ready = s.sem("var_ready")
        std_ready = s.sem("std_ready")
        coef_ready = s.sem("coef_ready")
        block = ctx.enter_context(nc.Block())

        @block.sync
        def _(sp):
            for u in range(NU):
                if inner is not None:
                    if u >= 2:
                        sp.wait_ge(sum_ready, u - 1)
                    sp.dma_start(act_out[u % 2][:, :, :], inner[:, u * UR:(u + 1) * UR, :]).then_inc(inner_loaded[u % 2], 16)
                sp.dma_start(xg[:, u * UR:(u + 1) * UR, :], base_v[:, u * UR:(u + 1) * UR, :]).then_inc(loaded[u], 16)

        @block.gpsimd
        def _(pool):
            for r in (PAD - 1, PAD + H):
                pool.memset(xn[:, r, PAD - 1:PAD + W + 1], 0.0)
            for c in (PAD - 1, PAD + W):
                pool.memset(xn[:, PAD:PAD + H, c:c + 1], 0.0)
            for u in range(NU):
                pool.wait_ge(sum_ready, u + 1)
                pool.dma_start(result_v[:, u * UR:(u + 1) * UR, :], xg[:, u * UR:(u + 1) * UR, :]).then_inc(stored, 16)
            pool.wait_ge(stored, 16 * NU)

        @block.scalar
        def _(act):
            for u in range(NU):
                if inner is not None:
                    act.wait_ge(inner_loaded[u % 2], 16 * (u // 2 + 1))
                    src = act_out[u % 2][:, :, :]
                else:
                    act.wait_ge(loaded[u], 16)
                    if u >= 2:
                        act.wait_ge(sum_ready, u - 1)
                    src = xg[:, u * UR:(u + 1) * UR, :]
                act.activation(act_out[u % 2][:, :, :], src, func, bias=bias, scale=scale).then_inc(act_ready, 1)
            act.wait_ge(var_ready, 1)
            act.activation(std[:, :], mv[:, 1:2], ACT.Sqrt, bias=k.eps[:, :]).then_inc(std_ready, 1)
            act.wait_ge(coef_ready, 1)
            act.activation(xn[:, PAD:PAD + H, PAD:PAD + W], xg[:, :, :], ACT.Identity, bias=coef[:, 1:2], scale=coef[:, 0:1])

        @block.vector
        def _(dve):
            n = [0]

            def link(ins):
                n[0] += 1
                ins.then_inc(chain, 1)
                dve.wait_ge(chain, n[0])

            for u in range(NU):
                dve.wait_ge(loaded[u], 16)
                dve.wait_ge(act_ready, u + 1)
                v = xg[:, u * UR:(u + 1) * UR, :]
                dve.tensor_tensor(v, v, act_out[u % 2][:, :, :], ALU.add).then_inc(sum_ready, 1)
                dve.wait_ge(sum_ready, u + 1)
                for i in range(2):
                    ins = dve.bn_stats(st[:, 2 * u + i, :], xg[:, u * UR + i * HALF:u * UR + (i + 1) * HALF, :].rearrange("p h w -> p (h w)"))
            link(ins)
            dve.bn_aggr(mv[:, :], st[:, :, :].rearrange("p u s -> p (u s)")).then_inc(var_ready, 1)
            dve.wait_ge(std_ready, 1)
            link(dve.reciprocal(coef[:, 0:1], std[:, :]))
            dve.scalar_tensor_tensor(coef[:, 1:2], mv[:, 0:1], -1.0, coef[:, 0:1], ALU.mult, ALU.mult).then_inc(coef_ready, 1)


def schedule(groups):
    steps, ready, late = [], {}, None
    for m, terms in enumerate(groups):
        for i, term in enumerate(terms):
            steps.append((True, m, i, term))
            if len(terms) == 1:
                ready[m] = len(ready)
            if late is not None:
                steps.append((False, late, 0, None))
                ready[late] = len(ready)
                late = None
        if len(terms) == 2:
            late = m
    if late is not None:
        steps.append((False, late, 0, None))
        ready[late] = len(ready)
    return steps, ready


def make_sums(eng, u, groups, n0, per, shift, ring, more, ready, pair, pairs, pairs0, used, fresh, product, part, between=None):
    steps, number = schedule(groups)
    p0 = made = 0
    for at, (is_product, m, i, term) in enumerate(steps):
        if between is not None and at == (len(steps) + 1) // 2:
            between()
            between = None
        N = n0 + number[m]
        place = ring[(shift + N) % len(ring)]
        if not is_product:
            eng.wait_ge(pair, u * pairs + (pairs0 + p0))
            ins = eng.tensor_tensor(part(place), part(place), part(more[(pairs0 + p0) % len(more)]), ALU.add)
        elif i == 1:
            p0 += 1
            if len(more) == 1 and not (fresh and n0 + made == 0):
                eng.wait_ge(ready, u * per + (n0 + made))
            product(term, more[(pairs0 + p0) % len(more)]).then_inc(pair, 1)
            continue
        else:
            if not (fresh and N < len(ring)):
                eng.wait_ge(used, u * per + (N - len(ring) + 1))
            ins = product(term, place)
            if len(groups[m]) == 2:
                continue
        ins.then_inc(ready, 1)
        made += 1
    if between is not None:
        between()


def by_turns(of_v, of_p):
    spread = [((i + 1) / len(x), which, i) for which, x in enumerate((of_v, of_p)) for i in range(len(x))]
    return [(of_v, of_p)[which][i] for _, which, i in sorted(spread)]


def pairs_in(groups):
    return sum(len(m) == 2 for m in groups)


def snake_offsets(nc, k, xn, off, g):
    UR = BANK // W
    NU = H // UR
    TR = 8
    NT = H // TR
    with ExitStack() as ctx:
        s = Space(nc, ctx, f"snakeoff{g}")
        raw = s.sb("raw", [P, H, W])
        tanh = [s.sb(f"tanh{i}", [P, TR, W]) for i in range(2)]
        st = s.sb("stats", [P, NU, 6])
        mv = s.sb("mean_var", [P, 2])
        gm = s.sb("group_mean", [P, 1])
        d = s.sb("d", [P, 1])
        e = s.sb("e", [P, 1])
        std = s.sb("std", [P, 1])
        coef = s.sb("coef", [P, 2])
        acc = [s.ps(f"acc{i}") for i in range(2)]
        p_mean = s.ps("mean")
        p_var = s.ps("var")
        p_off = [s.ps(f"off{i}", [P, TR, 32]) for i in range(2)]
        chain = s.sem("vector_chain")
        conv_done = s.sem("conv_done")
        raw_ready = s.sem("raw_ready")
        stats_done = s.sem("stats_done")
        mean_in = s.sem("mean_in")
        mean_ready = s.sem("mean_ready")
        var_in = s.sem("var_in")
        var_ready = s.sem("var_ready")
        std_ready = s.sem("std_ready")
        coef_ready = s.sem("coef_ready")
        tanh_ready = s.sem("tanh_ready")
        sums_ready = s.sem("sums_ready")
        off_ready = s.sem("off_ready")
        block = ctx.enter_context(nc.Block())

        @block.tensor
        def _(pe):
            def conv(u, slot, first):
                if not first:
                    pe.wait_ge(raw_ready, u - 1)
                for t in range(9):
                    dy, dx = divmod(t, 3)
                    ins = pe.matmul(acc[slot][:, :], k.w_off2[:, t, :],
                                    xn[:, bass.ds(u * UR + (PAD - 1 + dy), UR), PAD - 1 + dx:PAD - 1 + dx + W],
                                    start=(t == 0), stop=(t == 8))
                ins.then_inc(conv_done, 1)

            in_pairs(pe, NU, conv)
            pe.wait_ge(mean_in, 1)
            pe.matmul(p_mean[:, 0:1], k.pair_mean, mv[:, 0:1], start=True, stop=True).then_inc(mean_ready, 1)
            pe.wait_ge(var_in, 1)
            pe.matmul(p_var[:, 0:1], k.pair_mean, e[:, :], start=True, stop=True).then_inc(var_ready, 1)

            def cumulate(t, slot, first):
                pe.wait_ge(tanh_ready, t + 1)
                if not first:
                    pe.wait_ge(off_ready, t - 1)
                for i in range(TR):
                    ins = pe.matmul(p_off[slot][:, i, :], tanh[slot][:, i, :], k.cumulate, start=True, stop=True)
                ins.then_inc(sums_ready, 1)

            in_pairs(pe, NT, cumulate)

        @block.scalar
        def _(act):
            def evacuate(u, slot, first):
                act.wait_ge(conv_done, u + 1)
                act.activation(raw[:, bass.ds(u * UR, UR), :].rearrange("p h w -> p (h w)"), acc[slot][:, :], ACT.Identity,
                               bias=k.vec('L2_conv_b_off')).then_inc(raw_ready, 1)

            in_pairs(act, NU, evacuate)
            act.wait_ge(var_ready, 1)
            act.activation(std[:, :], p_var[:, 0:1], ACT.Sqrt, bias=k.eps[:, :]).then_inc(std_ready, 1)
            act.wait_ge(coef_ready, 1)

            def squash(t, slot, first):
                if not first:
                    act.wait_ge(sums_ready, t - 1)
                act.activation(tanh[slot][:, :, :], raw[:, bass.ds(t * TR, TR), :], ACT.Tanh, bias=coef[:, 1:2],
                               scale=coef[:, 0:1]).then_inc(tanh_ready, 1)

            in_pairs(act, NT, squash)

        @block.vector
        def _(dve):
            n = [0]

            def link(ins):
                n[0] += 1
                ins.then_inc(chain, 1)
                dve.wait_ge(chain, n[0])

            def stats(u, slot, first):
                dve.wait_ge(raw_ready, u + 1)
                dve.bn_stats(st[:, bass.ds(u, 1), :].rearrange("p u s -> p (u s)"),
                             raw[:, bass.ds(u * UR, UR), :].rearrange("p h w -> p (h w)")).then_inc(stats_done, 1)

            in_pairs(dve, NU, stats)
            dve.wait_ge(stats_done, NU)
            dve.bn_aggr(mv[:, :], st[:, :, :].rearrange("p u s -> p (u s)")).then_inc(mean_in, 1)
            dve.wait_ge(mean_in, 1)
            dve.wait_ge(mean_ready, 1)
            link(dve.tensor_copy(gm[:, :], p_mean[:, 0:1]))
            link(dve.tensor_tensor(d[:, :], mv[:, 0:1], gm[:, :], ALU.subtract))
            link(dve.tensor_tensor(d[:, :], d[:, :], d[:, :], ALU.mult))
            dve.tensor_tensor(e[:, :], d[:, :], mv[:, 1:2], ALU.add).then_inc(var_in, 1)
            dve.wait_ge(std_ready, 1)
            link(dve.reciprocal(std[:, :], std[:, :]))
            link(dve.tensor_tensor(coef[:, 0:1], std[:, :], k.vec('L2_conv_gn_off_g'), ALU.mult))
            link(dve.tensor_tensor(d[:, :], gm[:, :], coef[:, 0:1], ALU.mult))
            dve.tensor_tensor(coef[:, 1:2], k.vec('L2_conv_gn_off_b'), d[:, :], ALU.subtract).then_inc(coef_ready, 1)

            def keep(t, slot, first):
                dve.wait_ge(sums_ready, t + 1)
                dve.tensor_copy(off[:, bass.ds(t * TR, TR), :], p_off[slot][:, :, :]).then_inc(off_ready, 1)

            in_pairs(dve, NT, keep)


def snake(nc, k, xn, off, pre, g):
    UR = 8
    NU = H // UR
    COLS = UR * W
    REACH = [abs(t - 4) for t in SNAKE_TAPS]
    NS = len(SNAKE_TAPS)
    DR = UR + 7
    GROUPS = [[(r, min(4, UR - 1 + 2 * n - r)) for r in range(0, UR - 1 + 2 * n, 4)] for n in REACH]
    POOL_TERMS = {4: [((0, 0), (1, 0)), ((0, 1),)], 3: [((0, 0), (1, 0)), ((0, 1),)], 2: [((0, 0),)], 1: [((0, 0),)]}
    DVE_TERMS = {4: [((1, 1), (0, 2)), ((1, 2), (0, 3)), ((1, 3),)], 3: [((1, 1), (0, 2)), ((1, 2),)],
                 2: [((1, 0), (0, 1)), ((1, 1),)], 1: [((1, 0),)]}
    ON_POOL = [POOL_TERMS[n] for n in REACH]
    ON_DVE = [DVE_TERMS[n] for n in REACH]
    for n in REACH:
        assert sorted(sum(POOL_TERMS[n] + DVE_TERMS[n], ())) == [(sg, j) for sg in (0, 1) for j in range(n)]
    NV, NP_, NG_ = (sum(len(x) for x in y) for y in (ON_DVE, ON_POOL, GROUPS))
    pairs_v0, pairs_p0 = ([sum(pairs_in(x) for x in y[:q]) for q in range(NS + 1)] for y in (ON_DVE, ON_POOL))
    PAIRS_V, PAIRS_P = pairs_v0[NS], pairs_p0[NS]
    RV, RP = 4, 3
    assert NV % RV == 0 and NP_ % RP == 0 and NG_ % 2 == 0
    first_v = [sum(len(x) for x in ON_DVE[:q]) for q in range(NS)]
    first_p = [sum(len(x) for x in ON_POOL[:q]) for q in range(NS)]
    first_g = [sum(len(x) for x in GROUPS[:q]) for q in range(NS)]

    BASE_J = [0, 8, 14, 18]
    with ExitStack() as ctx:
        s = Space(nc, ctx, f"snake{g}")
        diff = s.sb("diff", [P, DR, HP])
        dk = [s.sb(f"dk{i}", [P, UR - 1 + 2 * REACH[i], P]) for i in range(4)]
        clip = [s.sb(f"clip{i}", [P, 2, 20, UR, GI]) for i in range(2)]
        prod_v = [s.sb(f"prod_v{i}", [P, UR, P]) for i in range(RV)]
        prod_p = [s.sb(f"prod_p{i}", [P, UR, P]) for i in range(RP)]
        more_v = [s.sb(f"more_v{i}", [P, UR, P]) for i in range(2)]
        more_p = [s.sb(f"more_p{i}", [P, UR, P]) for i in range(1)]
        minus = s.sb("minus", [P, 4])
        tk = [s.sb(f"tk{i}", [P, COLS]) for i in range(2)]
        ob = s.sb("ob", [P, COLS])
        st = s.sb("stats", [P, 2 * NU, 6])
        mv = s.sb("mean_var", [P, 2])
        gm = s.sb("group_mean", [P, 1])
        d = s.sb("d", [P, 1])
        e = s.sb("e", [P, 1])
        std = s.sb("std", [P, 1])
        p_d = [s.ps(f"d{i}") for i in range(2)]
        p_t = [s.ps(f"t{i}", [P, COLS]) for i in range(2)]
        p_o = s.ps("o", [P, COLS])
        chain = s.sem("vector_chain")
        padded = s.sem("padded")
        diff_ready = s.sem("diff_ready")
        minus_ready = s.sem("minus_ready")
        relu_ready = s.sem("relu_ready")
        clip_ready = s.sem("clip_ready")
        v_pair = s.sem("v_pair")
        p_pair = s.sem("p_pair")
        turned = s.sem("turned")
        dk_copied = s.sem("dk_copied")
        v_ready = s.sem("v_ready")
        v_used = s.sem("v_used")
        p_ready = s.sem("p_ready")
        p_used = s.sem("p_used")
        t_ready = s.sem("t_ready")
        t_copied = s.sem("t_copied")
        w_done = s.sem("w_done")
        out_ready = s.sem("out_ready")
        out_copied = s.sem("out_copied")
        ob_stats = s.sem("ob_stats")
        stored = s.sem("stored")
        mean_in = s.sem("mean_in")
        mean_ready = s.sem("mean_ready")
        var_in = s.sem("var_in")
        var_ready = s.sem("var_ready")
        std_ready = s.sem("std_ready")
        block = ctx.enter_context(nc.Block())

        def units(eng, body):
            body(0, True, False)
            with eng.Fori(1, NU - 1) as u:
                body(u, False, False)
            body(NU - 1, False, True)

        @block.sync
        def _(sp):
            def store(u, first, last):
                sp.wait_ge(out_copied, u + 1)
                sp.dma_start(pre[:, bass.ds(u * UR, UR), :].rearrange("p h w -> p (h w)"), ob[:, :]).then_inc(stored, 16)

            units(sp, store)
            sp.wait_ge(stored, 16 * NU)

        @block.tensor
        def _(pe):
            def turn_d(u, q, i, first):
                tap, n = SNAKE_TAPS[q], REACH[q]
                r0, nr = GROUPS[q][i]
                G = first_g[q] + i
                if G == 0:
                    pe.wait_ge(diff_ready, u + 1)
                if not (first and G < 2):
                    pe.wait_ge(dk_copied, u * NG_ + (G - 1))
                for r in range(nr):
                    ins = pe.transpose(p_d[G % 2][:, r * P:(r + 1) * P], diff[:, 4 - n + r0 + r, tap:tap + W], k.ident)
                ins.then_inc(turned, 1)

            def add_products(u, q, first, last):
                if not (first and q < 2):
                    pe.wait_ge(t_copied, u * NS + (q - 1))
                at, total = 0, len(ON_DVE[q]) + len(ON_POOL[q])
                later = [] if last and q + 2 >= NS else list(range(len(GROUPS[(q + 2) % NS])))

                def turn_next():
                    if q + 2 < NS:
                        turn_d(u, q + 2, later.pop(0), first)
                    else:
                        turn_d(u + 1, q + 2 - NS, later.pop(0), False)

                of_v = [(m, first_v[q], NV, prod_v, v_ready, v_used) for m in range(len(ON_DVE[q]))]
                of_p = [(m, first_p[q], NP_, prod_p, p_ready, p_used) for m in range(len(ON_POOL[q]))]
                for m, n0, per, ring, ready, used in by_turns(of_v, of_p):
                    if later and q != NS - 2:
                        turn_next()
                    pe.wait_ge(ready, u * per + (n0 + m + 1))
                    for r in range(UR):
                        ins = pe.matmul(p_t[q % 2][:, r * W:(r + 1) * W], ring[(n0 + m) % len(ring)][:, r, :], k.ident,
                                        start=(at == 0 and r % 4 == 0), stop=(at == total - 1 and r % 4 == 3), is_transpose=True)
                    ins.then_inc(used, 1)
                    at += 1
                while later:
                    turn_next()

            def middle_tap(u, first):
                if not first:
                    pe.wait_ge(out_copied, u)
                for half in range(2):
                    pe.matmul(p_o[:, half * BANK:(half + 1) * BANK], k.w_dsc[:, 4, :],
                              xn[:, bass.ds(u * UR + (PAD + 4 * half), 4), 4:4 + W], start=True, stop=False)

            def weigh(u, q):
                pe.wait_ge(t_copied, u * NS + (q + 1))
                for half in range(2):
                    ins = pe.matmul(p_o[:, half * BANK:(half + 1) * BANK], k.w_dsc[:, SNAKE_TAPS[q], :],
                                    tk[q % 2][:, half * BANK:(half + 1) * BANK], start=False, stop=(q == NS - 1))
                ins.then_inc(w_done, 1)

            pe.wait_ge(padded, 1)
            for q in range(2):
                for i in range(len(GROUPS[q])):
                    turn_d(0, q, i, True)

            def unit(u, first, last):
                for q in range(NS):
                    add_products(u, q, first, last)
                    if q == 0 and not first:
                        weigh(u - 1, NS - 1)
                    if q == 1:
                        middle_tap(u, first)
                    if q > 0:
                        weigh(u, q - 1)

            units(pe, unit)
            weigh(NU - 1, NS - 1)
            pe.wait_ge(mean_in, 1)
            pe.matmul(p_d[0][:, 0:1], k.quad_mean, mv[:, 0:1], start=True, stop=True).then_inc(mean_ready, 1)
            pe.wait_ge(var_in, 1)
            pe.matmul(p_d[1][:, 0:1], k.quad_mean, e[:, :], start=True, stop=True).then_inc(var_ready, 1)

        @block.scalar
        def _(act):
            def copy_d(u, q, first):
                if not (first and q < 4):
                    if q >= 4:
                        v, p = u * NV + first_v[q - 3], u * NP_ + first_p[q - 3]
                    else:
                        v, p = (u - 1) * NV + (first_v + [NV])[q + NS - 3], (u - 1) * NP_ + (first_p + [NP_])[q + NS - 3]
                    act.wait_ge(v_ready, v)
                    act.wait_ge(p_ready, p)
                for i, (r0, nr) in enumerate(GROUPS[q]):
                    G = first_g[q] + i
                    act.wait_ge(turned, u * NG_ + (G + 1))
                    act.activation(dk[q % 4][:, r0:r0 + nr, :].rearrange("p r c -> p (r c)"), p_d[G % 2][:, 0:nr * P],
                                   ACT.Copy).then_inc(dk_copied, 1)

            def relus(u, slot, first):
                if not first:
                    act.wait_ge(v_ready, (u - 1) * NV)
                    act.wait_ge(p_ready, (u - 1) * NP_)
                for sg in range(2):
                    for j in range(4):
                        w = 2 * (4 - j)
                        ins = act.activation(clip[slot][:, sg, BASE_J[j]:BASE_J[j] + w, :, :],
                                             off[:, bass.ds(u * UR, UR), 0:w * GI].rearrange("p r (s b) -> p s r b", b=GI),
                                             ACT.Relu, bias=minus[:, j:j + 1], scale=1.0 if sg == 0 else -1.0)
                ins.then_inc(relu_ready, 1)

            def copy_out(u, first):
                act.wait_ge(w_done, u * NS + NS)
                if not first:
                    act.wait_ge(stored, u * 16)
                    act.wait_ge(ob_stats, u)
                act.activation(ob[:, :], p_o[:, :], ACT.Identity, bias=k.vec('L2_conv_b_dsc')).then_inc(out_copied, 1)

            act.wait_ge(minus_ready, 4)
            relus(0, 0, True)
            copy_d(0, 0, True)
            copy_d(0, 1, True)

            def unit(u, slot, first, last):
                for q in range(NS):
                    if q < NS - 2:
                        copy_d(u, q + 2, first and slot == 0)
                    elif not last:
                        copy_d(u + 1, q + 2 - NS, False)
                    if q == 0 and not (first and slot == 0):
                        copy_out(u - 1, first)
                    if q == 1 and not last:
                        relus(u + 1, 1 - slot, first and slot == 0)

            in_pairs_last(act, NU, unit)
            copy_out(NU - 1, False)
            act.wait_ge(var_ready, 1)
            act.activation(std[:, :], p_d[1][:, 0:1], ACT.Sqrt, bias=k.eps[:, :]).then_inc(std_ready, 1)

        def product_of(eng, slot, q):
            def product(term, place):
                n = REACH[q]
                sg, j = term
                r = n + j if sg == 0 else n - 1 - j
                rows = dk[q % 4][:, r:r + UR, :].rearrange("p r (b c) -> p (r b) c", b=GI)
                f = clip[slot][:, sg, BASE_J[j] + q, :, :].rearrange("p r b -> p (r b)").unsqueeze(2).to_broadcast((P, UR * GI, C))
                return eng.tensor_tensor(place[:, :, :].rearrange("p r (b c) -> p (r b) c", b=GI), f, rows, ALU.mult)
            return product

        def whole(place):
            return place[:, :, :]

        @block.gpsimd
        def _(pool):
            def unit(u, slot, first):
                pool.wait_ge(clip_ready, u + 1)
                for q in range(NS):
                    pool.wait_ge(dk_copied, u * NG_ + (first_g[q] + len(GROUPS[q])))
                    make_sums(pool, u, ON_POOL[q], first_p[q], NP_, 0, prod_p, more_p, p_ready, p_pair, PAIRS_P,
                              pairs_p0[q], p_used, first and slot == 0, product_of(pool, slot, q), whole)

            in_pairs(pool, NU, unit)

        @block.vector
        def _(dve):
            n = [0]

            def link(ins):
                n[0] += 1
                ins.then_inc(chain, 1)
                dve.wait_ge(chain, n[0])

            dve.tensor_copy(xn[:, 0:PAD, PAD:PAD + W], xn[:, PAD:PAD + 1, PAD:PAD + W].to_broadcast((P, PAD, W)))
            link(dve.tensor_copy(xn[:, PAD + H:HP, PAD:PAD + W], xn[:, PAD + H - 1:PAD + H, PAD:PAD + W].to_broadcast((P, PAD, W))))
            dve.tensor_copy(xn[:, :, 0:PAD], xn[:, :, PAD:PAD + 1].to_broadcast((P, HP, PAD)))
            dve.tensor_copy(xn[:, :, PAD + W:HP], xn[:, :, PAD + W - 1:PAD + W].to_broadcast((P, HP, PAD))).then_inc(padded, 1)
            dve.wait_ge(padded, 1)

            def differences(u):
                dve.tensor_tensor(diff[:, :, :], xn[:, bass.ds(u * UR + 1, DR), :], xn[:, bass.ds(u * UR, DR), :],
                                  ALU.subtract).then_inc(diff_ready, 1)

            def clips(u, slot):
                dve.wait_ge(relu_ready, u + 1)
                for sg in range(2):
                    ins = dve.tensor_scalar(clip[slot][:, sg, :, :, :], clip[slot][:, sg, :, :, :], 1.0, 1.0 if sg == 0 else -1.0,
                                            ALU.min, ALU.mult)
                ins.then_inc(clip_ready, 1)

            def add_x(u, q, first):
                dve.wait_ge(v_used, u * NV + (first_v + [NV])[q + 1])
                dve.wait_ge(p_used, u * NP_ + (first_p + [NP_])[q + 1])
                if not (first and q < 2):
                    dve.wait_ge(w_done, u * NS + (q - 1))
                tap = SNAKE_TAPS[q]
                dve.tensor_tensor(tk[q % 2][:, :].rearrange("p (r w) -> p r w", w=W), p_t[q % 2][:, :].rearrange("p (r w) -> p r w", w=W),
                                  xn[:, bass.ds(u * UR + PAD, UR), tap:tap + W], ALU.add).then_inc(t_copied, 1)

            def stats(u):
                dve.wait_ge(out_copied, u + 1)
                for i in range(2):
                    ins = dve.bn_stats(st[:, bass.ds(2 * u + i, 1), :].rearrange("p u s -> p (u s)"), ob[:, i * BANK:(i + 1) * BANK])
                ins.then_inc(ob_stats, 1)

            for j in range(4):
                dve.memset(minus[:, j:j + 1], float(-j)).then_inc(minus_ready, 1)
            differences(0)

            def unit(u, slot, first, last=False):
                fresh = first and slot == 0
                clips(u, slot)
                dve.wait_ge(clip_ready, u + 1)
                for q in range(NS):
                    if q == NS - 2 and not last:
                        dve.wait_ge(turned, u * NG_ + NG_)
                        differences(u + 1)
                    if q == 3 and not (first and slot == 0):
                        stats(u - 1)
                    dve.wait_ge(dk_copied, u * NG_ + (first_g[q] + len(GROUPS[q])))

                    def between():
                        if q > 0:
                            add_x(u, q - 1, fresh)
                        elif not fresh:
                            add_x(u - 1, NS - 1, False)

                    make_sums(dve, u, ON_DVE[q], first_v[q], NV, 0, prod_v, more_v, v_ready, v_pair, PAIRS_V,
                              pairs_v0[q], v_used, fresh, product_of(dve, slot, q), whole, between)

            unit(0, 0, True)
            unit(1, 1, True)
            with dve.Fori(1, NU // 2 - 1) as i:
                unit(i * 2, 0, False)
                unit(i * 2 + 1, 1, False)
            unit(NU - 2, 0, False)
            unit(NU - 1, 1, False, True)
            add_x(NU - 1, NS - 1, False)
            stats(NU - 1)
            dve.wait_ge(ob_stats, NU)
            dve.bn_aggr(mv[:, :], st[:, :, :].rearrange("p u s -> p (u s)")).then_inc(mean_in, 1)
            dve.wait_ge(mean_in, 1)
            dve.wait_ge(mean_ready, 1)
            link(dve.tensor_copy(gm[:, :], p_d[0][:, 0:1]))
            link(dve.tensor_tensor(d[:, :], mv[:, 0:1], gm[:, :], ALU.subtract))
            link(dve.tensor_tensor(d[:, :], d[:, :], d[:, :], ALU.mult))
            dve.tensor_tensor(e[:, :], d[:, :], mv[:, 1:2], ALU.add).then_inc(var_in, 1)
            dve.wait_ge(std_ready, 1)
            link(dve.reciprocal(std[:, :], std[:, :]))
            link(dve.tensor_tensor(k.snake_gn[:, 0:1], std[:, :], k.vec('L2_conv_gn_g'), ALU.mult))
            link(dve.tensor_tensor(d[:, :], gm[:, :], k.snake_gn[:, 0:1], ALU.mult))
            dve.tensor_tensor(k.snake_gn[:, 1:2], k.vec('L2_conv_gn_b'), d[:, :], ALU.subtract)


def dcn_offsets(nc, k, xn, offs, g):
    UR = 8
    NU = H // UR
    K2 = 9
    with ExitStack() as ctx:
        s = Space(nc, ctx, f"dcnoff{g}")
        cm = [s.sb(f"cm{i}", [P, UR, W]) for i in range(2)]
        sig = [s.sb(f"sig{i}", [P, UR, GI, K2]) for i in range(2)]
        msum = [s.sb(f"msum{i}", [P, UR, GI]) for i in range(2)]
        keep = [s.sb(f"keep{i}", [P, UR, OFFS]) for i in range(2)]
        far = s.sb("far", [P, NU])
        far1 = s.sb("far1", [P, 1])
        far0 = s.sb("far0", [1, 1])
        acc = [s.ps(f"acc{i}", [P, UR * W]) for i in range(2)]
        p_t = [s.ps(f"t{i}", [P, UR, GI, 32]) for i in range(2)]
        conv_done = s.sem("conv_done")
        cm_ready = s.sem("cm_ready")
        turned = s.sem("turned")
        sig_ready = s.sem("sig_ready")
        msum_ready = s.sem("msum_ready")
        keep_ready = s.sem("keep_ready")
        stored = [s.sem(f"stored{i}") for i in range(2)]
        far_ready = s.sem("far_ready")
        far_turned = s.sem("far_turned")
        chain = s.sem("vector_chain")
        block = ctx.enter_context(nc.Block())

        @block.tensor
        def _(pe):
            def turn_back(u, slot, first):
                pe.wait_ge(cm_ready, u + 1)
                if not first:
                    pe.wait_ge(keep_ready, u - 1)
                for r in range(UR):
                    ins = pe.transpose(p_t[slot][:, r, :, :].rearrange("p b o -> p (b o)"), cm[slot][:, r, :], k.ident)
                ins.then_inc(turned, 1)

            def conv(u, slot, first):
                if not first:
                    pe.wait_ge(cm_ready, u - 1)
                for half in range(2):
                    for t in range(9):
                        dy, dx = divmod(t, 3)
                        ins = pe.matmul(acc[slot][:, half * BANK:(half + 1) * BANK], k.w_off3[:, t, :],
                                        xn[:, bass.ds(u * UR + (4 * half + PAD - 1 + dy), 4), PAD - 1 + dx:PAD - 1 + dx + W],
                                        start=(t == 0), stop=(t == 8))
                ins.then_inc(conv_done, 1)

            conv(0, 0, True)
            conv(1, 1, True)
            turn_back(0, 0, True)
            conv(2, 0, False)
            turn_back(1, 1, True)
            conv(3, 1, False)
            with pe.Fori(2, NU // 2) as i:
                turn_back(i * 2 - 2, 0, False)
                conv(i * 2, 0, False)
                turn_back(i * 2 - 1, 1, False)
                conv(i * 2 + 1, 1, False)
            turn_back(NU - 2, 0, False)
            turn_back(NU - 1, 1, False)
            pe.wait_ge(far_ready, 1)
            pe.matmul(acc[0][0:1, 0:P], far1[:, :], k.ident, start=True, stop=True).then_inc(far_turned, 1)

        @block.scalar
        def _(act):
            def bias(u, slot, first):
                act.wait_ge(conv_done, u + 1)
                if not first:
                    act.wait_ge(turned, u - 1)
                act.activation(cm[slot][:, :, :].rearrange("p h w -> p (h w)"), acc[slot][:, :], ACT.Identity, bias=k.bias3).then_inc(cm_ready, 1)

            def sigmoid(u, slot, first):
                act.wait_ge(turned, u + 1)
                if not first:
                    act.wait_ge(msum_ready, u - 1)
                act.activation(sig[slot][:, :, :, :], p_t[slot][:, :, :, 18:27], ACT.Sigmoid).then_inc(sig_ready, 1)

            bias(0, 0, True)
            bias(1, 1, True)
            sigmoid(0, 0, True)
            bias(2, 0, False)
            sigmoid(1, 1, True)
            bias(3, 1, False)
            with act.Fori(2, NU // 2) as i:
                sigmoid(i * 2 - 2, 0, False)
                bias(i * 2, 0, False)
                sigmoid(i * 2 - 1, 1, False)
                bias(i * 2 + 1, 1, False)
            sigmoid(NU - 2, 0, False)
            sigmoid(NU - 1, 1, False)

        @block.vector
        def _(dve):
            def unit(u, slot, first):
                dve.wait_ge(sig_ready, u + 1)
                o = p_t[slot][:, :, :, 0:18]
                dve.tensor_reduce(msum[slot][:, :, :], sig[slot][:, :, :, :], AX.X, ALU.add).then_inc(msum_ready, 1)
                dve.tensor_reduce(far[:, bass.ds(u, 1)], o, AX.XYZ, ALU.max, apply_absolute_value=True)
                if not first:
                    dve.wait_ge(stored[slot], turn(u) * 16)
                dve.tensor_copy(keep[slot][:, :, 0:GI * 18].rearrange("p h (b o) -> p h b o", b=GI), o)
                dve.wait_ge(msum_ready, u + 1)
                dve.tensor_scalar(keep[slot][:, :, GI * 18:OFFS], msum[slot][:, :, :], 1.0 / K2, None, ALU.mult).then_inc(keep_ready, 1)

            in_pairs(dve, NU, unit)
            dve.wait_ge(keep_ready, NU)
            dve.tensor_reduce(far1[:, :], far[:, :], AX.X, ALU.max).then_inc(far_ready, 1)
            dve.wait_ge(far_turned, 1)
            dve.tensor_reduce(far0[:, :], acc[0][0:1, 0:P], AX.X, ALU.max).then_inc(chain, 1)
            dve.wait_ge(chain, 1)
            dve.tensor_scalar(k.dense[:, :], far0[:, :], 1.0, None, ALU.is_le)

        @block.sync
        def _(sp):
            def store(u, slot, first):
                sp.wait_ge(keep_ready, u + 1)
                sp.dma_start(offs[bass.ds(u * UR, UR), :, :].rearrange("h w f -> w h f"), keep[slot][:, :, :]).then_inc(stored[slot], 16)

            in_pairs(sp, NU, store)
            for slot in range(2):
                sp.wait_ge(stored[slot], NU // 2 * 16)


def dcn_gather(nc, k, xn, offs, table, x3, out, g):
    x3_v, out_v = (t.rearrange("(g b) c h w -> g (b c) h w", g=NG)[g] for t in (x3, out))
    table_v = table.rearrange("(b h w) c -> b w h c", b=GI, h=H)
    UR = 4
    NU = H // UR
    with ExitStack() as ctx:
        s = Space(nc, ctx, f"table{g}")
        win = s.sb("win", [P, UR, W])
        tb = s.sb("tb", [P, UR, P])
        p_w = s.ps("w", [P, UR * P])
        win_ready = s.sem("win_ready")
        turned = s.sem("turned")
        tb_ready = s.sem("tb_ready")
        stored = s.sem("stored")
        block = ctx.enter_context(nc.Block())

        def rows(eng, n, body):
            body(0, True)
            with eng.Fori(1, n) as u:
                body(u, False)

        @block.scalar
        def _(act):
            def stage(u, first):
                if not first:
                    act.wait_ge(turned, u)
                act.activation(win[:, :, :], xn[:, bass.ds(u * UR + PAD, UR), PAD:PAD + W], ACT.Copy).then_inc(win_ready, 1)

            rows(act, NU, stage)

        @block.tensor
        def _(pe):
            def turn_rows(u, first):
                pe.wait_ge(win_ready, u + 1)
                if not first:
                    pe.wait_ge(tb_ready, u)
                for r in range(UR):
                    ins = pe.transpose(p_w[:, r * P:(r + 1) * P], win[:, r, :], k.ident)
                ins.then_inc(turned, 1)

            rows(pe, NU, turn_rows)

        @block.vector
        def _(dve):
            def copy(u, first):
                dve.wait_ge(turned, u + 1)
                if not first:
                    dve.wait_ge(stored, u * (16 * GI))
                dve.tensor_copy(tb[:, :, :].rearrange("p r c -> p (r c)"), p_w[:, :]).then_inc(tb_ready, 1)

            rows(dve, NU, copy)

        @block.sync
        def _(sp):
            def store(u, first):
                sp.wait_ge(tb_ready, u + 1)
                for b in range(GI):
                    sp.dma_start(table_v[b, :, bass.ds(u * UR, UR), :], tb[:, :, b * C:(b + 1) * C]).then_inc(stored, 16)

            rows(sp, NU, store)
            sp.wait_ge(stored, 16 * GI * NU)
    for part in range(2):
        gather_rows(nc, k, offs, table, x3_v, out_v, f"{g}_{part}", part * (H // 2), H // 2)


def gather_rows(nc, k, offs, table, x3_v, out_v, tag, h0, n_rows):
    K2 = 9
    with ExitStack() as ctx:
        s = Space(nc, ctx, f"gather{tag}")
        off = s.sb("off", [P, OFFS])
        xr = s.sb("x3", [P, W])
        ob = s.sb("ob", [P, W])
        row = s.sb("row", [P, 1])
        col = s.sb("col", [P, 1])
        image = s.sb("image", [P, GI, K2])
        pos = s.sb("pos", [P, GI, 18])
        inside = s.sb("inside", [P, GI, 18])
        whole = s.sb("whole", [P, GI, 18], I32)
        base = s.sb("base", [P, GI, 18])
        gt = s.sb("gt", [P, GI, 18])
        dist = s.sb("dist", [P, 2, GI, 18])
        dabs = s.sb("dabs", [P, 2, GI, 18])
        hat = s.sb("hat", [P, 2, GI, 18])
        weight = s.sb("weight", [P, 4, GI, K2])
        flat = s.sb("flat", [P, GI, K2])
        index = s.sb("index", [P, 4, GI, K2], U32)
        near = [s.sb(f"near{i}", [P, 4, GI, C]) for i in range(3)]
        prod = s.sb("prod", [P, 4, GI, C])
        half = s.sb("half", [P, 2, P])
        samp = [s.sb(f"samp{i}", [P, P]) for i in range(2)]
        tk = [s.sb(f"tk{i}", [P, P]) for i in range(2)]
        p_t = [s.ps(f"t{i}") for i in range(2)]
        p_o = s.ps("o")
        iota_done = s.sem("iota_done")
        loaded = s.sem("loaded")
        x3_loaded = s.sem("x3_loaded")
        chain = s.sem("vector_chain")
        index_ready = s.sem("index_ready")
        gathered = [s.sem(f"gathered{i}") for i in range(3)]
        near_used = s.sem("near_used")
        samp_ready = s.sem("samp_ready")
        turned = s.sem("turned")
        tk_ready = s.sem("tk_ready")
        w_done = s.sem("w_done")
        ob_ready = s.sem("ob_ready")
        stored = s.sem("stored")
        index_step = s.sem("index_step")
        gather_go = s.sem("gather_go")
        half_ready = s.sem("half_ready")
        block = ctx.enter_context(nc.Block())

        def rows(eng, body):
            body(0, True)
            with eng.Fori(1, n_rows) as h:
                body(h, False)

        @block.sync
        def _(sp):
            def load(h, first):
                if not first:
                    sp.wait_ge(index_ready, h)
                sp.dma_start(off[:, :], offs[bass.ds(h + h0, 1), :, :].rearrange("h w f -> (h w) f")).then_inc(loaded, 16)
                if not first:
                    sp.wait_ge(ob_ready, h)
                sp.dma_start(xr[:, :], x3_v[:, bass.ds(h + h0, 1), :].rearrange("p h w -> p (h w)")).then_inc(x3_loaded, 16)
                sp.wait_ge(ob_ready, h + 1)
                sp.dma_start(out_v[:, bass.ds(h + h0, 1), :].rearrange("p h w -> p (h w)"), ob[:, :]).then_inc(stored, 16)

            rows(sp, load)
            sp.wait_ge(stored, 16 * n_rows)

        @block.gpsimd
        def _(pool):
            pool.iota(col[:, :], pattern=[[0, 1]], base=0, channel_multiplier=1, allow_small_or_imprecise_dtypes=True).then_inc(iota_done, 1)
            pool.iota(image[:, :, :], pattern=[[PX, GI], [0, K2]], base=0, channel_multiplier=0,
                      allow_small_or_imprecise_dtypes=True).then_inc(iota_done, 1)

            def gather(h, first):
                pool.wait_ge(index_ready, h + 1)
                for t in range(K2):
                    if not (first and t < 3):
                        pool.wait_ge(near_used, h * K2 + (t - 2))
                    pool.sem_inc(gather_go, 1)
                    for corner in range(4):
                        for b in range(GI):
                            pool.indirect_dma_start(out=near[t % 3][:, corner, b, :], out_offset=None, in_=table,
                                                    in_offset=bass.IndirectOffsetOnAxis(ap=index[:, corner, b, t:t + 1], axis=0)
                                                    ).then_inc(gathered[t % 3], 16)

            rows(pool, gather)

        @block.vector
        def _(dve):
            dve.wait_ge(iota_done, 2)
            dve.memset(row[:, :], float(h0)).then_inc(chain, 1)
            dve.wait_ge(chain, 1)
            STEPS = 15

            def positions(h, first):
                n = [0]

                def link(ins):
                    n[0] += 1
                    ins.then_inc(chain, 1)
                    dve.wait_ge(chain, h * STEPS + (n[0] + 1))

                dve.wait_ge(loaded, h * 16 + 16)
                o = off[:, 0:GI * 18].rearrange("p (b o) -> p b o", b=GI)
                dve.tensor_scalar(pos[:, :, 0:K2], o[:, :, 0:K2], row[:, :], None, ALU.add)
                link(dve.tensor_scalar(pos[:, :, K2:18], o[:, :, K2:18], col[:, :], None, ALU.add))
                link(dve.tensor_scalar(row[:, :], row[:, :], 1.0, None, ALU.add))
                link(dve.tensor_scalar(inside[:, :, :], pos[:, :, :], 0.0, float(H - 1), ALU.max, ALU.min))
                link(dve.tensor_copy(whole[:, :, :], inside[:, :, :]))
                link(dve.tensor_copy(base[:, :, :], whole[:, :, :]))
                link(dve.tensor_tensor(gt[:, :, :], base[:, :, :], inside[:, :, :], ALU.is_gt))
                link(dve.tensor_tensor(base[:, :, :], base[:, :, :], gt[:, :, :], ALU.subtract))
                link(dve.tensor_scalar(base[:, :, :], base[:, :, :], float(H - 2), None, ALU.min))
                link(dve.tensor_tensor(dist[:, 0, :, :], pos[:, :, :], base[:, :, :], ALU.subtract))
                link(dve.tensor_scalar(dist[:, 1, :, :], dist[:, 0, :, :], -1.0, None, ALU.add))
                link(dve.tensor_scalar(dabs[:, :, :, :], dist[:, :, :, :], -1.0, None, ALU.mult))
                link(dve.tensor_tensor(dabs[:, :, :, :], dabs[:, :, :, :], dist[:, :, :, :], ALU.max))
                link(dve.tensor_scalar(hat[:, :, :, :], dabs[:, :, :, :], -1.0, 1.0, ALU.mult, ALU.add))
                link(dve.tensor_scalar(hat[:, :, :, :], hat[:, :, :, :], 0.0, None, ALU.max))
                dve.tensor_scalar(flat[:, :, :], base[:, :, 0:K2], float(W), None, ALU.mult)
                link(dve.tensor_tensor(hat[:, :, :, 0:K2], hat[:, :, :, 0:K2],
                                       off[:, GI * 18:OFFS].unsqueeze(1).unsqueeze(3).to_broadcast((P, 2, GI, K2)), ALU.mult))
                assert n[0] == STEPS
                for corner in range(4):
                    dy, dx = divmod(corner, 2)
                    dve.tensor_tensor(weight[:, corner, :, :], hat[:, dy, :, 0:K2], hat[:, dx, :, K2:18], ALU.mult)

            def indices(h, first):
                m = [0]

                def link(ins):
                    m[0] += 1
                    ins.then_inc(index_step, 1)
                    dve.wait_ge(index_step, h * 2 + m[0])

                link(dve.tensor_tensor(flat[:, :, :], flat[:, :, :], base[:, :, K2:18], ALU.add))
                link(dve.tensor_tensor(flat[:, :, :], flat[:, :, :], image[:, :, :], ALU.add))
                for corner in range(4):
                    dy, dx = divmod(corner, 2)
                    ins = dve.tensor_scalar(index[:, corner, :, :], flat[:, :, :], float(dy * W + dx), None, ALU.add)
                ins.then_inc(index_ready, 1)

            def row_of(h, first):
                if not first:
                    dve.wait_ge(near_used, h * K2)
                positions(h, first)
                indices(h, first)
                for t in range(K2):
                    dve.wait_ge(gathered[t % 3], h * (3 * 256) + (t // 3 + 1) * 256)
                    for corner in range(4):
                        ins = dve.tensor_tensor(prod[:, corner, :, :], near[t % 3][:, corner, :, :],
                                                weight[:, corner, :, t:t + 1].to_broadcast((P, GI, C)), ALU.mult)
                    ins.then_inc(near_used, 1)
                    dve.wait_ge(near_used, h * K2 + (t + 1))
                    dve.tensor_tensor(half[:, :, :].rearrange("p s (b c) -> p s b c", b=GI), prod[:, 0:2, :, :], prod[:, 2:4, :, :],
                                      ALU.add).then_inc(half_ready, 1)
                    dve.wait_ge(half_ready, h * K2 + (t + 1))
                    if t == 0 and not first:
                        dve.wait_ge(turned, h * K2)
                    elif t >= 2 or not first:
                        dve.wait_ge(turned, h * K2 + (t - 1))
                    dve.tensor_tensor(samp[t % 2][:, :], half[:, 0, :], half[:, 1, :], ALU.add).then_inc(samp_ready, 1)
                dve.wait_ge(w_done, h * K2 + K2)
                dve.wait_ge(x3_loaded, h * 16 + 16)
                if not first:
                    dve.wait_ge(stored, h * 16)
                dve.scalar_tensor_tensor(ob[:, :], p_o[:, 0:W], k.vec('L3_conv_bias'), xr[:, :], ALU.add, ALU.add).then_inc(ob_ready, 1)

            rows(dve, row_of)

        @block.tensor
        def _(pe):
            def row_of(h, first):
                for t in range(K2):
                    pe.wait_ge(samp_ready, h * K2 + (t + 1))
                    if t == 0 and not first:
                        pe.wait_ge(tk_ready, h * K2)
                    elif t >= 2 or not first:
                        pe.wait_ge(tk_ready, h * K2 + (t - 1))
                    pe.transpose(p_t[t % 2][:, 0:P], samp[t % 2][:, :], k.ident).then_inc(turned, 1)
                    pe.wait_ge(tk_ready, h * K2 + (t + 1))
                    if t == 0 and not first:
                        pe.wait_ge(ob_ready, h)
                    pe.matmul(p_o[:, 0:W], k.w_dcn[:, t, :], tk[t % 2][:, :], start=(t == 0), stop=(t == K2 - 1)).then_inc(w_done, 1)

            rows(pe, row_of)

        @block.scalar
        def _(act):
            def row_of(h, first):
                for t in range(K2):
                    act.wait_ge(turned, h * K2 + (t + 1))
                    if t == 0 and not first:
                        act.wait_ge(w_done, h * K2)
                    elif t >= 2 or not first:
                        act.wait_ge(w_done, h * K2 + (t - 1))
                    act.activation(tk[t % 2][:, :], p_t[t % 2][:, 0:P], ACT.Copy).then_inc(tk_ready, 1)

            rows(act, row_of)


def dcn_dense(nc, k, xn, offs, x3, out, g):
    x3_v, out_v = (t.rearrange("(g b) c h w -> g (b c) h w", g=NG)[g] for t in (x3, out))
    UR = BANK // W
    NU = H // UR
    K2 = 9
    HB = UR * GI
    TQ = P // C
    STEPS = [None] + [(t, r) for r in range(0, UR, 2) for t in range(0, K2 - 1, TQ)]
    NS = len(STEPS)
    D0, S0, X0 = 0, 3 * (UR + 1), 3 * (UR + 1) + 2 * UR
    NT = X0 + UR
    GROUPS = [(i, min(4, NT - i)) for i in range(0, NT, 4)]
    NG_ = len(GROUPS)
    TURN_IN = [[], [0, 1], [2, 3], [4, 5], [6]]
    assert sum(TURN_IN, []) == list(range(NG_)) and len(TURN_IN) == NS
    SOURCE = [S0 + UR, S0, D0 + 1, D0 + UR + 2, D0 + 2 * UR + 3, D0, D0 + UR + 1, D0 + 2 * UR + 2]
    PAIR_P, SINGLES_P = [(2,), (0, 1)], [(0,), (1,), (2,)]
    ON_POOL = [PAIR_P, PAIR_P, SINGLES_P, PAIR_P, SINGLES_P]
    ON_DVE = [[(5,), (3, 4), (6,), (7,)]] * NS
    first_v, first_p = ([sum(len(x) for x in y[:st]) for st in range(NS + 1)] for y in (ON_DVE, ON_POOL))
    pairs_v0, pairs_p0 = ([sum(pairs_in(x) for x in y[:st]) for st in range(NS + 1)] for y in (ON_DVE, ON_POOL))
    NV, NP_, PAIRS_V, PAIRS_P = first_v[NS], first_p[NS], pairs_v0[NS], pairs_p0[NS]
    X_WITH = next(ON_POOL[0][m][0] for m, n in schedule(ON_POOL[0])[1].items() if n == 0)
    RV, RP = 5, 4
    assert 2 * NV % RV == 0 and 2 * NP_ % RP == 0 and NS % 2 == 1
    with ExitStack() as ctx:
        s = Space(nc, ctx, f"dense{g}")
        drow = s.sb("drow", [P, UR + 1, W + 2])
        dcol = s.sb("dcol", [P, UR, W + 1])
        mid = s.sb("mid", [P, UR, W])
        xw = [s.sb(f"xw{i}", [P, NT, P]) for i in range(2)]
        off = [s.sb(f"off{i}", [P, UR, OFFS]) for i in range(2)]
        hats = s.sb("hats", [P, 3, HB, 18])
        minus_mod = s.sb("minus_mod", [P, HB])
        modt = [s.sb(f"modt{i}", [P, HB]) for i in range(2)]
        edge = [s.sb(f"edge{i}", [P, 2, HB, 18]) for i in range(2)]
        corner = [s.sb(f"corner{i}", [P, 6, HB, K2]) for i in range(2)]
        prod_v = [s.sb(f"prod_v{i}", [P, UR * 2 * P]) for i in range(RV)]
        prod_p = [s.sb(f"prod_p{i}", [P, UR * 2 * P]) for i in range(RP)]
        more_v = [s.sb(f"more_v{i}", [P, UR * 2 * P]) for i in range(1)]
        more_p = [s.sb(f"more_p{i}", [P, UR * 2 * P]) for i in range(1)]
        tk = [s.sb(f"tk{i}", [P, 2 * BANK]) for i in range(2)]
        xr = [s.sb(f"x3{i}", [P, BANK]) for i in range(2)]
        w_stack = s.sb("w_stack", [P, (K2 - 1) // TQ, C])
        w_sum = s.sb("w_sum", [P, P])
        p_w = [s.ps(f"w{i}") for i in range(2)]
        p_t = [s.ps(f"t{i}", [P, 2 * BANK]) for i in range(2)]
        p_o = [s.ps(f"o{i}") for i in range(2)]
        off_in = [s.sem(f"off_in{i}") for i in range(2)]
        x3_in = [s.sem(f"x3_in{i}") for i in range(2)]
        stored = [s.sem(f"stored{i}") for i in range(2)]
        w_ready = s.sem("w_ready")
        drow_ready = s.sem("drow_ready")
        dcol_ready = s.sem("dcol_ready")
        mid_ready = s.sem("mid_ready")
        abs_ready = s.sem("abs_ready")
        hats_ready = s.sem("hats_ready")
        edge_ready = s.sem("edge_ready")
        weights_ready = s.sem("weights_ready")
        turned = s.sem("turned")
        xw_copied = s.sem("xw_copied")
        v_pair = s.sem("v_pair")
        p_pair = s.sem("p_pair")
        v_ready = s.sem("v_ready")
        v_used = s.sem("v_used")
        p_ready = s.sem("p_ready")
        p_used = s.sem("p_used")
        t_copied = s.sem("t_copied")
        w_done = s.sem("w_done")
        out_done = s.sem("out_done")
        block = ctx.enter_context(nc.Block())

        @block.sync
        def _(sp):
            def load(u, slot):
                sp.dma_start(off[slot][:, :, :], offs[bass.ds(u * UR, UR), :, :].rearrange("h w f -> w h f")).then_inc(off_in[slot], 16)

            load(0, 0)

            def unit(u, slot, first, last):
                if not last:
                    if not (first and slot == 0):
                        sp.wait_ge(weights_ready, u)
                    load(u + 1, 1 - slot)
                if not first:
                    sp.wait_ge(stored[slot], turn(u) * 16)
                sp.dma_start(xr[slot][:, :], x3_v[:, bass.ds(u * UR, UR), :].rearrange("p h w -> p (h w)")).then_inc(x3_in[slot], 16)
                if not (first and slot == 0):
                    store(u - 1, 1 - slot)

            def store(u, slot):
                sp.wait_ge(out_done, u + 1)
                sp.dma_start(out_v[:, bass.ds(u * UR, UR), :].rearrange("p h w -> p (h w)"), xr[slot][:, :]).then_inc(stored[slot], 16)

            in_pairs_last(sp, NU, unit)
            store(NU - 1, 1)
            for slot in range(2):
                sp.wait_ge(stored[slot], 16 * (NU // 2))

        @block.scalar
        def _(act):
            def stage(u):
                act.activation(mid[:, :, :], xn[:, bass.ds(u * UR + PAD, UR), PAD:PAD + W], ACT.Copy).then_inc(mid_ready, 1)

            def make_hats(u, slot):
                act.wait_ge(off_in[slot], turn(u) * 16 + 16)
                o = off[slot][:, :, 0:GI * 18]
                h = [hats[:, i, :, :].rearrange("p (h b) o -> p h (b o)", b=GI) for i in range(3)]
                act.activation(h[1], o, ACT.Abs).then_inc(abs_ready, 1)
                act.activation(h[0], o, ACT.Relu, scale=-1.0)
                act.activation(h[2], o, ACT.Relu)
                for m, scale in ((modt[slot], 1.0), (minus_mod, -1.0)):
                    act.activation(m[:, :].rearrange("p (h b) -> p h b", b=GI), off[slot][:, :, GI * 18:OFFS], ACT.Copy, scale=scale)
                act.wait_ge(abs_ready, u + 1)
                act.activation(h[1], h[1], ACT.Copy, bias=1.0, scale=-1.0).then_inc(hats_ready, 1)

            def copy_rows(u, slot, i):
                act.wait_ge(turned, u * NG_ + (i + 1))
                r0, nr = GROUPS[i]
                act.activation(xw[slot][:, r0:r0 + nr, :].rearrange("p r c -> p (r c)"), p_w[(slot * NG_ + i) % 2][:, 0:nr * P],
                               ACT.Copy).then_inc(xw_copied, 1)

            stage(0)
            make_hats(0, 0)
            for i in range(NG_):
                copy_rows(0, 0, i)

            def unit(u, slot, first, last):
                fresh = first and slot == 0
                if not last:
                    act.wait_ge(turned, u * NG_ + NG_)
                    stage(u + 1)
                for st in range(NS):
                    if not last:
                        if st == 1 and not fresh:
                            act.wait_ge(v_ready, u * NV)
                            act.wait_ge(p_ready, u * NP_)
                        for i in TURN_IN[st]:
                            copy_rows(u + 1, 1 - slot, i)
                    act.wait_ge(v_used, u * NV + first_v[st + 1])
                    act.wait_ge(p_used, u * NP_ + first_p[st + 1])
                    if not (fresh and st < 2):
                        act.wait_ge(w_done, u * NS + (st - 1))
                    ts = (slot + st) % 2
                    act.activation(tk[ts][:, :], p_t[ts][:, :], ACT.Copy).then_inc(t_copied, 1)
                    if st == 0 and not last:
                        act.wait_ge(weights_ready, u + 1)
                        if not fresh:
                            act.wait_ge(p_ready, u * NP_)
                        make_hats(u + 1, 1 - slot)

            in_pairs_last(act, NU, unit)

        @block.tensor
        def _(pe):
            def source(i):
                if i < S0:
                    dx, row = divmod(i, UR + 1)
                    return drow[:, row, dx:dx + W]
                if i < X0:
                    side, row = divmod(i - S0, UR)
                    return dcol[:, row, side:side + W]
                return mid[:, i - X0, :]

            def turn_rows(u, slot, i, first):
                r0, nr = GROUPS[i]
                if i == 0:
                    pe.wait_ge(drow_ready, u + 1)
                if r0 <= S0 < r0 + nr:
                    pe.wait_ge(dcol_ready, u + 1)
                if r0 <= X0 < r0 + nr:
                    pe.wait_ge(mid_ready, u + 1)
                if not (first and i < 2):
                    pe.wait_ge(xw_copied, u * NG_ + (i - 1))
                for r in range(nr):
                    ins = pe.transpose(p_w[(slot * NG_ + i) % 2][:, r * P:(r + 1) * P], source(r0 + r), k.ident)
                ins.then_inc(turned, 1)

            def turn_back(st, ts, place, at, total, with_x):
                n = UR if STEPS[st] is None else 2 * GI
                for i in range(n):
                    src = i if STEPS[st] is None else i % 2 * GI + i // 2
                    ins = pe.matmul(p_t[ts][:, i * W:(i + 1) * W], place[:, src * P:(src + 1) * P], k.ident,
                                    start=(at == 0 and i % 4 == 0), stop=(at == total - 1 and i % 4 == 3), is_transpose=True)
                if with_x:
                    for i in range(UR):
                        ins = pe.matmul(p_t[ts][:, BANK + i * W:BANK + (i + 1) * W], place[:, BANK + i * P:BANK + (i + 1) * P], k.ident,
                                        start=(i == 0), stop=(i == UR - 1), is_transpose=True)
                return ins

            def weigh(u, slot, st, ts, first):
                pe.wait_ge(t_copied, u * NS + (st + 1))
                if st == 0 and not first:
                    pe.wait_ge(out_done, u - 1)
                if STEPS[st] is None:
                    pe.matmul(p_o[slot][:, :], k.w_dcn[:, K2 - 1, :], tk[ts][:, 0:BANK], start=True, stop=False)
                    ins = pe.matmul(p_o[slot][:, :], w_sum[:, :], tk[ts][:, BANK:2 * BANK], start=False, stop=False)
                else:
                    t0, r0 = STEPS[st]
                    for b in range(GI):
                        ins = pe.matmul(p_o[slot][b * C:(b + 1) * C, r0 * W:(r0 + 2) * W], w_stack[:, t0 // TQ, :],
                                        tk[ts][:, b * 2 * W:(b + 1) * 2 * W], start=False, stop=(st == NS - 1))
                ins.then_inc(w_done, 1)

            for i in range(NG_):
                turn_rows(0, 0, i, True)
            pe.wait_ge(w_ready, 2)

            def unit(u, slot, first, last):
                fresh = first and slot == 0
                for st in range(NS):
                    ts = (slot + st) % 2
                    later = [] if last else list(TURN_IN[st])
                    if not (fresh and st < 2):
                        pe.wait_ge(t_copied, u * NS + (st - 1))
                    of_v = [(m, first_v[st], NV, prod_v, v_ready, v_used) for m in range(len(ON_DVE[st]))]
                    of_p = [(m, first_p[st], NP_, prod_p, p_ready, p_used) for m in range(len(ON_POOL[st]))]
                    for at, (m, n0, per, ring, ready, used) in enumerate(by_turns(of_v, of_p)):
                        pe.wait_ge(ready, u * per + (n0 + m + 1))
                        turn_back(st, ts, ring[(slot * per + n0 + m) % len(ring)], at, len(of_v) + len(of_p), STEPS[st] is None and used is p_used and m == 0).then_inc(used, 1)
                        if later and at % 2:
                            turn_rows(u + 1, 1 - slot, later.pop(0), False)
                    if st == 0:
                        if not fresh:
                            weigh(u - 1, 1 - slot, NS - 1, 1 - ts, False)
                    else:
                        weigh(u, slot, st - 1, 1 - ts, first)

            in_pairs_last(pe, NU, unit)
            weigh(NU - 1, 1, NS - 1, (1 + NS - 1) % 2, False)

        def factor(slot, d):
            if d < 2:
                return edge[slot][:, d, :, K2:18]
            return corner[slot][:, d - 2, :, :]

        def product_of(eng, slot, st):
            def product(d, place):
                if STEPS[st] is None:
                    if d == X_WITH:
                        eng.tensor_tensor(place[:, BANK:2 * BANK].rearrange("p (r c) -> p r c", c=C),
                                          xw[slot][:, X0:NT, :].rearrange("p r (b c) -> p (r b) c", b=GI),
                                          modt[slot][:, :].unsqueeze(2).to_broadcast((P, HB, C)), ALU.mult)
                    rows = xw[slot][:, SOURCE[d]:SOURCE[d] + UR, :].rearrange("p r (b c) -> p (r b) c", b=GI)
                    f = factor(slot, d)[:, :, K2 - 1:K2].to_broadcast((P, HB, C))
                    return eng.tensor_tensor(place[:, 0:BANK].rearrange("p (r c) -> p r c", c=C), rows, f, ALU.mult)
                t0, r0 = STEPS[st]
                rows = xw[slot][:, SOURCE[d] + r0:SOURCE[d] + r0 + 2, :].rearrange("p r (b c) -> p (r b) c", b=GI)
                rows = rows.unsqueeze(2).to_broadcast((P, 2 * GI, TQ, C))
                f = factor(slot, d)[:, r0 * GI:(r0 + 2) * GI, t0:t0 + TQ].unsqueeze(3).to_broadcast((P, 2 * GI, TQ, C))
                return eng.tensor_tensor(place[:, :].rearrange("p (r t c) -> p r t c", t=TQ, c=C), rows, f, ALU.mult)
            return product

        def part_of(st):
            return lambda place: place[:, 0:BANK] if STEPS[st] is None else place[:, :]

        @block.gpsimd
        def _(pool):
            def difference_of_rows(u):
                pool.tensor_tensor(drow[:, :, :], xn[:, bass.ds(u * UR + PAD, UR + 1), PAD - 1:PAD + W + 1],
                                   xn[:, bass.ds(u * UR + (PAD - 1), UR + 1), PAD - 1:PAD + W + 1], ALU.subtract).then_inc(drow_ready, 1)

            difference_of_rows(0)

            def unit(u, slot, first, last):
                pool.wait_ge(weights_ready, u + 1)
                pool.wait_ge(xw_copied, u * NG_ + NG_)
                for st in range(NS):
                    make_sums(pool, u, ON_POOL[st], first_p[st], NP_, slot * NP_, prod_p, more_p, p_ready, p_pair, PAIRS_P, pairs_p0[st],
                              p_used, first and slot == 0, product_of(pool, slot, st), part_of(st))
                    if st == 0 and not last:
                        difference_of_rows(u + 1)

            in_pairs_last(pool, NU, unit)

        @block.vector
        def _(dve):
            def difference_of_columns(u):
                dve.tensor_tensor(dcol[:, :, :], xn[:, bass.ds(u * UR + PAD, UR), PAD:PAD + W + 1],
                                  xn[:, bass.ds(u * UR + PAD, UR), PAD - 1:PAD + W], ALU.subtract).then_inc(dcol_ready, 1)

            def make_factors(u, slot):
                dve.wait_ge(hats_ready, u + 1)
                for i, h, mod in ((0, 2, modt[slot]), (1, 0, minus_mod)):
                    ins = dve.tensor_tensor(edge[slot][:, i, :, :], hats[:, h, :, :], mod[:, :].unsqueeze(2).to_broadcast((P, HB, 18)), ALU.mult)
                ins.then_inc(edge_ready, 1)
                dve.wait_ge(edge_ready, u + 1)
                for i in range(2):
                    ins = dve.tensor_tensor(corner[slot][:, 3 * i:3 * i + 3, :, :],
                                            edge[slot][:, i, :, 0:K2].unsqueeze(1).to_broadcast((P, 3, HB, K2)),
                                            hats[:, :, :, K2:18], ALU.mult)
                ins.then_inc(weights_ready, 1)

            def finish(u, slot):
                dve.wait_ge(w_done, u * NS + NS)
                dve.wait_ge(x3_in[slot], turn(u) * 16 + 16)
                dve.scalar_tensor_tensor(xr[slot][:, :], p_o[slot][:, :], k.vec('L3_conv_bias'), xr[slot][:, :], ALU.add,
                                         ALU.add).then_inc(out_done, 1)

            difference_of_columns(0)
            for i in range(TQ):
                r = slice(C * i, C * i + C)
                ins = dve.tensor_copy(w_stack[r, :, :], k.w_dcn[r, i:K2 - 1:TQ, r])
            ins.then_inc(w_ready, 1)
            dve.tensor_reduce(w_sum[:, :], k.w_dcn[:, :, :].rearrange("p t o -> p o t"), AX.X, ALU.add).then_inc(w_ready, 1)
            make_factors(0, 0)

            def unit(u, slot, first, last):
                fresh = first and slot == 0
                dve.wait_ge(weights_ready, u + 1)
                dve.wait_ge(xw_copied, u * NG_ + NG_)
                for st in range(NS):
                    if st == 2 and not fresh:
                        finish(u - 1, 1 - slot)
                    if st == 3 and not last:
                        if not fresh:
                            dve.wait_ge(p_ready, u * NP_)
                            dve.wait_ge(v_ready, u * NV)
                        make_factors(u + 1, 1 - slot)
                    make_sums(dve, u, ON_DVE[st], first_v[st], NV, slot * NV, prod_v, more_v, v_ready, v_pair, PAIRS_V, pairs_v0[st],
                              v_used, fresh, product_of(dve, slot, st), part_of(st))
                    if st == 0 and not last:
                        difference_of_columns(u + 1)
            in_pairs_last(dve, NU, unit)
            finish(NU - 1, 1)


def build(nc, a, out):
    x1 = nc.dram_tensor("x1", (B, C, H, W), F32).ap()
    x2 = nc.dram_tensor("x2", (B, C, H, W), F32).ap()
    x3 = nc.dram_tensor("x3", (B, C, H, W), F32).ap()
    pre = [nc.dram_tensor(f"pre{g}", (P, H, W), F32).ap() for g in range(NG)]
    offs = [nc.dram_tensor(f"offs{g}", (H, W, OFFS), F32).ap() for g in range(NG)]
    table = nc.dram_tensor("table", (GI * PX, C), F32).ap()
    with ExitStack() as ctx:
        k = Kept(nc, ctx)
        with ExitStack() as gate_ctx:
            k.for_gate(nc, gate_ctx)
            make_weights(nc, a, k)
            blur(nc, a["x"], a["L0_conv_sigma"], x1)
            for g in range(NG):
                gate_conv(nc, k, x1, g)
            gate_scale(nc, k)
        xn = ctx.enter_context(nc.sbuf_tensor("xn", [P, HP, HP], F32))
        for g in range(NG):
            residual(nc, k, x1, None, ACT.Silu, k.gate[:, g, 0:1], k.gate[:, g, 1:2], x2, xn, g)
            with nc.sbuf_tensor(f"snake_off{g}", [P, H, 32], F32) as off:
                snake_offsets(nc, k, xn, off, g)
                snake(nc, k, xn, off, pre[g], g)
            residual(nc, k, x2, pre[g], ACT.Relu, k.snake_gn[:, 0:1], k.snake_gn[:, 1:2], x3, xn, g)
            dcn_offsets(nc, k, xn, offs[g], g)
            dense = nc.values_load(k.dense[:, :], min_val=0, max_val=1)
            with nc.If(dense > 0):
                dcn_dense(nc, k, xn, offs[g], x3, out, g)
            with nc.Else():
                dcn_gather(nc, k, xn, offs[g], table, x3, out, g)


_INS = ['x', 'L0_conv_sigma', 'L1_conv_proj_weight', 'L1_conv_proj_bias', 'L1_conv_bn_gamma', 'L1_conv_bn_beta',
        'L1_conv_scale_w', 'L1_conv_scale_b', 'L2_conv_w_off', 'L2_conv_b_off', 'L2_conv_gn_off_g', 'L2_conv_gn_off_b',
        'L2_conv_w_dsc', 'L2_conv_b_dsc', 'L2_conv_gn_g', 'L2_conv_gn_b', 'L3_conv_weight', 'L3_conv_bias',
        'L3_conv_offset_w', 'L3_conv_offset_b', 'L3_conv_mod_w', 'L3_conv_mod_b']


def _constants():
    import numpy as _np

    p, f = _np.arange(P)[:, None], _np.arange(P)[None, :]
    cumulate = _np.zeros((P, 8, 4), _np.float32)
    for b in range(4):
        for slot, tap in enumerate(SNAKE_TAPS):
            for step in (range(tap, 4) if tap < 4 else range(5, tap + 1)):
                cumulate[32 * b + step, slot, b] = 1
    return _np.concatenate([p == f, (p // 2 == f // 2) / 2, (p // 4 == f // 4) / 4, (p % 32 == f % 32) / 4,
                            cumulate.reshape(P, 32)], axis=1).astype(_np.float32)


def kernel(**inputs):
    import numpy as _np
    import concourse.bacc as _bacc
    from concourse import mybir as _mybir
    from concourse.bass_utils import run_bass_kernel_spmd as _run

    nc = _bacc.Bacc("TRN2", target_bir_lowering=False, num_devices=1)
    arrays, args = {"in_const": _constants()}, {}
    for name in _INS:
        a = _np.ascontiguousarray(inputs[name])
        arrays[f"in_{name}"] = a.reshape(a.shape or (1,))
    for name, a in arrays.items():
        args[name[3:]] = nc.dram_tensor(name, a.shape, _mybir.dt.from_np(a.dtype), kind="ExternalInput").ap()
    out = nc.dram_tensor("out", (8, 32, 128, 128), _mybir.dt.float32, kind="ExternalOutput").ap()
    build(nc, args, out)
    r = _run(nc, [arrays], core_ids=[0])
    return r.results[0]["out"]
```

```python
from contextlib import ExitStack

import concourse.bass as bass
from concourse import mybir

F32 = mybir.dt.float32
I32 = mybir.dt.int32
U32 = mybir.dt.uint32
ALU = mybir.AluOpType
ACT = mybir.ActivationFunctionType
AX = mybir.AxisListType

B, C, H, W = 8, 32, 128, 128
P = 128
GI = P // C
NG = B // GI
PX = H * W
BANK = 512
GN_EPS = 1e-5


class Space:

    def __init__(self, nc, ctx, tag):
        self.nc, self.ctx, self.tag = nc, ctx, tag
        self.sems = []
        ctx.callback(self.close)

    def sb(self, name, shape, dt=F32):
        return self.ctx.enter_context(self.nc.sbuf_tensor(f"{self.tag}_{name}", shape, dt))

    def ps(self, name, shape=(P, BANK), dt=F32):
        return self.ctx.enter_context(self.nc.psum_tensor(f"{self.tag}_{name}", list(shape), dt))

    def sem(self, name):
        self.sems.append(self.nc.alloc_semaphore(f"{self.tag}_{name}"))
        return self.sems[-1]

    def close(self):
        if self.sems:
            self.nc.clear_and_free_semaphores(self.sems)
            self.nc.all_engine_barrier()


def in_pairs(eng, n, body):
    body(0, 0, True)
    body(1, 1, True)
    if n > 2:
        with eng.Fori(1, n // 2) as i:
            body(i * 2, 0, False)
            body(i * 2 + 1, 1, False)


def turn(t):
    return t // 2
SNAKE_TAPS = (3, 5, 2, 6, 1, 7, 0, 8)


def in_pairs_last(eng, n, body):
    body(0, 0, True, False)
    body(1, 1, True, False)
    with eng.Fori(1, n // 2 - 1) as i:
        body(i * 2, 0, False, False)
        body(i * 2 + 1, 1, False, False)
    body(n - 2, 0, False, False)
    body(n - 1, 1, False, True)


OFFS = GI * 18 + GI


def blur(nc, x, sigma, x1):
    NB = 16
    CH = B * C // NB
    COLS = NB * W
    Q = COLS // BANK
    SLOTS = 4
    R = 5
    K = 2 * R + 1
    x_v = x.rearrange("b c h w -> h (b c) w")
    x1_v = x1.rearrange("b c h w -> h (b c) w")

    with ExitStack() as ctx:
        s = Space(nc, ctx, "blur")
        xs = [s.sb(f"x{i}", [P, NB, W]) for i in range(SLOTS)]
        cen = [s.sb(f"centred{i}", [P, NB, W]) for i in range(2)]
        st = [s.sb(f"stats{i}", [P, NB, 6]) for i in range(2)]
        mv = [s.sb(f"mean_var{i}", [P, NB, 2]) for i in range(2)]
        mean = [s.sb(f"mean{i}", [P, NB]) for i in range(2)]
        d = s.sb("d", [P, NB])
        e = s.sb("e", [P, NB])
        std = s.sb("std", [P, NB])
        rstd = [s.sb(f"rstd{i}", [P, NB]) for i in range(2)]
        half = s.sb("half", [P, Q, BANK])
        mean_w = s.sb("mean_w", [P, P])
        band = s.sb("band", [P, P])
        dist = s.sb("dist", [P, P])
        term = s.sb("term", [P, P])
        sg = s.sb("sigma", [P, 1])
        rs = s.sb("rsigma", [P, 1])
        ax = s.sb("ax", [P, K])
        ax2 = s.sb("ax2", [P, K])
        g = s.sb("g", [P, K])
        gs = s.sb("gsum", [P, 1])
        eps = s.sb("eps", [P, 1])
        p_stat = s.ps("stat", [P, 2, 2, NB])
        p_half = [s.ps(f"half{i}") for i in range(2)]
        p_out = [s.ps(f"out{i}") for i in range(Q)]

        sigma_in = s.sem("sigma_in")
        iota_done = s.sem("iota_done")
        chain = s.sem("vector_chain")
        exp_in = s.sem("exp_in")
        exp_done = s.sem("exp_done")
        consts = s.sem("constants_ready")
        loaded = [s.sem(f"loaded{i}") for i in range(SLOTS)]
        stored = [s.sem(f"stored{i}") for i in range(SLOTS)]
        rows_measured = s.sem("rows_measured")
        aggregate_go = s.sem("aggregate_go")
        mv_ready = s.sem("mv_ready")
        mean_ready = s.sem("mean_ready")
        mean_kept = s.sem("mean_kept")
        spread_step = s.sem("spread_step")
        spread_ready = s.sem("spread_ready")
        var_ready = s.sem("var_ready")
        std_ready = s.sem("std_ready")
        rstd_ready = s.sem("rstd_ready")
        centred = s.sem("centred")
        half_ready = s.sem("half_ready")
        half_copied = s.sem("half_copied")
        out_ready = s.sem("out_ready")
        out_used = s.sem("out_used")
        x1_ready = s.sem("x1_ready")
        block = ctx.enter_context(nc.Block())

        @block.sync
        def _(sp):
            sp.dma_start(sg[:, :], bass.AP(tensor=sigma.tensor, offset=0, ap=[[0, P], [1, 1]])).then_inc(sigma_in, 16)

            def load(t, slot):
                sp.dma_start(xs[slot][:, :, :], x_v[:, bass.ds(t * NB, NB), :]).then_inc(loaded[slot], 16)

            def store(t, slot):
                sp.wait_ge(x1_ready, t + 1)
                sp.dma_start(x1_v[:, bass.ds(t * NB, NB), :], xs[slot][:, :, :]).then_inc(stored[slot], 16)

            for t in range(SLOTS):
                load(t, t)
            for t in range(CH):
                store(t, t % SLOTS)
                if t + SLOTS < CH:
                    sp.wait_ge(stored[t % SLOTS], (t // SLOTS + 1) * 16)
                    load(t + SLOTS, t % SLOTS)
            for slot in range(SLOTS):
                sp.wait_ge(stored[slot], CH // SLOTS * 16)

        def in_fours(eng, body):
            for t in range(SLOTS):
                body(t, t, t, False)
            with eng.Fori(1, CH // SLOTS - 1) as i:
                for slot in range(SLOTS):
                    body(i * SLOTS + slot, slot, SLOTS, False)
            for slot in range(SLOTS):
                body(CH - SLOTS + slot, slot, SLOTS, slot == SLOTS - 1)

        @block.gpsimd
        def _(pool):
            pool.iota(dist[:, :], pattern=[[1, P]], base=0, channel_multiplier=-1,
                      allow_small_or_imprecise_dtypes=True).then_inc(iota_done, 1)
            pool.iota(ax[:, :], pattern=[[1, K]], base=-R, channel_multiplier=0,
                      allow_small_or_imprecise_dtypes=True).then_inc(iota_done, 1)

            def centre(t, slot, before, last):
                pool.wait_ge(mean_kept, t + 1)
                if before >= 2:
                    pool.wait_ge(half_ready, (t - 1) * Q)
                pool.tensor_tensor(cen[slot % 2][:, :, :], xs[slot][:, :, :], mean[slot % 2][:, :].unsqueeze(2).to_broadcast((P, NB, W)),
                                   ALU.subtract).then_inc(centred, 1)

            in_fours(pool, centre)

        @block.scalar
        def _(act):
            act.wait_ge(exp_in, 1)
            act.activation(g[:, :], ax2[:, :], ACT.Exp, scale=-0.5).then_inc(exp_done, 1)

            def root(t, first):
                act.wait_ge(var_ready, t + 1)
                if not first:
                    act.wait_ge(rstd_ready, t)
                act.activation(std[:, :], p_stat[:, 1, 0, :], ACT.Sqrt, bias=eps[:, :]).then_inc(std_ready, 1)

            root(0, True)

            def chunk(t, slot, before, last):
                for q in range(Q):
                    act.wait_ge(half_ready, t * Q + q + 1)
                    if before >= 1:
                        act.wait_ge(out_ready, (t - 1) * Q + q + 1)
                    act.activation(half[:, q, :], p_half[q % 2][:, :], ACT.Copy).then_inc(half_copied, 1)
                if not last:
                    root(t + 1, False)

            in_fours(act, chunk)

        @block.vector
        def _(dve):
            n = [0]

            def link(ins):
                n[0] += 1
                ins.then_inc(chain, 1)
                dve.wait_ge(chain, n[0])

            dve.memset(mean_w[:, :], 1.0 / H)
            dve.memset(eps[:, :], GN_EPS)
            dve.wait_ge(sigma_in, 16)
            link(dve.tensor_scalar(rs[:, :], sg[:, :], -1.0, None, ALU.mult))
            link(dve.tensor_tensor(rs[:, :], rs[:, :], sg[:, :], ALU.max))
            link(dve.tensor_scalar(rs[:, :], rs[:, :], 1e-6, None, ALU.add))
            link(dve.reciprocal(rs[:, :], rs[:, :]))
            dve.wait_ge(iota_done, 2)
            link(dve.tensor_scalar(ax[:, :], ax[:, :], rs[:, :], None, ALU.mult))
            dve.tensor_tensor(ax2[:, :], ax[:, :], ax[:, :], ALU.mult).then_inc(exp_in, 1)
            dve.wait_ge(exp_done, 1)
            for _ in range(2):
                link(dve.tensor_reduce(gs[:, :], g[:, :], AX.X, ALU.add))
                link(dve.reciprocal(gs[:, :], gs[:, :]))
                link(dve.tensor_scalar(g[:, :], g[:, :], gs[:, :], None, ALU.mult))
            link(dve.tensor_scalar(band[:, :], dist[:, :], float(-R), g[:, 0:1], ALU.is_equal, ALU.mult))
            for k in range(1, K):
                link(dve.tensor_scalar(term[:, :], dist[:, :], float(k - R), g[:, k:k + 1], ALU.is_equal, ALU.mult))
                ins = dve.tensor_tensor(band[:, :], band[:, :], term[:, :], ALU.add)
                if k < K - 1:
                    link(ins)
            ins.then_inc(consts, 1)

            def measure(t, slot, before):
                dve.wait_ge(loaded[slot], (t // SLOTS) * 16 + 16)
                for n in range(NB):
                    ins = dve.bn_stats(st[slot % 2][:, n, :], xs[slot][:, n, :])
                ins.then_inc(rows_measured, 1)
                dve.wait_ge(rows_measured, t + 1)
                dve.sem_inc(aggregate_go, 1)
                for n in range(NB):
                    ins = dve.bn_aggr(mv[slot % 2][:, n, :], st[slot % 2][:, n, :])
                ins.then_inc(mv_ready, 1)

            def spread(t, slot, before):
                dve.wait_ge(mean_ready, t + 1)
                if before >= 2:
                    dve.wait_ge(centred, t - 1)
                dve.tensor_copy(mean[slot % 2][:, :], p_stat[:, 0, slot % 2, :]).then_inc(mean_kept, 1)
                dve.wait_ge(mean_kept, t + 1)
                dve.wait_ge(mv_ready, t + 1)
                dve.tensor_tensor(d[:, :], mv[slot % 2][:, :, 0], mean[slot % 2][:, :], ALU.subtract).then_inc(spread_step, 1)
                dve.wait_ge(spread_step, t * 2 + 1)
                dve.tensor_tensor(d[:, :], d[:, :], d[:, :], ALU.mult).then_inc(spread_step, 1)
                dve.wait_ge(spread_step, t * 2 + 2)
                if before >= 1:
                    dve.wait_ge(var_ready, t)
                dve.tensor_tensor(e[:, :], d[:, :], mv[slot % 2][:, :, 1], ALU.add).then_inc(spread_ready, 1)

            def invert(t, slot):
                dve.wait_ge(std_ready, t + 1)
                dve.reciprocal(rstd[slot % 2][:, :], std[:, :]).then_inc(rstd_ready, 1)

            def finish(t, slot):
                dve.wait_ge(rstd_ready, t + 1)
                for q in range(Q):
                    dve.wait_ge(out_ready, t * Q + q + 1)
                    for j in range(4):
                        n = 4 * q + j
                        ins = dve.scalar_tensor_tensor(xs[slot][:, n, :], p_out[q][:, j * W:(j + 1) * W], rstd[slot % 2][:, n:n + 1],
                                                       xs[slot][:, n, :], ALU.mult, ALU.add)
                    ins.then_inc(out_used, 1)
                dve.wait_ge(out_used, t * Q + Q)
                dve.sem_inc(x1_ready, 1)

            measure(0, 0, 0)
            spread(0, 0, 0)
            invert(0, 0)

            def chunk(t, slot, before, last):
                if not last:
                    measure(t + 1, (slot + 1) % SLOTS, before + 1)
                    spread(t + 1, (slot + 1) % SLOTS, before + 1)
                finish(t, slot)
                if not last:
                    invert(t + 1, (slot + 1) % SLOTS)

            in_fours(dve, chunk)

        @block.tensor
        def _(pe):
            pe.wait_ge(consts, 1)

            def row_mean(t, slot):
                pe.wait_ge(mv_ready, t + 1)
                pe.matmul(p_stat[:, 0, slot % 2, :], mean_w[:, :], mv[slot % 2][:, :, 0], start=True, stop=True).then_inc(mean_ready, 1)

            def row_spread(t, first):
                pe.wait_ge(spread_ready, t + 1)
                if not first:
                    pe.wait_ge(std_ready, t)
                pe.matmul(p_stat[:, 1, 0, :], mean_w[:, :], e[:, :], start=True, stop=True).then_inc(var_ready, 1)

            row_mean(0, 0)
            row_spread(0, True)

            def chunk(t, slot, before, last):
                def along_h(q):
                    if not (before == 0 and q < 2):
                        pe.wait_ge(half_copied, t * Q + q - 1)
                    for j in range(4):
                        ins = pe.matmul(p_half[q % 2][:, j * W:(j + 1) * W], cen[slot % 2][:, q * 4 + j, :], band[:, :],
                                        start=True, stop=True)
                    ins.then_inc(half_ready, 1)

                def along_w(q):
                    pe.wait_ge(half_copied, t * Q + q + 1)
                    if before >= 1:
                        pe.wait_ge(out_used, (t - 1) * Q + q + 1)
                    for j in range(4):
                        ins = pe.matmul(p_out[q][:, j * W:(j + 1) * W], half[:, q, j * W:(j + 1) * W], band[:, :],
                                        start=True, stop=True)
                    ins.then_inc(out_ready, 1)

                pe.wait_ge(centred, t + 1)
                along_h(0)
                for q in range(1, Q):
                    along_h(q)
                    along_w(q - 1)
                    if not last and q == 2:
                        row_mean(t + 1, slot + 1)
                if not last:
                    row_spread(t + 1, False)
                along_w(Q - 1)

            in_fours(pe, chunk)


class Kept:

    VECTORS = ['L1_conv_proj_bias', 'L1_conv_bn_gamma', 'L1_conv_bn_beta', 'L1_conv_scale_b', 'L2_conv_b_off',
               'L2_conv_gn_off_g', 'L2_conv_gn_off_b', 'L2_conv_b_dsc', 'L2_conv_gn_g', 'L2_conv_gn_b', 'L3_conv_bias']
    N_PAR = len(VECTORS) + 1

    def __init__(self, nc, ctx):
        s = Space(nc, ctx, "kept")
        self.const = s.sb("const", [P, 4 * P + 32])
        self.ident = self.const[:, 0:P]
        self.pair_mean = self.const[:, P:2 * P]
        self.quad_mean = self.const[:, 2 * P:3 * P]
        self.image_mean = self.const[:, 3 * P:4 * P]
        self.cumulate = self.const[:, 4 * P:4 * P + 32]
        self.par = s.sb("par", [P, self.N_PAR])
        self.w_off2 = s.sb("w_off2", [P, 3, 2 * C])
        self.w_dsc = s.sb("w_dsc", [P, 9, P])
        self.w_off3 = s.sb("w_off3", [P, 3, 2 * C])
        self.w_dcn = s.sb("w_dcn", [P, 9, P])
        self.eps = s.sb("eps", [P, 1])
        self.norm1 = s.sb("norm1", [P, NG, 2])
        self.hidden = s.sb("hidden", [P, NG, 2])
        self.gate = s.sb("gate", [P, NG, 2])
        self.dense = s.sb("dense", [1, 1], I32)
        self.snake_gn = s.sb("snake_gn", [P, 2])

    def for_gate(self, nc, ctx):
        s = Space(nc, ctx, "kept_gate")
        self.w_gate = s.sb("w_gate", [P, 3, 2 * C])
        self.w_scale = s.sb("w_scale", [P, 1, P])

    def vec(self, name):
        i = self.VECTORS.index(name)
        return self.par[:, i:i + 1]

    @property
    def bias3(self):
        return self.par[:, self.N_PAR - 1:self.N_PAR]


def make_weights(nc, a, k):
    with ExitStack() as ctx:
        s = Space(nc, ctx, "weights")
        diag = [s.sb(f"diag{i}", [P, 9, P]) for i in range(3)]
        jobs = [(diag[0], [('L1_conv_proj_weight', 0, 32)], 9), (k.w_scale, [('L1_conv_scale_w', 0, 32)], 1),
                (diag[1], [('L2_conv_w_off', 0, 18)], 9), (k.w_dsc, [('L2_conv_w_dsc', 0, 32)], 9),
                (diag[2], [('L3_conv_offset_w', 0, 18), ('L3_conv_mod_w', 18, 9)], 9), (k.w_dcn, [('L3_conv_weight', 0, 32)], 9)]
        nat = [s.sb(f"nat{n}", [P, C, j[2]]) for n, j in enumerate(jobs)]
        big = [s.sb(f"big{n}", [P, j[2], P]) for n, j in enumerate(jobs)]
        rows = s.sb("rows", [k.N_PAR, GI, 32])
        tr = [s.ps(f"tr{i}") for i in range(4)]
        cleared = s.sem("cleared")
        const_in = s.sem("const_in")
        rows_in = s.sem("rows_in")
        nat_in = s.sem("nat_in")
        blocks = s.sem("blocks")
        turned = s.sem("turned")
        copied = s.sem("copied")
        turns = [(n, t0, min(4, j[2] - t0)) for n, j in enumerate(jobs) for t0 in range(0, j[2], 4)]
        block = ctx.enter_context(nc.Block())

        @block.gpsimd
        def _(pool):
            pool.memset(rows[:, :, :], 0.0).then_inc(cleared, 1)
            for n in range(len(jobs)):
                pool.memset(nat[n][:, :, :], 0.0).then_inc(cleared, 1)

        @block.sync
        def _(sp):
            sp.dma_start(k.const[:, :], a["const"]).then_inc(const_in, 16)
            sp.wait_ge(cleared, 1)
            for i, name in enumerate(k.VECTORS + ['L3_conv_offset_b']):
                n = a[name].shape[0]
                sp.dma_start(rows[i:i + 1, :, 0:n], bass.AP(tensor=a[name].tensor, offset=0, ap=[[0, 1], [0, GI], [1, n]])).then_inc(rows_in, 16)
            sp.dma_start(rows[k.N_PAR - 1:k.N_PAR, :, 18:27],
                         bass.AP(tensor=a['L3_conv_mod_b'].tensor, offset=0, ap=[[0, 1], [0, GI], [1, 9]])).then_inc(rows_in, 16)
            sp.wait_ge(cleared, 1 + len(jobs))
            for n, (_, parts, taps) in enumerate(jobs):
                for name, o0, no in parts:
                    src = bass.AP(tensor=a[name].tensor, offset=0, ap=[[C * taps, no], [1, C * taps]])
                    for b in range(GI):
                        sp.dma_start(nat[n][32 * b + o0:32 * b + o0 + no, :, :].rearrange("p c t -> p (c t)"), src).then_inc(nat_in, 16)

        @block.vector
        def _(dve):
            dve.memset(k.eps[:, :], GN_EPS)
            for w in (k.w_gate, k.w_off2, k.w_off3):
                dve.memset(w[:, :, :], 0.0)
            for n in range(len(jobs)):
                ins = dve.memset(big[n][:, :, :], 0.0)
            ins.then_inc(blocks, 1)
            dve.wait_ge(blocks, 1)
            dve.wait_ge(nat_in, 16 * GI * sum(len(j[1]) for j in jobs))
            for n in range(len(jobs)):
                for b in range(GI):
                    r = slice(32 * b, 32 * b + 32)
                    ins = dve.tensor_copy(big[n][r, :, r], nat[n][r, :, :].rearrange("p c t -> p t c"))
            ins.then_inc(blocks, 1)
            dve.wait_ge(copied, 1 + len(turns))
            for w, of in zip((k.w_gate, k.w_off2, k.w_off3), diag):
                for q in range(GI):
                    for out_row in range(2):
                        dy = q - out_row
                        if 0 <= dy <= 2:
                            r = slice(C * q, C * q + C)
                            dve.tensor_copy(w[r, :, C * out_row:C * out_row + C], of[r, 3 * dy:3 * dy + 3, r])

        @block.tensor
        def _(pe):
            pe.wait_ge(const_in, 16)
            pe.wait_ge(rows_in, 16 * (k.N_PAR + 1))
            pe.transpose(tr[0][:, 0:k.N_PAR], rows[:, :, :].rearrange("v b o -> v (b o)"), k.ident[0:k.N_PAR, 0:k.N_PAR]).then_inc(turned, 1)
            pe.wait_ge(blocks, 2)
            for i, (n, t0, nt) in enumerate(turns, 1):
                if i >= 4:
                    pe.wait_ge(copied, i - 3)
                for t in range(nt):
                    ins = pe.transpose(tr[i % 4][:, t * P:(t + 1) * P], big[n][:, t0 + t, :], k.ident)
                ins.then_inc(turned, 1)

        @block.scalar
        def _(act):
            act.wait_ge(turned, 1)
            act.activation(k.par[:, :], tr[0][:, 0:k.N_PAR], ACT.Copy).then_inc(copied, 1)
            for i, (n, t0, nt) in enumerate(turns, 1):
                act.wait_ge(turned, i + 1)
                act.activation(jobs[n][0][:, t0:t0 + nt, :].rearrange("p t o -> p (t o)"), tr[i % 4][:, 0:nt * P],
                               ACT.Copy).then_inc(copied, 1)


ACT_ROWS = 48
PAD = 4
HP = H + 2 * PAD


class RowConv:
    NI = H // 4
    UI = BANK // W
    NU = NI // UI
    BANKS = 4
    OF_ACT = [((0, 0), 0), ((0, 1), 2), ((0, 2), 4)]
    OF_DVE = [((0, 3), 0), ((1, 0), 1), ((1, 1), 2), ((1, 2), 3), ((1, 3), 4)]

    def __init__(self, s, xn, top, left, w):
        self.xn, self.top, self.left, self.w = xn, top, left, w
        self.rows = [[s.sb(f"{n}{i}", [P, self.NI, W + 2]) for i in range(2)] for n in ("low", "high")]
        self.acc = [s.ps(f"acc{i}") for i in range(self.BANKS)]
        self.moved_act, self.moved_dve = s.sem("moved_act"), s.sem("moved_dve")
        self.conv_done = s.sem("conv_done")

    def bank(self, b, u):
        return self.acc[(b * self.NU + u) % self.BANKS]

    def move(self, eng, copy, moved, share, b, u=None):
        for (high, q), after in share:
            if u is not None and u != after:
                continue
            if b >= 2:
                eng.wait_ge(self.conv_done, (b - 1) * self.NU)
            r0 = self.top - 1 + 2 * high + q
            copy(self.rows[high][b % 2][C * q:C * q + C, :, :],
                 self.xn[C * b:C * b + C, r0:r0 + 4 * self.NI - 3:4, self.left - 1:self.left + W + 1]).then_inc(moved, 1)

    def wait_moved(self, pe, b):
        pe.wait_ge(self.moved_act, (b + 1) * len(self.OF_ACT))
        pe.wait_ge(self.moved_dve, (b + 1) * len(self.OF_DVE))

    def convolve(self, pe, b, u):
        for dx in range(3):
            for high in range(2):
                ins = pe.matmul(self.bank(b, u)[2 * C * high:2 * C * (high + 1), :], self.w[:, dx, :],
                                self.rows[high][b % 2][:, u * self.UI:(u + 1) * self.UI, dx:dx + W], start=(dx == 0), stop=(dx == 2))
        ins.then_inc(self.conv_done, 1)


def act_copy(act):
    return lambda o, i: act.activation(o, i, ACT.Copy)


def gate_conv(nc, k, x1, g):
    x1_v = x1.rearrange("(g b) c h w -> g (b c) h w", g=NG)[g]
    LR = 16
    NL = H // LR
    UR = BANK // W
    NU = H // UR
    with ExitStack() as ctx:
        s = Space(nc, ctx, f"gateconv{g}")
        xn = s.sb("xn", [P, H + 2, W + 2])
        xg = xn[:, 1:H + 1, 1:W + 1]
        st = s.sb("stats", [P, NU, 6])
        mv = s.sb("mean_var", [P, 2])
        std = s.sb("std", [P, 1])
        conv = RowConv(s, xn, 1, 1, k.w_gate)
        hid = [s.sb(f"hid{i}", [P, BANK]) for i in range(4)]
        hst = s.sb("hid_stats", [P, GI, conv.NU, 6])
        hmv = s.sb("hid_mean_var", [P, GI, 2])
        hmean = s.sb("hid_mean", [P, GI])
        he = s.sb("hid_e", [P, GI])
        p_hid = [s.ps(f"hid_stat{i}") for i in range(2)]
        loaded = [s.sem(f"loaded{i}") for i in range(NL)]
        chain = s.sem("vector_chain")
        var_ready = s.sem("var_ready")
        std_ready = s.sem("std_ready")
        coef_ready = s.sem("coef_ready")
        normed = s.sem("normed")
        padded = s.sem("padded")
        hid_ready = s.sem("hid_ready")
        hid_used = s.sem("hid_used")
        hmv_ready = s.sem("hmv_ready")
        hmean_ready = s.sem("hmean_ready")
        he_ready = s.sem("he_ready")
        hvar_ready = s.sem("hvar_ready")
        block = ctx.enter_context(nc.Block())

        @block.sync
        def _(sp):
            for l in range(NL):
                sp.dma_start(xg[:, l * LR:(l + 1) * LR, :], x1_v[:, l * LR:(l + 1) * LR, :]).then_inc(loaded[l], 16)

        @block.vector
        def _(dve):
            n = [0]

            def link(ins):
                n[0] += 1
                ins.then_inc(chain, 1)
                dve.wait_ge(chain, n[0])

            for u in range(NU):
                if u % (LR // UR) == 0:
                    dve.wait_ge(loaded[u // (LR // UR)], 16)
                ins = dve.bn_stats(st[:, u, :], xg[:, u * UR:(u + 1) * UR, :])
            link(ins)
            dve.bn_aggr(mv[:, :], st[:, :, :].rearrange("p u s -> p (u s)")).then_inc(var_ready, 1)
            dve.wait_ge(std_ready, 1)
            link(dve.reciprocal(k.norm1[:, g, 0:1], std[:, :]))
            dve.scalar_tensor_tensor(k.norm1[:, g, 1:2], mv[:, 0:1], -1.0, k.norm1[:, g, 0:1], ALU.mult, ALU.mult).then_inc(coef_ready, 1)
            dve.wait_ge(coef_ready, 1)
            v = xg[:, ACT_ROWS:H, :]
            dve.tensor_scalar(v, v, k.norm1[:, g, 0:1], k.norm1[:, g, 1:2], ALU.mult, ALU.add).then_inc(normed, 1)
            dve.wait_ge(normed, 2)
            dve.tensor_copy(xn[:, 1:H + 1, 0:1], xn[:, 1:H + 1, W:W + 1])
            link(dve.tensor_copy(xn[:, 1:H + 1, W + 1:W + 2], xn[:, 1:H + 1, 1:2]))
            dve.tensor_copy(xn[:, 0, :], xn[:, H, :])
            dve.tensor_copy(xn[:, H + 1, :], xn[:, 1, :]).then_inc(padded, 1)

            dve.wait_ge(padded, 1)
            conv.move(dve, dve.tensor_copy, conv.moved_dve, conv.OF_DVE, 0)
            for b in range(GI):
                for u in range(conv.NU):
                    v = b * conv.NU + u
                    dve.wait_ge(hid_ready, v + 1)
                    dve.bn_stats(hst[:, b, u, :], hid[v % 4][:, :]).then_inc(hid_used, 1)
                    if b + 1 < GI:
                        conv.move(dve, dve.tensor_copy, conv.moved_dve, conv.OF_DVE, b + 1, u)
            dve.wait_ge(hid_used, GI * conv.NU)
            for b in range(GI):
                ins = dve.bn_aggr(hmv[:, b, :], hst[:, b, :, :].rearrange("p u s -> p (u s)"))
            ins.then_inc(hmv_ready, 1)
            dve.wait_ge(hmv_ready, 1)
            dve.wait_ge(hmean_ready, 1)
            link(dve.tensor_copy(hmean[:, :], p_hid[0][:, 0:GI]))
            link(dve.tensor_tensor(he[:, :], hmv[:, :, 0], hmean[:, :], ALU.subtract))
            link(dve.tensor_tensor(he[:, :], he[:, :], he[:, :], ALU.mult))
            dve.tensor_tensor(he[:, :], he[:, :], hmv[:, :, 1], ALU.add).then_inc(he_ready, 1)
            dve.wait_ge(hvar_ready, 1)
            for b in range(GI):
                r = slice(C * b, C * b + C)
                dve.tensor_copy(k.hidden[r, g, 0:1], hmean[r, b:b + 1])
                dve.tensor_copy(k.hidden[r, g, 1:2], p_hid[1][r, b:b + 1])

        @block.scalar
        def _(act):
            act.wait_ge(var_ready, 1)
            act.activation(std[:, :], mv[:, 1:2], ACT.Sqrt, bias=k.eps[:, :]).then_inc(std_ready, 1)
            act.wait_ge(coef_ready, 1)
            v = xg[:, 0:ACT_ROWS, :]
            act.activation(v, v, ACT.Identity, bias=k.norm1[:, g, 1:2], scale=k.norm1[:, g, 0:1]).then_inc(normed, 1)

            act.wait_ge(padded, 1)
            conv.move(act, act_copy(act), conv.moved_act, conv.OF_ACT, 0)
            for b in range(GI):
                for u in range(conv.NU):
                    v = b * conv.NU + u
                    act.wait_ge(conv.conv_done, v + 1)
                    if v >= 4:
                        act.wait_ge(hid_used, v - 3)
                    act.activation(hid[v % 4][:, :], conv.bank(b, u)[:, :], ACT.Silu, bias=k.vec('L1_conv_proj_bias')).then_inc(hid_ready, 1)
                    if b + 1 < GI:
                        conv.move(act, act_copy(act), conv.moved_act, conv.OF_ACT, b + 1, u)

        @block.tensor
        def _(pe):
            for b in range(GI):
                conv.wait_moved(pe, b)
                for u in range(conv.NU):
                    if b * conv.NU + u >= conv.BANKS:
                        pe.wait_ge(hid_ready, b * conv.NU + u - conv.BANKS + 1)
                    conv.convolve(pe, b, u)
            pe.wait_ge(hmv_ready, 1)
            pe.matmul(p_hid[0][:, 0:GI], k.image_mean, hmv[:, :, 0], start=True, stop=True).then_inc(hmean_ready, 1)
            pe.wait_ge(he_ready, 1)
            pe.matmul(p_hid[1][:, 0:GI], k.image_mean, he[:, :], start=True, stop=True).then_inc(hvar_ready, 1)


def gate_scale(nc, k):
    with ExitStack() as ctx:
        s = Space(nc, ctx, "gatescale")
        mu = s.sb("mu", [P, 1])
        d = s.sb("d", [P, NG])
        e = s.sb("e", [P, NG])
        std = s.sb("std", [P, 1])
        pooled = s.sb("pooled", [P, NG])
        sig = s.sb("sig", [P, NG])
        p_mean = s.ps("mean")
        p_var = s.ps("var")
        p_log = s.ps("logits")
        chain = s.sem("vector_chain")
        mean_ready = s.sem("mean_ready")
        spread_in = s.sem("spread_in")
        spread_ready = s.sem("spread_ready")
        var_in = s.sem("var_in")
        std_ready = s.sem("std_ready")
        pooled_ready = s.sem("pooled_ready")
        logits_ready = s.sem("logits_ready")
        sig_ready = s.sem("sig_ready")
        block = ctx.enter_context(nc.Block())

        @block.tensor
        def _(pe):
            pe.matmul(p_mean[:, 0:NG], k.image_mean, k.hidden[:, :, 0], start=True, stop=True).then_inc(mean_ready, 1)
            pe.wait_ge(spread_in, 1)
            pe.matmul(p_var[:, 0:NG], k.image_mean, e[:, :], start=True, stop=True).then_inc(spread_ready, 1)
            pe.wait_ge(pooled_ready, 1)
            pe.matmul(p_log[:, 0:NG], k.w_scale[:, 0, :], pooled[:, :], start=True, stop=True).then_inc(logits_ready, 1)

        @block.scalar
        def _(act):
            act.wait_ge(var_in, 1)
            act.activation(std[:, :], mu[:, :], ACT.Sqrt, bias=k.eps[:, :], scale=1.0 / NG).then_inc(std_ready, 1)
            act.wait_ge(logits_ready, 1)
            act.activation(sig[:, :], p_log[:, 0:NG], ACT.Sigmoid, bias=k.vec('L1_conv_scale_b')).then_inc(sig_ready, 1)

        @block.vector
        def _(dve):
            n = [0]

            def link(ins):
                n[0] += 1
                ins.then_inc(chain, 1)
                dve.wait_ge(chain, n[0])

            dve.wait_ge(mean_ready, 1)
            link(dve.tensor_reduce(mu[:, :], p_mean[:, 0:NG], AX.X, ALU.add))
            link(dve.tensor_scalar(mu[:, :], mu[:, :], 1.0 / NG, None, ALU.mult))
            link(dve.tensor_scalar(d[:, :], k.hidden[:, :, 0], mu[:, :], None, ALU.subtract))
            link(dve.tensor_tensor(e[:, :], d[:, :], d[:, :], ALU.mult))
            dve.tensor_tensor(e[:, :], e[:, :], k.hidden[:, :, 1], ALU.add).then_inc(spread_in, 1)
            dve.wait_ge(spread_ready, 1)
            dve.tensor_reduce(mu[:, :], p_var[:, 0:NG], AX.X, ALU.add).then_inc(var_in, 1)
            dve.wait_ge(std_ready, 1)
            link(dve.reciprocal(std[:, :], std[:, :]))
            link(dve.tensor_tensor(std[:, :], std[:, :], k.vec('L1_conv_bn_gamma'), ALU.mult))
            dve.tensor_scalar(pooled[:, :], d[:, :], std[:, :], k.vec('L1_conv_bn_beta'), ALU.mult, ALU.add).then_inc(pooled_ready, 1)
            dve.wait_ge(sig_ready, 1)
            link(dve.tensor_scalar(sig[:, :], sig[:, :], 0.1, None, ALU.add))
            dve.tensor_tensor(k.gate[:, :, :], k.norm1[:, :, :], sig[:, :].unsqueeze(2).to_broadcast((P, NG, 2)), ALU.mult)


def residual(nc, k, base, inner, func, scale, bias, result, xn, g):
    base_v, result_v = (t.rearrange("(g b) c h w -> g (b c) h w", g=NG)[g] for t in (base, result))
    UR = 8
    NU = H // UR
    HALF = UR // 2
    with ExitStack() as ctx:
        s = Space(nc, ctx, f"residual{g}{func.name}")
        xg = s.sb("x", [P, H, W])
        act_out = [s.sb(f"act{i}", [P, UR, W]) for i in range(2)]
        st = s.sb("stats", [P, 2 * NU, 6])
        mv = s.sb("mean_var", [P, 2])
        std = s.sb("std", [P, 1])
        coef = s.sb("coef", [P, 2])
        loaded = [s.sem(f"loaded{i}") for i in range(NU)]
        inner_loaded = [s.sem(f"inner_loaded{i}") for i in range(2)]
        chain = s.sem("vector_chain")
        act_ready = s.sem("act_ready")
        sum_ready = s.sem("sum_ready")
        stored = s.sem("stored")
        var_ready = s.sem("var_ready")
        std_ready = s.sem("std_ready")
        coef_ready = s.sem("coef_ready")
        block = ctx.enter_context(nc.Block())

        @block.sync
        def _(sp):
            for u in range(NU):
                if inner is not None:
                    if u >= 2:
                        sp.wait_ge(sum_ready, u - 1)
                    sp.dma_start(act_out[u % 2][:, :, :], inner[:, u * UR:(u + 1) * UR, :]).then_inc(inner_loaded[u % 2], 16)
                sp.dma_start(xg[:, u * UR:(u + 1) * UR, :], base_v[:, u * UR:(u + 1) * UR, :]).then_inc(loaded[u], 16)

        @block.gpsimd
        def _(pool):
            for r in (PAD - 1, PAD + H):
                pool.memset(xn[:, r, PAD - 1:PAD + W + 1], 0.0)
            for c in (PAD - 1, PAD + W):
                pool.memset(xn[:, PAD:PAD + H, c:c + 1], 0.0)
            for u in range(NU):
                pool.wait_ge(sum_ready, u + 1)
                pool.dma_start(result_v[:, u * UR:(u + 1) * UR, :], xg[:, u * UR:(u + 1) * UR, :]).then_inc(stored, 16)
            pool.wait_ge(stored, 16 * NU)

        @block.scalar
        def _(act):
            for u in range(NU):
                if inner is not None:
                    act.wait_ge(inner_loaded[u % 2], 16 * (u // 2 + 1))
                    src = act_out[u % 2][:, :, :]
                else:
                    act.wait_ge(loaded[u], 16)
                    if u >= 2:
                        act.wait_ge(sum_ready, u - 1)
                    src = xg[:, u * UR:(u + 1) * UR, :]
                act.activation(act_out[u % 2][:, :, :], src, func, bias=bias, scale=scale).then_inc(act_ready, 1)
            act.wait_ge(var_ready, 1)
            act.activation(std[:, :], mv[:, 1:2], ACT.Sqrt, bias=k.eps[:, :]).then_inc(std_ready, 1)
            act.wait_ge(coef_ready, 1)
            act.activation(xn[:, PAD:PAD + ACT_ROWS, PAD:PAD + W], xg[:, 0:ACT_ROWS, :], ACT.Identity, bias=coef[:, 1:2], scale=coef[:, 0:1])

        @block.vector
        def _(dve):
            n = [0]

            def link(ins):
                n[0] += 1
                ins.then_inc(chain, 1)
                dve.wait_ge(chain, n[0])

            for u in range(NU):
                dve.wait_ge(loaded[u], 16)
                dve.wait_ge(act_ready, u + 1)
                v = xg[:, u * UR:(u + 1) * UR, :]
                dve.tensor_tensor(v, v, act_out[u % 2][:, :, :], ALU.add).then_inc(sum_ready, 1)
                dve.wait_ge(sum_ready, u + 1)
                for i in range(2):
                    ins = dve.bn_stats(st[:, 2 * u + i, :], xg[:, u * UR + i * HALF:u * UR + (i + 1) * HALF, :].rearrange("p h w -> p (h w)"))
            link(ins)
            dve.bn_aggr(mv[:, :], st[:, :, :].rearrange("p u s -> p (u s)")).then_inc(var_ready, 1)
            dve.wait_ge(std_ready, 1)
            link(dve.reciprocal(coef[:, 0:1], std[:, :]))
            dve.scalar_tensor_tensor(coef[:, 1:2], mv[:, 0:1], -1.0, coef[:, 0:1], ALU.mult, ALU.mult).then_inc(coef_ready, 1)
            dve.wait_ge(coef_ready, 1)
            dve.tensor_scalar(xn[:, PAD + ACT_ROWS:PAD + H, PAD:PAD + W], xg[:, ACT_ROWS:H, :], coef[:, 0:1], coef[:, 1:2], ALU.mult, ALU.add)


def schedule(groups):
    steps, ready, late = [], {}, None
    for m, terms in enumerate(groups):
        for i, term in enumerate(terms):
            steps.append((True, m, i, term))
            if len(terms) == 1:
                ready[m] = len(ready)
            if late is not None:
                steps.append((False, late, 0, None))
                ready[late] = len(ready)
                late = None
        if len(terms) == 2:
            late = m
    if late is not None:
        steps.append((False, late, 0, None))
        ready[late] = len(ready)
    return steps, ready


def make_sums(eng, u, groups, n0, per, shift, ring, more, ready, pair, pairs, pairs0, used, fresh, product, part, between=None):
    steps, number = schedule(groups)
    p0 = made = 0
    for at, (is_product, m, i, term) in enumerate(steps):
        if between is not None and at == (3 * len(steps) + 3) // 4:
            between()
            between = None
        N = n0 + number[m]
        place = ring[(shift + N) % len(ring)]
        if not is_product:
            eng.wait_ge(pair, u * pairs + (pairs0 + p0))
            ins = eng.tensor_tensor(part(place), part(place), part(more[(pairs0 + p0) % len(more)]), ALU.add)
        elif i == 1:
            p0 += 1
            if len(more) == 1 and not (fresh and n0 + made == 0):
                eng.wait_ge(ready, u * per + (n0 + made))
            product(term, more[(pairs0 + p0) % len(more)]).then_inc(pair, 1)
            continue
        else:
            if not (fresh and N < len(ring)):
                eng.wait_ge(used, u * per + (N - len(ring) + 1))
            ins = product(term, place)
            if len(groups[m]) == 2:
                continue
        ins.then_inc(ready, 1)
        made += 1
    if between is not None:
        between()


def by_turns(of_v, of_p):
    spread = [((i + 1) / len(x), which, i) for which, x in enumerate((of_v, of_p)) for i in range(len(x))]
    return [(of_v, of_p)[which][i] for _, which, i in sorted(spread)]


def pairs_in(groups):
    return sum(len(m) == 2 for m in groups)


def snake_offsets(nc, k, xn, off, g):
    HALF = H // 2
    with ExitStack() as ctx:
        s = Space(nc, ctx, f"snakeoff{g}")
        conv = RowConv(s, xn, PAD, PAD, k.w_off2)
        NU = conv.NU
        raw = [s.sb(f"raw{i}", [P, conv.NI, W]) for i in range(2)]
        st = [s.sb(f"stats{i}", [P, NU, 6]) for i in range(2)]
        mv = s.sb("mean_var", [P, GI, 2])
        gm = s.sb("group_mean", [P, GI])
        d = s.sb("d", [P, GI])
        e = s.sb("e", [P, GI])
        std = s.sb("std", [P, GI])
        coef = s.sb("coef", [P, GI, 2])
        p_stat = s.ps("stat", [P, 2, GI])
        p_off = [s.ps(f"off{i}", [P, HALF, 8]) for i in range(2)]
        chain = s.sem("vector_chain")
        raw_ready = s.sem("raw_ready")
        stats_done = s.sem("stats_done")
        mean_in = s.sem("mean_in")
        mean_ready = s.sem("mean_ready")
        var_in = s.sem("var_in")
        var_ready = s.sem("var_ready")
        std_ready = s.sem("std_ready")
        coef_ready = s.sem("coef_ready")
        tanh_ready = s.sem("tanh_ready")
        sums_ready = s.sem("sums_ready")
        off_ready = s.sem("off_ready")
        block = ctx.enter_context(nc.Block())

        @block.tensor
        def _(pe):
            def mean(b):
                pe.wait_ge(mean_in, b + 1)
                pe.matmul(p_stat[:, 0, b:b + 1], k.pair_mean, mv[:, b, 0:1], start=True, stop=True).then_inc(mean_ready, 1)

            def variance(b):
                pe.wait_ge(var_in, b + 1)
                pe.matmul(p_stat[:, 1, b:b + 1], k.pair_mean, e[:, b:b + 1], start=True, stop=True).then_inc(var_ready, 1)

            def cumulate(b, half):
                pe.wait_ge(tanh_ready, 2 * b + half + 1)
                if b > 0:
                    pe.wait_ge(off_ready, 2 * (b - 1) + half + 1)
                for i in range(conv.NI // 2):
                    ins = pe.matmul(p_off[half][:, 4 * i:4 * i + 4, :].rearrange("p q s -> p (q s)"),
                                    raw[b % 2][:, half * (conv.NI // 2) + i, :], k.cumulate, start=True, stop=True)
                ins.then_inc(sums_ready, 1)

            for b in range(GI):
                conv.wait_moved(pe, b)
                for u in range(NU):
                    if b * NU + u >= conv.BANKS:
                        pe.wait_ge(raw_ready, b * NU + u - conv.BANKS + 1)
                    conv.convolve(pe, b, u)
                    if b > 0 and u in (1, 2, 4, 6):
                        (mean, variance, lambda x: cumulate(x, 0), lambda x: cumulate(x, 1))[(1, 2, 4, 6).index(u)](b - 1)
            mean(GI - 1)
            variance(GI - 1)
            cumulate(GI - 1, 0)
            cumulate(GI - 1, 1)

        @block.scalar
        def _(act):
            def root(b):
                act.wait_ge(var_ready, b + 1)
                act.activation(std[:, b:b + 1], p_stat[:, 1, b:b + 1], ACT.Sqrt, bias=k.eps[:, :]).then_inc(std_ready, 1)

            def squash(b, half):
                act.wait_ge(coef_ready, b + 1)
                x = raw[b % 2][:, half * (conv.NI // 2):(half + 1) * (conv.NI // 2), :]
                act.activation(x, x, ACT.Tanh, bias=coef[:, b, 1:2], scale=coef[:, b, 0:1]).then_inc(tanh_ready, 1)

            conv.move(act, act_copy(act), conv.moved_act, conv.OF_ACT, 0)
            for b in range(GI):
                for u in range(NU):
                    v = b * NU + u
                    act.wait_ge(conv.conv_done, v + 1)
                    if b >= 2 and u == 0:
                        act.wait_ge(sums_ready, 2 * (b - 1))
                    act.activation(raw[b % 2][:, u * conv.UI:(u + 1) * conv.UI, :].rearrange("p i w -> p (i w)"), conv.bank(b, u)[:, :],
                                   ACT.Identity, bias=k.vec('L2_conv_b_off')).then_inc(raw_ready, 1)
                    if b > 0 and u in (2, 3, 5):
                        (root, lambda x: squash(x, 0), lambda x: squash(x, 1))[(2, 3, 5).index(u)](b - 1)
                    if b + 1 < GI:
                        conv.move(act, act_copy(act), conv.moved_act, conv.OF_ACT, b + 1, u)
            root(GI - 1)
            squash(GI - 1, 0)
            squash(GI - 1, 1)

        @block.vector
        def _(dve):
            n = [0]

            def link(ins):
                n[0] += 1
                ins.then_inc(chain, 1)
                dve.wait_ge(chain, n[0])

            def aggregate(b):
                dve.wait_ge(stats_done, (b + 1) * NU)
                dve.bn_aggr(mv[:, b, :], st[b % 2][:, :, :].rearrange("p u s -> p (u s)")).then_inc(mean_in, 1)

            def spread(b):
                c = slice(b, b + 1)
                dve.wait_ge(mean_in, b + 1)
                dve.wait_ge(mean_ready, b + 1)
                link(dve.tensor_copy(gm[:, c], p_stat[:, 0, c]))
                link(dve.tensor_tensor(d[:, c], mv[:, b, 0:1], gm[:, c], ALU.subtract))
                link(dve.tensor_tensor(d[:, c], d[:, c], d[:, c], ALU.mult))
                dve.tensor_tensor(e[:, c], d[:, c], mv[:, b, 1:2], ALU.add).then_inc(var_in, 1)

            def coefficients(b):
                c = slice(b, b + 1)
                dve.wait_ge(std_ready, b + 1)
                link(dve.reciprocal(std[:, c], std[:, c]))
                link(dve.tensor_tensor(coef[:, b, 0:1], std[:, c], k.vec('L2_conv_gn_off_g'), ALU.mult))
                link(dve.tensor_tensor(d[:, c], gm[:, c], coef[:, b, 0:1], ALU.mult))
                dve.tensor_tensor(coef[:, b, 1:2], k.vec('L2_conv_gn_off_b'), d[:, c], ALU.subtract).then_inc(coef_ready, 1)

            def keep(b, half):
                dve.wait_ge(sums_ready, 2 * b + half + 1)
                dve.tensor_copy(off[:, half * HALF:(half + 1) * HALF, b:32:GI], p_off[half][:, :, :]).then_inc(off_ready, 1)

            conv.move(dve, dve.tensor_copy, conv.moved_dve, conv.OF_DVE, 0)
            for b in range(GI):
                for u in range(NU):
                    v = b * NU + u
                    if b > 0 and u in (1, 2, 5, 7):
                        (spread, coefficients, lambda x: keep(x, 0), lambda x: keep(x, 1))[(1, 2, 5, 7).index(u)](b - 1)
                    dve.wait_ge(raw_ready, v + 1)
                    dve.bn_stats(st[b % 2][:, u, :], raw[b % 2][:, u * conv.UI:(u + 1) * conv.UI, :].rearrange("p i w -> p (i w)")).then_inc(stats_done, 1)
                    if b + 1 < GI:
                        conv.move(dve, dve.tensor_copy, conv.moved_dve, conv.OF_DVE, b + 1, u)
                aggregate(b)
            spread(GI - 1)
            coefficients(GI - 1)
            keep(GI - 1, 0)
            keep(GI - 1, 1)


def snake(nc, k, xn, off, pre, g):
    UR = 8
    NU = H // UR
    COLS = UR * W
    REACH = [abs(t - 4) for t in SNAKE_TAPS]
    NS = len(SNAKE_TAPS)
    DR = UR + 7
    GROUPS = [[(r, min(4, UR - 1 + 2 * n - r)) for r in range(0, UR - 1 + 2 * n, 4)] for n in REACH]
    POOL_TERMS = {4: [((0, 0), (1, 0)), ((0, 1),)], 3: [((0, 0), (1, 0)), ((0, 1),)], 2: [((0, 0), (1, 0))],
                  1: [((0, 0),)]}
    DVE_TERMS = {4: [((1, 1), (0, 2)), ((1, 2), (0, 3)), ((1, 3),)], 3: [((1, 1), (0, 2)), ((1, 2),)],
                 2: [((0, 1), (1, 1))], 1: [((1, 0),)]}
    ON_POOL = [POOL_TERMS[n] for n in REACH]
    ON_DVE = [DVE_TERMS[n] for n in REACH]
    for n in REACH:
        assert sorted(sum(POOL_TERMS[n] + DVE_TERMS[n], ())) == [(sg, j) for sg in (0, 1) for j in range(n)]
    NV, NP_, NG_ = (sum(len(x) for x in y) for y in (ON_DVE, ON_POOL, GROUPS))
    pairs_v0, pairs_p0 = ([sum(pairs_in(x) for x in y[:q]) for q in range(NS + 1)] for y in (ON_DVE, ON_POOL))
    PAIRS_V, PAIRS_P = pairs_v0[NS], pairs_p0[NS]
    AHEAD = 2
    RV, RP = 4, 4
    assert 2 * NV % RV == 0 and 2 * NP_ % RP == 0 and NG_ % 2 == 0
    first_v = [sum(len(x) for x in ON_DVE[:q]) for q in range(NS)]
    first_p = [sum(len(x) for x in ON_POOL[:q]) for q in range(NS)]
    first_g = [sum(len(x) for x in GROUPS[:q]) for q in range(NS)]

    BASE_J = [0, 8, 14, 18]
    FROM_J = [2 * j for j in range(4)]
    with ExitStack() as ctx:
        s = Space(nc, ctx, f"snake{g}")
        diff = s.sb("diff", [P, DR, HP])
        dk = [s.sb(f"dk{i}", [P, UR - 1 + 2 * REACH[i + 4], P]) for i in range(4)]
        clip = [s.sb(f"clip{i}", [P, 2, 20, UR, GI]) for i in range(2)]
        prod_v = [s.sb(f"prod_v{i}", [P, UR, P]) for i in range(RV)]
        prod_p = [s.sb(f"prod_p{i}", [P, UR, P]) for i in range(RP)]
        more_v = [s.sb(f"more_v{i}", [P, UR, P]) for i in range(2)]
        more_p = [s.sb(f"more_p{i}", [P, UR, P]) for i in range(1)]
        minus = s.sb("minus", [P, 4])
        tk = [s.sb(f"tk{i}", [P, COLS]) for i in range(2)]
        ob = s.sb("ob", [P, COLS])
        st = s.sb("stats", [P, 2 * NU, 6])
        mv = s.sb("mean_var", [P, 2])
        gm = s.sb("group_mean", [P, 1])
        d = s.sb("d", [P, 1])
        e = s.sb("e", [P, 1])
        std = s.sb("std", [P, 1])
        p_d = [s.ps(f"d{i}") for i in range(2)]
        p_t = [s.ps(f"t{i}", [P, COLS]) for i in range(2)]
        p_o = s.ps("o", [P, COLS])
        chain = s.sem("vector_chain")
        padded = s.sem("padded")
        diff_ready = s.sem("diff_ready")
        minus_ready = s.sem("minus_ready")
        relu_ready = s.sem("relu_ready")
        clip_ready = s.sem("clip_ready")
        v_pair = s.sem("v_pair")
        p_pair = s.sem("p_pair")
        turned = s.sem("turned")
        dk_copied = s.sem("dk_copied")
        v_ready = s.sem("v_ready")
        v_used = s.sem("v_used")
        p_ready = s.sem("p_ready")
        p_used = s.sem("p_used")
        t_ready = s.sem("t_ready")
        t_copied = s.sem("t_copied")
        w_done = s.sem("w_done")
        out_ready = s.sem("out_ready")
        out_copied = s.sem("out_copied")
        ob_stats = s.sem("ob_stats")
        stored = s.sem("stored")
        mean_in = s.sem("mean_in")
        mean_ready = s.sem("mean_ready")
        var_in = s.sem("var_in")
        var_ready = s.sem("var_ready")
        std_ready = s.sem("std_ready")
        block = ctx.enter_context(nc.Block())

        def units(eng, body):
            body(0, True, False)
            with eng.Fori(1, NU - 1) as u:
                body(u, False, False)
            body(NU - 1, False, True)

        @block.sync
        def _(sp):
            def store(u, first, last):
                sp.wait_ge(out_copied, u + 1)
                sp.dma_start(pre[:, bass.ds(u * UR, UR), :].rearrange("p h w -> p (h w)"), ob[:, :]).then_inc(stored, 16)

            units(sp, store)
            sp.wait_ge(stored, 16 * NU)

        @block.tensor
        def _(pe):
            def turn_d(u, q, i, first):
                tap, n = SNAKE_TAPS[q], REACH[q]
                r0, nr = GROUPS[q][i]
                G = first_g[q] + i
                if G == 0:
                    pe.wait_ge(diff_ready, u + 1)
                if not (first and G < 2):
                    pe.wait_ge(dk_copied, u * NG_ + (G - 1))
                for r in range(nr):
                    ins = pe.transpose(p_d[G % 2][:, r * P:(r + 1) * P], diff[:, 4 - n + r0 + r, tap:tap + W], k.ident)
                ins.then_inc(turned, 1)

            def add_products(u, slot, q, first, last):
                if not (first and q < 2):
                    pe.wait_ge(t_copied, u * NS + (q - 1))
                at, total = 0, len(ON_DVE[q]) + len(ON_POOL[q])
                later = [] if last and q + AHEAD >= NS else list(range(len(GROUPS[(q + AHEAD) % NS])))

                def turn_next():
                    if q + AHEAD < NS:
                        turn_d(u, q + AHEAD, later.pop(0), first)
                    else:
                        turn_d(u + 1, q + AHEAD - NS, later.pop(0), False)

                of_v = [(m, first_v[q], NV, prod_v, v_ready, v_used) for m in range(len(ON_DVE[q]))]
                of_p = [(m, first_p[q], NP_, prod_p, p_ready, p_used) for m in range(len(ON_POOL[q]))]
                for m, n0, per, ring, ready, used in by_turns(of_v, of_p):
                    if later and q != NS - AHEAD:
                        turn_next()
                    pe.wait_ge(ready, u * per + (n0 + m + 1))
                    for r in range(UR):
                        ins = pe.matmul(p_t[q % 2][:, r * W:(r + 1) * W], ring[(slot * per + n0 + m) % len(ring)][:, r, :], k.ident,
                                        start=(at == 0 and r % 4 == 0), stop=(at == total - 1 and r % 4 == 3), is_transpose=True)
                    ins.then_inc(used, 1)
                    at += 1
                while later:
                    turn_next()

            def middle_tap(u, first):
                if not first:
                    pe.wait_ge(out_copied, u)
                for half in range(2):
                    pe.matmul(p_o[:, half * BANK:(half + 1) * BANK], k.w_dsc[:, 4, :],
                              xn[:, bass.ds(u * UR + (PAD + 4 * half), 4), 4:4 + W], start=True, stop=False)

            def weigh(u, q):
                pe.wait_ge(t_copied, u * NS + (q + 1))
                for half in range(2):
                    ins = pe.matmul(p_o[:, half * BANK:(half + 1) * BANK], k.w_dsc[:, SNAKE_TAPS[q], :],
                                    tk[q % 2][:, half * BANK:(half + 1) * BANK], start=False, stop=(q == NS - 1))
                ins.then_inc(w_done, 1)

            pe.wait_ge(padded, 1)
            for q in range(AHEAD):
                for i in range(len(GROUPS[q])):
                    turn_d(0, q, i, True)

            def unit(u, slot, first_pair, last):
                first = first_pair and slot == 0
                for q in range(NS):
                    add_products(u, slot, q, first, last)
                    if q == 0 and not first:
                        weigh(u - 1, NS - 1)
                    if q == 1:
                        middle_tap(u, first)
                    if q > 0:
                        weigh(u, q - 1)

            in_pairs_last(pe, NU, unit)
            weigh(NU - 1, NS - 1)
            pe.wait_ge(mean_in, 1)
            pe.matmul(p_d[0][:, 0:1], k.quad_mean, mv[:, 0:1], start=True, stop=True).then_inc(mean_ready, 1)
            pe.wait_ge(var_in, 1)
            pe.matmul(p_d[1][:, 0:1], k.quad_mean, e[:, :], start=True, stop=True).then_inc(var_ready, 1)

        @block.scalar
        def _(act):
            def copy_d(u, q, first):
                if not (first and q < 4):
                    if q >= 4:
                        v, p = u * NV + first_v[q - 3], u * NP_ + first_p[q - 3]
                    else:
                        v, p = (u - 1) * NV + (first_v + [NV])[q + NS - 3], (u - 1) * NP_ + (first_p + [NP_])[q + NS - 3]
                    act.wait_ge(v_ready, v)
                    act.wait_ge(p_ready, p)
                for i, (r0, nr) in enumerate(GROUPS[q]):
                    G = first_g[q] + i
                    act.wait_ge(turned, u * NG_ + (G + 1))
                    act.activation(dk[q % 4][:, r0:r0 + nr, :].rearrange("p r c -> p (r c)"), p_d[G % 2][:, 0:nr * P],
                                   ACT.Copy).then_inc(dk_copied, 1)

            def relus(u, slot, first):
                if not first:
                    act.wait_ge(v_ready, (u - 1) * NV)
                    act.wait_ge(p_ready, (u - 1) * NP_)
                for sg in range(2):
                    for j in range(4):
                        w = 2 * (4 - j)
                        ins = act.activation(clip[slot][:, sg, BASE_J[j]:BASE_J[j] + w, :, :],
                                             off[:, bass.ds(u * UR, UR), FROM_J[j] * GI:32].rearrange("p r (s b) -> p s r b", b=GI),
                                             ACT.Relu, bias=minus[:, j:j + 1], scale=1.0 if sg == 0 else -1.0)
                ins.then_inc(relu_ready, 1)

            def copy_out(u, first):
                act.wait_ge(w_done, u * NS + NS)
                if not first:
                    act.wait_ge(stored, u * 16)
                    act.wait_ge(ob_stats, u)
                act.activation(ob[:, :], p_o[:, :], ACT.Identity, bias=k.vec('L2_conv_b_dsc')).then_inc(out_copied, 1)

            act.wait_ge(minus_ready, 4)
            relus(0, 0, True)
            for q in range(AHEAD):
                copy_d(0, q, True)

            def unit(u, slot, first, last):
                for q in range(NS):
                    if q < NS - AHEAD:
                        copy_d(u, q + AHEAD, first and slot == 0)
                    elif not last:
                        copy_d(u + 1, q + AHEAD - NS, False)
                    if q == 0 and not (first and slot == 0):
                        copy_out(u - 1, first)
                    if q == 1 and not last:
                        relus(u + 1, 1 - slot, first and slot == 0)

            in_pairs_last(act, NU, unit)
            copy_out(NU - 1, False)
            act.wait_ge(var_ready, 1)
            act.activation(std[:, :], p_d[1][:, 0:1], ACT.Sqrt, bias=k.eps[:, :]).then_inc(std_ready, 1)

        def product_of(eng, slot, q):
            def product(term, place):
                n = REACH[q]
                sg, j = term
                r = n + j if sg == 0 else n - 1 - j
                rows = dk[q % 4][:, r:r + UR, :].rearrange("p r (b c) -> p (r b) c", b=GI)
                f = clip[slot][:, sg, BASE_J[j] + q - FROM_J[j], :, :].rearrange("p r b -> p (r b)").unsqueeze(2).to_broadcast((P, UR * GI, C))
                return eng.tensor_tensor(place[:, :, :].rearrange("p r (b c) -> p (r b) c", b=GI), f, rows, ALU.mult)
            return product

        def whole(place):
            return place[:, :, :]

        @block.gpsimd
        def _(pool):
            def unit(u, slot, first):
                pool.wait_ge(clip_ready, u + 1)
                for q in range(NS):
                    pool.wait_ge(dk_copied, u * NG_ + (first_g[q] + len(GROUPS[q])))
                    make_sums(pool, u, ON_POOL[q], first_p[q], NP_, slot * NP_, prod_p, more_p, p_ready, p_pair, PAIRS_P,
                              pairs_p0[q], p_used, first and slot == 0, product_of(pool, slot, q), whole)

            in_pairs(pool, NU, unit)

        @block.vector
        def _(dve):
            n = [0]

            def link(ins):
                n[0] += 1
                ins.then_inc(chain, 1)
                dve.wait_ge(chain, n[0])

            dve.tensor_copy(xn[:, 0:PAD, PAD:PAD + W], xn[:, PAD:PAD + 1, PAD:PAD + W].to_broadcast((P, PAD, W)))
            link(dve.tensor_copy(xn[:, PAD + H:HP, PAD:PAD + W], xn[:, PAD + H - 1:PAD + H, PAD:PAD + W].to_broadcast((P, PAD, W))))
            dve.tensor_copy(xn[:, :, 0:PAD], xn[:, :, PAD:PAD + 1].to_broadcast((P, HP, PAD)))
            dve.tensor_copy(xn[:, :, PAD + W:HP], xn[:, :, PAD + W - 1:PAD + W].to_broadcast((P, HP, PAD))).then_inc(padded, 1)
            dve.wait_ge(padded, 1)

            def differences(u):
                dve.tensor_tensor(diff[:, :, :], xn[:, bass.ds(u * UR + 1, DR), :], xn[:, bass.ds(u * UR, DR), :],
                                  ALU.subtract).then_inc(diff_ready, 1)

            def clips(u, slot):
                dve.wait_ge(relu_ready, u + 1)
                for sg in range(2):
                    ins = dve.tensor_scalar(clip[slot][:, sg, :, :, :], clip[slot][:, sg, :, :, :], 1.0, 1.0 if sg == 0 else -1.0,
                                            ALU.min, ALU.mult)
                ins.then_inc(clip_ready, 1)

            def add_x(u, q, first):
                dve.wait_ge(v_used, u * NV + (first_v + [NV])[q + 1])
                dve.wait_ge(p_used, u * NP_ + (first_p + [NP_])[q + 1])
                if not (first and q < 2):
                    dve.wait_ge(w_done, u * NS + (q - 1))
                tap = SNAKE_TAPS[q]
                dve.tensor_tensor(tk[q % 2][:, :].rearrange("p (r w) -> p r w", w=W), p_t[q % 2][:, :].rearrange("p (r w) -> p r w", w=W),
                                  xn[:, bass.ds(u * UR + PAD, UR), tap:tap + W], ALU.add).then_inc(t_copied, 1)

            def stats(u):
                dve.wait_ge(out_copied, u + 1)
                for i in range(2):
                    ins = dve.bn_stats(st[:, bass.ds(2 * u + i, 1), :].rearrange("p u s -> p (u s)"), ob[:, i * BANK:(i + 1) * BANK])
                ins.then_inc(ob_stats, 1)

            for j in range(4):
                dve.memset(minus[:, j:j + 1], float(-j)).then_inc(minus_ready, 1)
            differences(0)

            def unit(u, slot, first, last=False):
                fresh = first and slot == 0
                clips(u, slot)
                dve.wait_ge(clip_ready, u + 1)
                for q in range(NS):
                    if q == 3 and not (first and slot == 0):
                        stats(u - 1)
                    dve.wait_ge(dk_copied, u * NG_ + (first_g[q] + len(GROUPS[q])))

                    def between():
                        if q > 0:
                            add_x(u, q - 1, fresh)
                        elif not fresh:
                            add_x(u - 1, NS - 1, False)
                        if q == NS - AHEAD and not last:
                            dve.wait_ge(turned, u * NG_ + NG_)
                            differences(u + 1)

                    make_sums(dve, u, ON_DVE[q], first_v[q], NV, slot * NV, prod_v, more_v, v_ready, v_pair, PAIRS_V,
                              pairs_v0[q], v_used, fresh, product_of(dve, slot, q), whole, between)

            unit(0, 0, True)
            unit(1, 1, True)
            with dve.Fori(1, NU // 2 - 1) as i:
                unit(i * 2, 0, False)
                unit(i * 2 + 1, 1, False)
            unit(NU - 2, 0, False)
            unit(NU - 1, 1, False, True)
            add_x(NU - 1, NS - 1, False)
            stats(NU - 1)
            dve.wait_ge(ob_stats, NU)
            dve.bn_aggr(mv[:, :], st[:, :, :].rearrange("p u s -> p (u s)")).then_inc(mean_in, 1)
            dve.wait_ge(mean_in, 1)
            dve.wait_ge(mean_ready, 1)
            link(dve.tensor_copy(gm[:, :], p_d[0][:, 0:1]))
            link(dve.tensor_tensor(d[:, :], mv[:, 0:1], gm[:, :], ALU.subtract))
            link(dve.tensor_tensor(d[:, :], d[:, :], d[:, :], ALU.mult))
            dve.tensor_tensor(e[:, :], d[:, :], mv[:, 1:2], ALU.add).then_inc(var_in, 1)
            dve.wait_ge(std_ready, 1)
            link(dve.reciprocal(std[:, :], std[:, :]))
            link(dve.tensor_tensor(k.snake_gn[:, 0:1], std[:, :], k.vec('L2_conv_gn_g'), ALU.mult))
            link(dve.tensor_tensor(d[:, :], gm[:, :], k.snake_gn[:, 0:1], ALU.mult))
            dve.tensor_tensor(k.snake_gn[:, 1:2], k.vec('L2_conv_gn_b'), d[:, :], ALU.subtract)


def dcn_offsets(nc, k, xn, offs, g):
    K2 = 9
    with ExitStack() as ctx:
        s = Space(nc, ctx, f"dcnoff{g}")
        conv = RowConv(s, xn, PAD, PAD, k.w_off3)
        NU, UI = conv.NU, conv.UI
        R = 4 * UI
        cm = [s.sb(f"cm{i}", [P, UI, W]) for i in range(2)]
        sig = [s.sb(f"sig{i}", [P, R, K2]) for i in range(2)]
        msum = [s.sb(f"msum{i}", [P, R]) for i in range(2)]
        keep = s.sb("keep", [P, H, OFFS])
        far = s.sb("far", [P, GI * NU])
        far1 = s.sb("far1", [P, 1])
        far0 = s.sb("far0", [1, 1])
        p_t = [s.ps(f"t{i}", [P, R, 32]) for i in range(2)]
        p_far = s.ps("far_row")
        cm_ready = s.sem("cm_ready")
        turned = s.sem("turned")
        sig_ready = s.sem("sig_ready")
        msum_ready = s.sem("msum_ready")
        keep_ready = s.sem("keep_ready")
        stored = s.sem("stored")
        far_ready = s.sem("far_ready")
        far_turned = s.sem("far_turned")
        chain = s.sem("vector_chain")
        block = ctx.enter_context(nc.Block())

        @block.tensor
        def _(pe):
            def turn_back(v):
                pe.wait_ge(cm_ready, v + 1)
                if v >= 2:
                    pe.wait_ge(keep_ready, v - 1)
                for i in range(UI):
                    ins = pe.transpose(p_t[v % 2][:, 4 * i:4 * i + 4, :].rearrange("p q o -> p (q o)"), cm[v % 2][:, i, :], k.ident)
                ins.then_inc(turned, 1)

            for b in range(GI):
                conv.wait_moved(pe, b)
                for u in range(NU):
                    v = b * NU + u
                    if v >= conv.BANKS:
                        pe.wait_ge(cm_ready, v - conv.BANKS + 1)
                    conv.convolve(pe, b, u)
                    if v > 0:
                        turn_back(v - 1)
            turn_back(GI * NU - 1)
            pe.wait_ge(far_ready, 1)
            pe.matmul(p_far[0:1, 0:P], far1[:, :], k.ident, start=True, stop=True).then_inc(far_turned, 1)

        @block.scalar
        def _(act):
            def sigmoid(v):
                act.wait_ge(turned, v + 1)
                if v >= 2:
                    act.wait_ge(msum_ready, v - 1)
                act.activation(sig[v % 2][:, :, :], p_t[v % 2][:, :, 18:27], ACT.Sigmoid).then_inc(sig_ready, 1)

            conv.move(act, act_copy(act), conv.moved_act, conv.OF_ACT, 0)
            for b in range(GI):
                for u in range(NU):
                    v = b * NU + u
                    act.wait_ge(conv.conv_done, v + 1)
                    if v >= 2:
                        act.wait_ge(turned, v - 1)
                    act.activation(cm[v % 2][:, :, :].rearrange("p i w -> p (i w)"), conv.bank(b, u)[:, :], ACT.Identity,
                                   bias=k.bias3).then_inc(cm_ready, 1)
                    if v > 0:
                        sigmoid(v - 1)
                    if b + 1 < GI:
                        conv.move(act, act_copy(act), conv.moved_act, conv.OF_ACT, b + 1, u)
            sigmoid(GI * NU - 1)

        @block.vector
        def _(dve):
            conv.move(dve, dve.tensor_copy, conv.moved_dve, conv.OF_DVE, 0)
            for b in range(GI):
                for u in range(NU):
                    v = b * NU + u
                    rows = slice(u * R, (u + 1) * R)
                    dve.wait_ge(sig_ready, v + 1)
                    o = p_t[v % 2][:, :, 0:18]
                    dve.tensor_reduce(msum[v % 2][:, :], sig[v % 2][:, :, :], AX.X, ALU.add).then_inc(msum_ready, 1)
                    dve.tensor_reduce(far[:, v:v + 1], o, AX.XY, ALU.max, apply_absolute_value=True)
                    dve.tensor_copy(keep[:, rows, b * 18:b * 18 + 18], o)
                    dve.wait_ge(msum_ready, v + 1)
                    dve.tensor_scalar(keep[:, rows, GI * 18 + b], msum[v % 2][:, :], 1.0 / K2, None, ALU.mult).then_inc(keep_ready, 1)
                    if b + 1 < GI:
                        conv.move(dve, dve.tensor_copy, conv.moved_dve, conv.OF_DVE, b + 1, u)
            dve.wait_ge(keep_ready, GI * NU)
            dve.tensor_reduce(far1[:, :], far[:, :], AX.X, ALU.max).then_inc(far_ready, 1)
            dve.wait_ge(far_turned, 1)
            dve.tensor_reduce(far0[:, :], p_far[0:1, 0:P], AX.X, ALU.max).then_inc(chain, 1)
            dve.wait_ge(chain, 1)
            dve.tensor_scalar(k.dense[:, :], far0[:, :], 1.0, None, ALU.is_le)

        @block.sync
        def _(sp):
            for u in range(NU):
                sp.wait_ge(keep_ready, (GI - 1) * NU + u + 1)
                sp.dma_start(offs[u * R:(u + 1) * R, :, :].rearrange("h w f -> w h f"), keep[:, u * R:(u + 1) * R, :]).then_inc(stored, 16)
            sp.wait_ge(stored, NU * 16)


def dcn_gather(nc, k, xn, offs, table, x3, out, g):
    x3_v, out_v = (t.rearrange("(g b) c h w -> g (b c) h w", g=NG)[g] for t in (x3, out))
    table_v = table.rearrange("(b h w) c -> b w h c", b=GI, h=H)
    UR = 4
    NU = H // UR
    with ExitStack() as ctx:
        s = Space(nc, ctx, f"table{g}")
        win = s.sb("win", [P, UR, W])
        tb = s.sb("tb", [P, UR, P])
        p_w = s.ps("w", [P, UR * P])
        win_ready = s.sem("win_ready")
        turned = s.sem("turned")
        tb_ready = s.sem("tb_ready")
        stored = s.sem("stored")
        block = ctx.enter_context(nc.Block())

        def rows(eng, n, body):
            body(0, True)
            with eng.Fori(1, n) as u:
                body(u, False)

        @block.scalar
        def _(act):
            def stage(u, first):
                if not first:
                    act.wait_ge(turned, u)
                act.activation(win[:, :, :], xn[:, bass.ds(u * UR + PAD, UR), PAD:PAD + W], ACT.Copy).then_inc(win_ready, 1)

            rows(act, NU, stage)

        @block.tensor
        def _(pe):
            def turn_rows(u, first):
                pe.wait_ge(win_ready, u + 1)
                if not first:
                    pe.wait_ge(tb_ready, u)
                for r in range(UR):
                    ins = pe.transpose(p_w[:, r * P:(r + 1) * P], win[:, r, :], k.ident)
                ins.then_inc(turned, 1)

            rows(pe, NU, turn_rows)

        @block.vector
        def _(dve):
            def copy(u, first):
                dve.wait_ge(turned, u + 1)
                if not first:
                    dve.wait_ge(stored, u * (16 * GI))
                dve.tensor_copy(tb[:, :, :].rearrange("p r c -> p (r c)"), p_w[:, :]).then_inc(tb_ready, 1)

            rows(dve, NU, copy)

        @block.sync
        def _(sp):
            def store(u, first):
                sp.wait_ge(tb_ready, u + 1)
                for b in range(GI):
                    sp.dma_start(table_v[b, :, bass.ds(u * UR, UR), :], tb[:, :, b * C:(b + 1) * C]).then_inc(stored, 16)

            rows(sp, NU, store)
            sp.wait_ge(stored, 16 * GI * NU)
    for part in range(2):
        gather_rows(nc, k, offs, table, x3_v, out_v, f"{g}_{part}", part * (H // 2), H // 2)


def gather_rows(nc, k, offs, table, x3_v, out_v, tag, h0, n_rows):
    K2 = 9
    with ExitStack() as ctx:
        s = Space(nc, ctx, f"gather{tag}")
        off = s.sb("off", [P, OFFS])
        xr = s.sb("x3", [P, W])
        ob = s.sb("ob", [P, W])
        row = s.sb("row", [P, 1])
        col = s.sb("col", [P, 1])
        image = s.sb("image", [P, GI, K2])
        pos = s.sb("pos", [P, GI, 18])
        inside = s.sb("inside", [P, GI, 18])
        whole = s.sb("whole", [P, GI, 18], I32)
        base = s.sb("base", [P, GI, 18])
        gt = s.sb("gt", [P, GI, 18])
        dist = s.sb("dist", [P, 2, GI, 18])
        dabs = s.sb("dabs", [P, 2, GI, 18])
        hat = s.sb("hat", [P, 2, GI, 18])
        weight = s.sb("weight", [P, 4, GI, K2])
        flat = s.sb("flat", [P, GI, K2])
        index = s.sb("index", [P, 4, GI, K2], U32)
        near = [s.sb(f"near{i}", [P, 4, GI, C]) for i in range(3)]
        prod = s.sb("prod", [P, 4, GI, C])
        half = s.sb("half", [P, 2, P])
        samp = [s.sb(f"samp{i}", [P, P]) for i in range(2)]
        tk = [s.sb(f"tk{i}", [P, P]) for i in range(2)]
        p_t = [s.ps(f"t{i}") for i in range(2)]
        p_o = s.ps("o")
        iota_done = s.sem("iota_done")
        loaded = s.sem("loaded")
        x3_loaded = s.sem("x3_loaded")
        chain = s.sem("vector_chain")
        index_ready = s.sem("index_ready")
        gathered = [s.sem(f"gathered{i}") for i in range(3)]
        near_used = s.sem("near_used")
        samp_ready = s.sem("samp_ready")
        turned = s.sem("turned")
        tk_ready = s.sem("tk_ready")
        w_done = s.sem("w_done")
        ob_ready = s.sem("ob_ready")
        stored = s.sem("stored")
        index_step = s.sem("index_step")
        gather_go = s.sem("gather_go")
        half_ready = s.sem("half_ready")
        block = ctx.enter_context(nc.Block())

        def rows(eng, body):
            body(0, True)
            with eng.Fori(1, n_rows) as h:
                body(h, False)

        @block.sync
        def _(sp):
            def load(h, first):
                if not first:
                    sp.wait_ge(index_ready, h)
                sp.dma_start(off[:, :], offs[bass.ds(h + h0, 1), :, :].rearrange("h w f -> (h w) f")).then_inc(loaded, 16)
                if not first:
                    sp.wait_ge(ob_ready, h)
                sp.dma_start(xr[:, :], x3_v[:, bass.ds(h + h0, 1), :].rearrange("p h w -> p (h w)")).then_inc(x3_loaded, 16)
                sp.wait_ge(ob_ready, h + 1)
                sp.dma_start(out_v[:, bass.ds(h + h0, 1), :].rearrange("p h w -> p (h w)"), ob[:, :]).then_inc(stored, 16)

            rows(sp, load)
            sp.wait_ge(stored, 16 * n_rows)

        @block.gpsimd
        def _(pool):
            pool.iota(col[:, :], pattern=[[0, 1]], base=0, channel_multiplier=1, allow_small_or_imprecise_dtypes=True).then_inc(iota_done, 1)
            pool.iota(image[:, :, :], pattern=[[PX, GI], [0, K2]], base=0, channel_multiplier=0,
                      allow_small_or_imprecise_dtypes=True).then_inc(iota_done, 1)

            def gather(h, first):
                pool.wait_ge(index_ready, h + 1)
                for t in range(K2):
                    if not (first and t < 3):
                        pool.wait_ge(near_used, h * K2 + (t - 2))
                    pool.sem_inc(gather_go, 1)
                    for corner in range(4):
                        for b in range(GI):
                            pool.indirect_dma_start(out=near[t % 3][:, corner, b, :], out_offset=None, in_=table,
                                                    in_offset=bass.IndirectOffsetOnAxis(ap=index[:, corner, b, t:t + 1], axis=0)
                                                    ).then_inc(gathered[t % 3], 16)

            rows(pool, gather)

        @block.vector
        def _(dve):
            dve.wait_ge(iota_done, 2)
            dve.memset(row[:, :], float(h0)).then_inc(chain, 1)
            dve.wait_ge(chain, 1)
            STEPS = 15

            def positions(h, first):
                n = [0]

                def link(ins):
                    n[0] += 1
                    ins.then_inc(chain, 1)
                    dve.wait_ge(chain, h * STEPS + (n[0] + 1))

                dve.wait_ge(loaded, h * 16 + 16)
                o = off[:, 0:GI * 18].rearrange("p (b o) -> p b o", b=GI)
                dve.tensor_scalar(pos[:, :, 0:K2], o[:, :, 0:K2], row[:, :], None, ALU.add)
                link(dve.tensor_scalar(pos[:, :, K2:18], o[:, :, K2:18], col[:, :], None, ALU.add))
                link(dve.tensor_scalar(row[:, :], row[:, :], 1.0, None, ALU.add))
                link(dve.tensor_scalar(inside[:, :, :], pos[:, :, :], 0.0, float(H - 1), ALU.max, ALU.min))
                link(dve.tensor_copy(whole[:, :, :], inside[:, :, :]))
                link(dve.tensor_copy(base[:, :, :], whole[:, :, :]))
                link(dve.tensor_tensor(gt[:, :, :], base[:, :, :], inside[:, :, :], ALU.is_gt))
                link(dve.tensor_tensor(base[:, :, :], base[:, :, :], gt[:, :, :], ALU.subtract))
                link(dve.tensor_scalar(base[:, :, :], base[:, :, :], float(H - 2), None, ALU.min))
                link(dve.tensor_tensor(dist[:, 0, :, :], pos[:, :, :], base[:, :, :], ALU.subtract))
                link(dve.tensor_scalar(dist[:, 1, :, :], dist[:, 0, :, :], -1.0, None, ALU.add))
                link(dve.tensor_scalar(dabs[:, :, :, :], dist[:, :, :, :], -1.0, None, ALU.mult))
                link(dve.tensor_tensor(dabs[:, :, :, :], dabs[:, :, :, :], dist[:, :, :, :], ALU.max))
                link(dve.tensor_scalar(hat[:, :, :, :], dabs[:, :, :, :], -1.0, 1.0, ALU.mult, ALU.add))
                link(dve.tensor_scalar(hat[:, :, :, :], hat[:, :, :, :], 0.0, None, ALU.max))
                dve.tensor_scalar(flat[:, :, :], base[:, :, 0:K2], float(W), None, ALU.mult)
                link(dve.tensor_tensor(hat[:, :, :, 0:K2], hat[:, :, :, 0:K2],
                                       off[:, GI * 18:OFFS].unsqueeze(1).unsqueeze(3).to_broadcast((P, 2, GI, K2)), ALU.mult))
                assert n[0] == STEPS
                for corner in range(4):
                    dy, dx = divmod(corner, 2)
                    dve.tensor_tensor(weight[:, corner, :, :], hat[:, dy, :, 0:K2], hat[:, dx, :, K2:18], ALU.mult)

            def indices(h, first):
                m = [0]

                def link(ins):
                    m[0] += 1
                    ins.then_inc(index_step, 1)
                    dve.wait_ge(index_step, h * 2 + m[0])

                link(dve.tensor_tensor(flat[:, :, :], flat[:, :, :], base[:, :, K2:18], ALU.add))
                link(dve.tensor_tensor(flat[:, :, :], flat[:, :, :], image[:, :, :], ALU.add))
                for corner in range(4):
                    dy, dx = divmod(corner, 2)
                    ins = dve.tensor_scalar(index[:, corner, :, :], flat[:, :, :], float(dy * W + dx), None, ALU.add)
                ins.then_inc(index_ready, 1)

            def row_of(h, first):
                if not first:
                    dve.wait_ge(near_used, h * K2)
                positions(h, first)
                indices(h, first)
                for t in range(K2):
                    dve.wait_ge(gathered[t % 3], h * (3 * 256) + (t // 3 + 1) * 256)
                    for corner in range(4):
                        ins = dve.tensor_tensor(prod[:, corner, :, :], near[t % 3][:, corner, :, :],
                                                weight[:, corner, :, t:t + 1].to_broadcast((P, GI, C)), ALU.mult)
                    ins.then_inc(near_used, 1)
                    dve.wait_ge(near_used, h * K2 + (t + 1))
                    dve.tensor_tensor(half[:, :, :].rearrange("p s (b c) -> p s b c", b=GI), prod[:, 0:2, :, :], prod[:, 2:4, :, :],
                                      ALU.add).then_inc(half_ready, 1)
                    dve.wait_ge(half_ready, h * K2 + (t + 1))
                    if t == 0 and not first:
                        dve.wait_ge(turned, h * K2)
                    elif t >= 2 or not first:
                        dve.wait_ge(turned, h * K2 + (t - 1))
                    dve.tensor_tensor(samp[t % 2][:, :], half[:, 0, :], half[:, 1, :], ALU.add).then_inc(samp_ready, 1)
                dve.wait_ge(w_done, h * K2 + K2)
                dve.wait_ge(x3_loaded, h * 16 + 16)
                if not first:
                    dve.wait_ge(stored, h * 16)
                dve.scalar_tensor_tensor(ob[:, :], p_o[:, 0:W], k.vec('L3_conv_bias'), xr[:, :], ALU.add, ALU.add).then_inc(ob_ready, 1)

            rows(dve, row_of)

        @block.tensor
        def _(pe):
            def row_of(h, first):
                for t in range(K2):
                    pe.wait_ge(samp_ready, h * K2 + (t + 1))
                    if t == 0 and not first:
                        pe.wait_ge(tk_ready, h * K2)
                    elif t >= 2 or not first:
                        pe.wait_ge(tk_ready, h * K2 + (t - 1))
                    pe.transpose(p_t[t % 2][:, 0:P], samp[t % 2][:, :], k.ident).then_inc(turned, 1)
                    pe.wait_ge(tk_ready, h * K2 + (t + 1))
                    if t == 0 and not first:
                        pe.wait_ge(ob_ready, h)
                    pe.matmul(p_o[:, 0:W], k.w_dcn[:, t, :], tk[t % 2][:, :], start=(t == 0), stop=(t == K2 - 1)).then_inc(w_done, 1)

            rows(pe, row_of)

        @block.scalar
        def _(act):
            def row_of(h, first):
                for t in range(K2):
                    act.wait_ge(turned, h * K2 + (t + 1))
                    if t == 0 and not first:
                        act.wait_ge(w_done, h * K2)
                    elif t >= 2 or not first:
                        act.wait_ge(w_done, h * K2 + (t - 1))
                    act.activation(tk[t % 2][:, :], p_t[t % 2][:, 0:P], ACT.Copy).then_inc(tk_ready, 1)

            rows(act, row_of)


def dcn_dense(nc, k, xn, offs, x3, out, g):
    x3_v, out_v = (t.rearrange("(g b) c h w -> g (b c) h w", g=NG)[g] for t in (x3, out))
    UR = BANK // W
    NU = H // UR
    K2 = 9
    HB = UR * GI
    TQ = P // C
    STEPS = [None] + [(t, r) for r in range(0, UR, 2) for t in range(0, K2 - 1, TQ)]
    NS = len(STEPS)
    D0, S0, X0 = 0, 3 * (UR + 1), 3 * (UR + 1) + 2 * UR
    NT = X0 + UR
    GROUPS = [(i, min(4, NT - i)) for i in range(0, NT, 4)]
    NG_ = len(GROUPS)
    TURN_IN = [[], [0, 1], [2, 3], [4, 5], [6]]
    assert sum(TURN_IN, []) == list(range(NG_)) and len(TURN_IN) == NS
    SOURCE = [S0 + UR, S0, D0 + 1, D0 + UR + 2, D0 + 2 * UR + 3, D0, D0 + UR + 1, D0 + 2 * UR + 2]
    PAIR_P, SINGLES_P = [(2,), (0, 1)], [(0,), (1,), (2,)]
    ON_POOL = [PAIR_P, PAIR_P, SINGLES_P, PAIR_P, SINGLES_P]
    ON_DVE = [[(5,), (3, 4), (6,), (7,)]] * NS
    first_v, first_p = ([sum(len(x) for x in y[:st]) for st in range(NS + 1)] for y in (ON_DVE, ON_POOL))
    pairs_v0, pairs_p0 = ([sum(pairs_in(x) for x in y[:st]) for st in range(NS + 1)] for y in (ON_DVE, ON_POOL))
    NV, NP_, PAIRS_V, PAIRS_P = first_v[NS], first_p[NS], pairs_v0[NS], pairs_p0[NS]
    X_WITH = next(ON_POOL[0][m][0] for m, n in schedule(ON_POOL[0])[1].items() if n == 0)
    RV, RP = 5, 4
    assert 2 * NV % RV == 0 and 2 * NP_ % RP == 0 and NS % 2 == 1
    with ExitStack() as ctx:
        s = Space(nc, ctx, f"dense{g}")
        drow = s.sb("drow", [P, UR + 1, W + 2])
        dcol = s.sb("dcol", [P, UR, W + 1])
        mid = s.sb("mid", [P, UR, W])
        xw = [s.sb(f"xw{i}", [P, NT, P]) for i in range(2)]
        off = [s.sb(f"off{i}", [P, UR, OFFS]) for i in range(2)]
        hats = s.sb("hats", [P, 3, HB, 18])
        minus_mod = s.sb("minus_mod", [P, HB])
        modt = [s.sb(f"modt{i}", [P, HB]) for i in range(2)]
        edge = [s.sb(f"edge{i}", [P, 2, HB, 18]) for i in range(2)]
        corner = [s.sb(f"corner{i}", [P, 6, HB, K2]) for i in range(2)]
        prod_v = [s.sb(f"prod_v{i}", [P, UR * 2 * P]) for i in range(RV)]
        prod_p = [s.sb(f"prod_p{i}", [P, UR * 2 * P]) for i in range(RP)]
        more_v = [s.sb(f"more_v{i}", [P, UR * 2 * P]) for i in range(1)]
        more_p = [s.sb(f"more_p{i}", [P, UR * 2 * P]) for i in range(1)]
        tk = [s.sb(f"tk{i}", [P, 2 * BANK]) for i in range(2)]
        xr = [s.sb(f"x3{i}", [P, BANK]) for i in range(2)]
        w_stack = s.sb("w_stack", [P, (K2 - 1) // TQ, C])
        w_sum = s.sb("w_sum", [P, P])
        p_w = [s.ps(f"w{i}") for i in range(2)]
        p_t = [s.ps(f"t{i}", [P, 2 * BANK]) for i in range(2)]
        p_o = [s.ps(f"o{i}") for i in range(2)]
        off_in = [s.sem(f"off_in{i}") for i in range(2)]
        x3_in = [s.sem(f"x3_in{i}") for i in range(2)]
        stored = [s.sem(f"stored{i}") for i in range(2)]
        w_ready = s.sem("w_ready")
        drow_ready = s.sem("drow_ready")
        dcol_ready = s.sem("dcol_ready")
        mid_ready = s.sem("mid_ready")
        abs_ready = s.sem("abs_ready")
        hats_ready = s.sem("hats_ready")
        edge_ready = s.sem("edge_ready")
        weights_ready = s.sem("weights_ready")
        turned = s.sem("turned")
        xw_copied = s.sem("xw_copied")
        v_pair = s.sem("v_pair")
        p_pair = s.sem("p_pair")
        v_ready = s.sem("v_ready")
        v_used = s.sem("v_used")
        p_ready = s.sem("p_ready")
        p_used = s.sem("p_used")
        t_copied = s.sem("t_copied")
        w_done = s.sem("w_done")
        out_done = s.sem("out_done")
        block = ctx.enter_context(nc.Block())

        @block.sync
        def _(sp):
            def load(u, slot):
                sp.dma_start(off[slot][:, :, :], offs[bass.ds(u * UR, UR), :, :].rearrange("h w f -> w h f")).then_inc(off_in[slot], 16)

            load(0, 0)

            def unit(u, slot, first, last):
                if not last:
                    if not (first and slot == 0):
                        sp.wait_ge(weights_ready, u)
                    load(u + 1, 1 - slot)
                if not first:
                    sp.wait_ge(stored[slot], turn(u) * 16)
                sp.dma_start(xr[slot][:, :], x3_v[:, bass.ds(u * UR, UR), :].rearrange("p h w -> p (h w)")).then_inc(x3_in[slot], 16)
                if not (first and slot == 0):
                    store(u - 1, 1 - slot)

            def store(u, slot):
                sp.wait_ge(out_done, u + 1)
                sp.dma_start(out_v[:, bass.ds(u * UR, UR), :].rearrange("p h w -> p (h w)"), xr[slot][:, :]).then_inc(stored[slot], 16)

            in_pairs_last(sp, NU, unit)
            store(NU - 1, 1)
            for slot in range(2):
                sp.wait_ge(stored[slot], 16 * (NU // 2))

        @block.scalar
        def _(act):
            def stage(u):
                act.activation(mid[:, :, :], xn[:, bass.ds(u * UR + PAD, UR), PAD:PAD + W], ACT.Copy).then_inc(mid_ready, 1)

            def make_hats(u, slot):
                act.wait_ge(off_in[slot], turn(u) * 16 + 16)
                o = off[slot][:, :, 0:GI * 18]
                h = [hats[:, i, :, :].rearrange("p (h b) o -> p h (b o)", b=GI) for i in range(3)]
                act.activation(h[1], o, ACT.Abs).then_inc(abs_ready, 1)
                act.activation(h[0], o, ACT.Relu, scale=-1.0)
                act.activation(h[2], o, ACT.Relu)
                for m, scale in ((modt[slot], 1.0), (minus_mod, -1.0)):
                    act.activation(m[:, :].rearrange("p (h b) -> p h b", b=GI), off[slot][:, :, GI * 18:OFFS], ACT.Copy, scale=scale)
                act.wait_ge(abs_ready, u + 1)
                act.activation(h[1], h[1], ACT.Copy, bias=1.0, scale=-1.0).then_inc(hats_ready, 1)

            def copy_rows(u, slot, i):
                act.wait_ge(turned, u * NG_ + (i + 1))
                r0, nr = GROUPS[i]
                act.activation(xw[slot][:, r0:r0 + nr, :].rearrange("p r c -> p (r c)"), p_w[(slot * NG_ + i) % 2][:, 0:nr * P],
                               ACT.Copy).then_inc(xw_copied, 1)

            stage(0)
            make_hats(0, 0)
            for i in range(NG_):
                copy_rows(0, 0, i)

            def unit(u, slot, first, last):
                fresh = first and slot == 0
                if not last:
                    act.wait_ge(turned, u * NG_ + NG_)
                    stage(u + 1)
                for st in range(NS):
                    if not last:
                        if st == 1 and not fresh:
                            act.wait_ge(v_ready, u * NV)
                            act.wait_ge(p_ready, u * NP_)
                        for i in TURN_IN[st]:
                            copy_rows(u + 1, 1 - slot, i)
                    act.wait_ge(v_used, u * NV + first_v[st + 1])
                    act.wait_ge(p_used, u * NP_ + first_p[st + 1])
                    if not (fresh and st < 2):
                        act.wait_ge(w_done, u * NS + (st - 1))
                    ts = (slot + st) % 2
                    act.activation(tk[ts][:, :], p_t[ts][:, :], ACT.Copy).then_inc(t_copied, 1)
                    if st == 0 and not last:
                        act.wait_ge(weights_ready, u + 1)
                        if not fresh:
                            act.wait_ge(p_ready, u * NP_)
                        make_hats(u + 1, 1 - slot)

            in_pairs_last(act, NU, unit)

        @block.tensor
        def _(pe):
            def source(i):
                if i < S0:
                    dx, row = divmod(i, UR + 1)
                    return drow[:, row, dx:dx + W]
                if i < X0:
                    side, row = divmod(i - S0, UR)
                    return dcol[:, row, side:side + W]
                return mid[:, i - X0, :]

            def turn_rows(u, slot, i, first):
                r0, nr = GROUPS[i]
                if i == 0:
                    pe.wait_ge(drow_ready, u + 1)
                if r0 <= S0 < r0 + nr:
                    pe.wait_ge(dcol_ready, u + 1)
                if r0 <= X0 < r0 + nr:
                    pe.wait_ge(mid_ready, u + 1)
                if not (first and i < 2):
                    pe.wait_ge(xw_copied, u * NG_ + (i - 1))
                for r in range(nr):
                    ins = pe.transpose(p_w[(slot * NG_ + i) % 2][:, r * P:(r + 1) * P], source(r0 + r), k.ident)
                ins.then_inc(turned, 1)

            def turn_back(st, ts, place, at, total, with_x):
                n = UR if STEPS[st] is None else 2 * GI
                for i in range(n):
                    src = i if STEPS[st] is None else i % 2 * GI + i // 2
                    ins = pe.matmul(p_t[ts][:, i * W:(i + 1) * W], place[:, src * P:(src + 1) * P], k.ident,
                                    start=(at == 0 and i % 4 == 0), stop=(at == total - 1 and i % 4 == 3), is_transpose=True)
                if with_x:
                    for i in range(UR):
                        ins = pe.matmul(p_t[ts][:, BANK + i * W:BANK + (i + 1) * W], place[:, BANK + i * P:BANK + (i + 1) * P], k.ident,
                                        start=(i == 0), stop=(i == UR - 1), is_transpose=True)
                return ins

            def weigh(u, slot, st, ts, first):
                pe.wait_ge(t_copied, u * NS + (st + 1))
                if st == 0 and not first:
                    pe.wait_ge(out_done, u - 1)
                if STEPS[st] is None:
                    pe.matmul(p_o[slot][:, :], k.w_dcn[:, K2 - 1, :], tk[ts][:, 0:BANK], start=True, stop=False)
                    ins = pe.matmul(p_o[slot][:, :], w_sum[:, :], tk[ts][:, BANK:2 * BANK], start=False, stop=False)
                else:
                    t0, r0 = STEPS[st]
                    for b in range(GI):
                        ins = pe.matmul(p_o[slot][b * C:(b + 1) * C, r0 * W:(r0 + 2) * W], w_stack[:, t0 // TQ, :],
                                        tk[ts][:, b * 2 * W:(b + 1) * 2 * W], start=False, stop=(st == NS - 1))
                ins.then_inc(w_done, 1)

            for i in range(NG_):
                turn_rows(0, 0, i, True)
            pe.wait_ge(w_ready, 2)

            def unit(u, slot, first, last):
                fresh = first and slot == 0
                for st in range(NS):
                    ts = (slot + st) % 2
                    later = [] if last else list(TURN_IN[st])
                    if not (fresh and st < 2):
                        pe.wait_ge(t_copied, u * NS + (st - 1))
                    of_v = [(m, first_v[st], NV, prod_v, v_ready, v_used) for m in range(len(ON_DVE[st]))]
                    of_p = [(m, first_p[st], NP_, prod_p, p_ready, p_used) for m in range(len(ON_POOL[st]))]
                    for at, (m, n0, per, ring, ready, used) in enumerate(by_turns(of_v, of_p)):
                        pe.wait_ge(ready, u * per + (n0 + m + 1))
                        turn_back(st, ts, ring[(slot * per + n0 + m) % len(ring)], at, len(of_v) + len(of_p), STEPS[st] is None and used is p_used and m == 0).then_inc(used, 1)
                        if later and at % 2:
                            turn_rows(u + 1, 1 - slot, later.pop(0), False)
                    if st == 0:
                        if not fresh:
                            weigh(u - 1, 1 - slot, NS - 1, 1 - ts, False)
                    else:
                        weigh(u, slot, st - 1, 1 - ts, first)

            in_pairs_last(pe, NU, unit)
            weigh(NU - 1, 1, NS - 1, (1 + NS - 1) % 2, False)

        def factor(slot, d):
            if d < 2:
                return edge[slot][:, d, :, K2:18]
            return corner[slot][:, d - 2, :, :]

        def product_of(eng, slot, st):
            def product(d, place):
                if STEPS[st] is None:
                    if d == X_WITH:
                        eng.tensor_tensor(place[:, BANK:2 * BANK].rearrange("p (r c) -> p r c", c=C),
                                          xw[slot][:, X0:NT, :].rearrange("p r (b c) -> p (r b) c", b=GI),
                                          modt[slot][:, :].unsqueeze(2).to_broadcast((P, HB, C)), ALU.mult)
                    rows = xw[slot][:, SOURCE[d]:SOURCE[d] + UR, :].rearrange("p r (b c) -> p (r b) c", b=GI)
                    f = factor(slot, d)[:, :, K2 - 1:K2].to_broadcast((P, HB, C))
                    return eng.tensor_tensor(place[:, 0:BANK].rearrange("p (r c) -> p r c", c=C), rows, f, ALU.mult)
                t0, r0 = STEPS[st]
                rows = xw[slot][:, SOURCE[d] + r0:SOURCE[d] + r0 + 2, :].rearrange("p r (b c) -> p (r b) c", b=GI)
                rows = rows.unsqueeze(2).to_broadcast((P, 2 * GI, TQ, C))
                f = factor(slot, d)[:, r0 * GI:(r0 + 2) * GI, t0:t0 + TQ].unsqueeze(3).to_broadcast((P, 2 * GI, TQ, C))
                return eng.tensor_tensor(place[:, :].rearrange("p (r t c) -> p r t c", t=TQ, c=C), rows, f, ALU.mult)
            return product

        def part_of(st):
            return lambda place: place[:, 0:BANK] if STEPS[st] is None else place[:, :]

        @block.gpsimd
        def _(pool):
            def difference_of_rows(u):
                pool.tensor_tensor(drow[:, :, :], xn[:, bass.ds(u * UR + PAD, UR + 1), PAD - 1:PAD + W + 1],
                                   xn[:, bass.ds(u * UR + (PAD - 1), UR + 1), PAD - 1:PAD + W + 1], ALU.subtract).then_inc(drow_ready, 1)

            difference_of_rows(0)

            def unit(u, slot, first, last):
                pool.wait_ge(weights_ready, u + 1)
                pool.wait_ge(xw_copied, u * NG_ + NG_)
                for st in range(NS):
                    make_sums(pool, u, ON_POOL[st], first_p[st], NP_, slot * NP_, prod_p, more_p, p_ready, p_pair, PAIRS_P, pairs_p0[st],
                              p_used, first and slot == 0, product_of(pool, slot, st), part_of(st))
                    if st == 0 and not last:
                        difference_of_rows(u + 1)

            in_pairs_last(pool, NU, unit)

        @block.vector
        def _(dve):
            def difference_of_columns(u):
                dve.tensor_tensor(dcol[:, :, :], xn[:, bass.ds(u * UR + PAD, UR), PAD:PAD + W + 1],
                                  xn[:, bass.ds(u * UR + PAD, UR), PAD - 1:PAD + W], ALU.subtract).then_inc(dcol_ready, 1)

            def make_factors(u, slot):
                dve.wait_ge(hats_ready, u + 1)
                for i, h, mod in ((0, 2, modt[slot]), (1, 0, minus_mod)):
                    ins = dve.tensor_tensor(edge[slot][:, i, :, :], hats[:, h, :, :], mod[:, :].unsqueeze(2).to_broadcast((P, HB, 18)), ALU.mult)
                ins.then_inc(edge_ready, 1)
                dve.wait_ge(edge_ready, u + 1)
                for i in range(2):
                    ins = dve.tensor_tensor(corner[slot][:, 3 * i:3 * i + 3, :, :],
                                            edge[slot][:, i, :, 0:K2].unsqueeze(1).to_broadcast((P, 3, HB, K2)),
                                            hats[:, :, :, K2:18], ALU.mult)
                ins.then_inc(weights_ready, 1)

            def finish(u, slot):
                dve.wait_ge(w_done, u * NS + NS)
                dve.wait_ge(x3_in[slot], turn(u) * 16 + 16)
                dve.scalar_tensor_tensor(xr[slot][:, :], p_o[slot][:, :], k.vec('L3_conv_bias'), xr[slot][:, :], ALU.add,
                                         ALU.add).then_inc(out_done, 1)

            difference_of_columns(0)
            for i in range(TQ):
                r = slice(C * i, C * i + C)
                ins = dve.tensor_copy(w_stack[r, :, :], k.w_dcn[r, i:K2 - 1:TQ, r])
            ins.then_inc(w_ready, 1)
            dve.tensor_reduce(w_sum[:, :], k.w_dcn[:, :, :].rearrange("p t o -> p o t"), AX.X, ALU.add).then_inc(w_ready, 1)
            make_factors(0, 0)

            def unit(u, slot, first, last):
                fresh = first and slot == 0
                dve.wait_ge(weights_ready, u + 1)
                dve.wait_ge(xw_copied, u * NG_ + NG_)
                for st in range(NS):
                    if st == 2 and not fresh:
                        finish(u - 1, 1 - slot)
                    if st == 3 and not last:
                        if not fresh:
                            dve.wait_ge(p_ready, u * NP_)
                            dve.wait_ge(v_ready, u * NV)
                        make_factors(u + 1, 1 - slot)
                    make_sums(dve, u, ON_DVE[st], first_v[st], NV, slot * NV, prod_v, more_v, v_ready, v_pair, PAIRS_V, pairs_v0[st],
                              v_used, fresh, product_of(dve, slot, st), part_of(st))
                    if st == 0 and not last:
                        difference_of_columns(u + 1)
            in_pairs_last(dve, NU, unit)
            finish(NU - 1, 1)


def build(nc, a, out):
    x1 = nc.dram_tensor("x1", (B, C, H, W), F32).ap()
    x2 = nc.dram_tensor("x2", (B, C, H, W), F32).ap()
    x3 = nc.dram_tensor("x3", (B, C, H, W), F32).ap()
    pre = [nc.dram_tensor(f"pre{g}", (P, H, W), F32).ap() for g in range(NG)]
    offs = [nc.dram_tensor(f"offs{g}", (H, W, OFFS), F32).ap() for g in range(NG)]
    table = nc.dram_tensor("table", (GI * PX, C), F32).ap()
    with ExitStack() as ctx:
        k = Kept(nc, ctx)
        with ExitStack() as gate_ctx:
            k.for_gate(nc, gate_ctx)
            make_weights(nc, a, k)
            blur(nc, a["x"], a["L0_conv_sigma"], x1)
            for g in range(NG):
                gate_conv(nc, k, x1, g)
            gate_scale(nc, k)
        xn = ctx.enter_context(nc.sbuf_tensor("xn", [P, HP, HP], F32))
        for g in range(NG):
            residual(nc, k, x1, None, ACT.Silu, k.gate[:, g, 0:1], k.gate[:, g, 1:2], x2, xn, g)
            with nc.sbuf_tensor(f"snake_off{g}", [P, H, 32], F32) as off:
                snake_offsets(nc, k, xn, off, g)
                snake(nc, k, xn, off, pre[g], g)
            residual(nc, k, x2, pre[g], ACT.Relu, k.snake_gn[:, 0:1], k.snake_gn[:, 1:2], x3, xn, g)
            dcn_offsets(nc, k, xn, offs[g], g)
            dense = nc.values_load(k.dense[:, :], min_val=0, max_val=1)
            with nc.If(dense > 0):
                dcn_dense(nc, k, xn, offs[g], x3, out, g)
            with nc.Else():
                dcn_gather(nc, k, xn, offs[g], table, x3, out, g)


_INS = ['x', 'L0_conv_sigma', 'L1_conv_proj_weight', 'L1_conv_proj_bias', 'L1_conv_bn_gamma', 'L1_conv_bn_beta',
        'L1_conv_scale_w', 'L1_conv_scale_b', 'L2_conv_w_off', 'L2_conv_b_off', 'L2_conv_gn_off_g', 'L2_conv_gn_off_b',
        'L2_conv_w_dsc', 'L2_conv_b_dsc', 'L2_conv_gn_g', 'L2_conv_gn_b', 'L3_conv_weight', 'L3_conv_bias',
        'L3_conv_offset_w', 'L3_conv_offset_b', 'L3_conv_mod_w', 'L3_conv_mod_b']


def _constants():
    import numpy as _np

    p, f = _np.arange(P)[:, None], _np.arange(P)[None, :]
    cumulate = _np.zeros((P, 4, 8), _np.float32)
    for block in range(4):
        for slot, tap in enumerate(SNAKE_TAPS):
            for step in (range(tap, 4) if tap < 4 else range(5, tap + 1)):
                cumulate[32 * block + step, block, slot] = 1
    return _np.concatenate([p == f, (p % 32 // 2 == f % 32 // 2) / 8, (p // 4 == f // 4) / 4, (p % 32 == f % 32) / 4,
                            cumulate.reshape(P, 32)], axis=1).astype(_np.float32)


def kernel(**inputs):
    import numpy as _np
    import concourse.bacc as _bacc
    from concourse import mybir as _mybir
    from concourse.bass_utils import run_bass_kernel_spmd as _run

    nc = _bacc.Bacc("TRN2", target_bir_lowering=False, num_devices=1)
    arrays, args = {"in_const": _constants()}, {}
    for name in _INS:
        a = _np.ascontiguousarray(inputs[name])
        arrays[f"in_{name}"] = a.reshape(a.shape or (1,))
    for name, a in arrays.items():
        args[name[3:]] = nc.dram_tensor(name, a.shape, _mybir.dt.from_np(a.dtype), kind="ExternalInput").ap()
    out = nc.dram_tensor("out", (8, 32, 128, 128), _mybir.dt.float32, kind="ExternalOutput").ap()
    build(nc, args, out)
    r = _run(nc, [arrays], core_ids=[0])
    return r.results[0]["out"]
```
